# Optimizing a Trainium2 kernel written in Bass

```python
import numpy as np
import jax
import jax.numpy as jnp

def _softmax(x, axis=-1):
    return jax.nn.softmax(x, axis=axis)

def _gelu(x):
    return jax.nn.gelu(x, approximate=True)

def _silu(x):
    return jax.nn.silu(x)

def _sigmoid(x):
    return jax.nn.sigmoid(x)

def _layernorm(x, axis=-1, eps=1e-05):
    m = jnp.mean(x, axis=axis, keepdims=True)
    v = jnp.var(x, axis=axis, keepdims=True)
    return (x - m) / jnp.sqrt(v + eps)

def _scatter_add(tgt, idx, src, axis=0):
    return tgt.at[idx].add(src)

def _segment_sum(src, seg, n):
    return jax.ops.segment_sum(src, seg, n)
kernel_name = 'mk_xattn_ffn_d2_seqx_r8_e19464'

def setup_inputs(seed: int=0):
    np.random.seed(seed)
    _w = jnp.asarray

    def _rec_inputs():
        import jax
        import jax.numpy as jnp
        _rk = jax.random.key(seed)
        x = 4.136e-05 + 0.9999 * jax.random.normal(jax.random.fold_in(_rk, 1), (2, 512, 128), jnp.float32)
        _lenS = 512 - jax.random.randint(jax.random.fold_in(_rk, 7), (2,), 0, max(1, 512 // 4) + 1, jnp.int32)
        _lenS2 = 32 - jax.random.randint(jax.random.fold_in(_rk, 8), (2,), 0, max(1, 32 // 4) + 1, jnp.int32)
        _ctx_1024P = jax.random.normal(jax.random.fold_in(_rk, 11), (2, 16, 128), jnp.float32)
        _ctx_1024c = jax.random.dirichlet(jax.random.fold_in(_rk, 511), 0.3 * jnp.ones((16,), jnp.float32), (2, 32))
        _ctx_1024t = jnp.einsum('bsk,bkd->bsd', _ctx_1024c, _ctx_1024P)
        _ctx_1024t = _ctx_1024t * jax.lax.rsqrt(jnp.mean(jnp.square(_ctx_1024t)) + 1e-12) * 0.953939
        ctx_1024 = 7.22013e-05 + 1.00017 * (_ctx_1024t + 0.3 * jax.random.normal(jax.random.fold_in(_rk, 611), (2, 32, 128), jnp.float32))
        _validS = jnp.arange(512)[None, :] < _lenS[:, None]
        _validS2 = jnp.arange(32)[None, :] < _lenS2[:, None]
        _causal = jnp.tril(jnp.ones((512, 512), dtype=bool))
        mask_BxS2_bk1 = jnp.broadcast_to(_validS2[:, :], (2, 32))
        mask_BxS2_bk0 = jnp.logical_not(jnp.broadcast_to(_validS2[:, :], (2, 32)))
        return (x, ctx_1024, mask_BxS2_bk1, mask_BxS2_bk0)
    x, ctx_1024, mask_BxS2_bk1, mask_BxS2_bk0 = _rec_inputs()

    def _L0_xattn_setup():
        import jax, jax.numpy as jnp
        import numpy as np
        B, S, T, D, H = (4, 256, 256, 128, 16)
        HD = D // H
        key = jax.random.key(seed)
        ks = jax.random.split(key, 7)
        src = jax.random.normal(ks[0], (B, S, D), dtype=jnp.float32)
        tgt = jax.random.normal(ks[1], (B, T, D), dtype=jnp.float32)
        attention_mask = jax.random.bernoulli(ks[2], 0.9, (B, S))
        scale = 1.0 / np.sqrt(D)
        Wq = jax.random.normal(ks[3], (D, D), dtype=jnp.float32) * scale
        Wk = jax.random.normal(ks[4], (D, D), dtype=jnp.float32) * scale
        Wv = jax.random.normal(ks[5], (D, D), dtype=jnp.float32) * scale
        Wo = jax.random.normal(ks[6], (D, D), dtype=jnp.float32) * scale
        return {'src': src, 'tgt': tgt, 'attention_mask': attention_mask, 'Wq': Wq, 'Wk': Wk, 'Wv': Wv, 'Wo': Wo}
    _L0_xattn_all = _L0_xattn_setup()
    _L0_xattn_in = {k: v for k, v in _L0_xattn_all.items() if k in ('Wq', 'Wk', 'Wv', 'Wo')}
    del _L0_xattn_all

    def _L0_ffn_setup():
        import jax, jax.numpy as jnp
        import numpy as np
        H = 128
        I = 256
        E = 8
        B, S = (2, 128)

        def _swiglu(x, wg, wu, wd):
            return jax.nn.silu(x @ wg) * (x @ wu) @ wd
        key = jax.random.key(seed)
        ks = jax.random.split(key, 8)
        sc_h = 1.0 / np.sqrt(H)
        sc_i = 1.0 / np.sqrt(I)
        return {'hidden_states': jax.random.normal(ks[0], (B, S, H), jnp.float32), 'gate_w': jax.random.normal(ks[1], (H, E), jnp.float32) * sc_h, 'sh_gate': jax.random.normal(ks[2], (H, I), jnp.float32) * sc_h, 'sh_up': jax.random.normal(ks[3], (H, I), jnp.float32) * sc_h, 'sh_down': jax.random.normal(ks[4], (I, H), jnp.float32) * sc_i, 'rt_gate': jax.random.normal(ks[5], (E, H, I), jnp.float32) * sc_h, 'rt_up': jax.random.normal(ks[6], (E, H, I), jnp.float32) * sc_h, 'rt_down': jax.random.normal(ks[7], (E, I, H), jnp.float32) * sc_i}
    _L0_ffn_all = _L0_ffn_setup()
    _L0_ffn_in = {k: v for k, v in _L0_ffn_all.items() if k in ('gate_w', 'sh_gate', 'sh_up', 'sh_down', 'rt_gate', 'rt_up', 'rt_down')}
    del _L0_ffn_all

    def _L1_xattn_setup():
        import jax, jax.numpy as jnp
        import numpy as np
        NUM_HEADS, NUM_KV, HEAD_DIM, WIDTH = (4, 1, 32, 128)
        MASK_FILL = -2.3819763e+38

        def _apply_rope(x, positions, max_wavelength=10000.0):
            d = x.shape[-1]
            freq_exp = 2.0 / d * jnp.arange(d // 2, dtype=jnp.float32)
            timescale = max_wavelength ** freq_exp
            radians = positions[..., None].astype(jnp.float32) / timescale
            radians = radians[..., None, :]
            sin, cos = (jnp.sin(radians), jnp.cos(radians))
            x1, x2 = jnp.split(x, 2, axis=-1)
            out = jnp.concatenate([x1 * cos - x2 * sin, x2 * cos + x1 * sin], axis=-1)
            return out.astype(x.dtype)

        def _rmsnorm(x, scale):
            var = jnp.mean(jnp.square(x.astype(jnp.float32)), axis=-1, keepdims=True)
            normed = x * jax.lax.rsqrt(var + 1e-06)
            return (normed * (1 + scale)).astype(x.dtype)
        key = jax.random.key(seed)
        ks = jax.random.split(key, 7)
        B, T, S = (8, 64, 256)
        return {'x': jax.random.normal(ks[0], (B, T, WIDTH), jnp.float32), 'mem_seq': jax.random.normal(ks[1], (B, S, WIDTH), jnp.float32), 'mem_mask': jax.random.randint(ks[2], (B, S), 0, 2).astype(bool), 'rms_scale': jax.random.normal(ks[3], (WIDTH,), jnp.float32) * 0.02, 'q_w': jax.random.normal(ks[4], (NUM_HEADS, WIDTH, HEAD_DIM), jnp.float32) / np.sqrt(WIDTH), 'kv_w': jax.random.normal(ks[5], (2, NUM_KV, WIDTH, HEAD_DIM), jnp.float32) / np.sqrt(WIDTH), 'out_w': jax.random.normal(ks[6], (NUM_HEADS, HEAD_DIM, WIDTH), jnp.float32) / np.sqrt(NUM_HEADS * HEAD_DIM)}
    _L1_xattn_all = _L1_xattn_setup()
    _L1_xattn_in = {k: v for k, v in _L1_xattn_all.items() if k in ('rms_scale', 'q_w', 'kv_w', 'out_w')}
    del _L1_xattn_all

    def _L1_ffn_setup():
        import jax, jax.numpy as jnp
        import numpy as np
        B, S, D, E, F, TOP_K = (4, 256, 128, 8, 512, 2)
        key = jax.random.key(seed)
        k0, k1, k2, k3 = jax.random.split(key, 4)
        init = lambda k, shape, fan: (jax.random.normal(k, shape, jnp.float32) / np.sqrt(fan)).astype(jnp.float32)
        return {'x': jax.random.normal(k0, (B, S, D), jnp.float32), 'gate_w': init(k1, (D, E), D), 'w1': init(k2, (E, D, F), D), 'b1': jnp.zeros((E, F), jnp.float32), 'w2': init(k3, (E, F, D), F), 'b2': jnp.zeros((E, D), jnp.float32)}
    _L1_ffn_all = _L1_ffn_setup()
    _L1_ffn_in = {k: v for k, v in _L1_ffn_all.items() if k in ('gate_w', 'w1', 'b1', 'w2', 'b2')}
    del _L1_ffn_all
    return {'x': x, 'ctx_1024': ctx_1024, 'mask_BxS2_bk1': mask_BxS2_bk1, 'mask_BxS2_bk0': mask_BxS2_bk0, 'L0_xattn_Wq': _L0_xattn_in['Wq'], 'L0_xattn_Wk': _L0_xattn_in['Wk'], 'L0_xattn_Wv': _L0_xattn_in['Wv'], 'L0_xattn_Wo': _L0_xattn_in['Wo'], 'L0_ffn_gate_w': _L0_ffn_in['gate_w'], 'L0_ffn_sh_gate': _L0_ffn_in['sh_gate'], 'L0_ffn_sh_up': _L0_ffn_in['sh_up'], 'L0_ffn_sh_down': _L0_ffn_in['sh_down'], 'L0_ffn_rt_gate': _L0_ffn_in['rt_gate'], 'L0_ffn_rt_up': _L0_ffn_in['rt_up'], 'L0_ffn_rt_down': _L0_ffn_in['rt_down'], 'L1_xattn_rms_scale': _L1_xattn_in['rms_scale'], 'L1_xattn_q_w': _L1_xattn_in['q_w'], 'L1_xattn_kv_w': _L1_xattn_in['kv_w'], 'L1_xattn_out_w': _L1_xattn_in['out_w'], 'L1_ffn_gate_w': _L1_ffn_in['gate_w'], 'L1_ffn_w1': _L1_ffn_in['w1'], 'L1_ffn_b1': _L1_ffn_in['b1'], 'L1_ffn_w2': _L1_ffn_in['w2'], 'L1_ffn_b2': _L1_ffn_in['b2']}

def reference(x, ctx_1024, mask_BxS2_bk1, mask_BxS2_bk0, L0_xattn_Wq, L0_xattn_Wk, L0_xattn_Wv, L0_xattn_Wo, L0_ffn_gate_w, L0_ffn_sh_gate, L0_ffn_sh_up, L0_ffn_sh_down, L0_ffn_rt_gate, L0_ffn_rt_up, L0_ffn_rt_down, L1_xattn_rms_scale, L1_xattn_q_w, L1_xattn_kv_w, L1_xattn_out_w, L1_ffn_gate_w, L1_ffn_w1, L1_ffn_b1, L1_ffn_w2, L1_ffn_b2):
    import jax
    import jax.numpy as jnp

    def _L0_xattn_ref(src, tgt, attention_mask, Wq, Wk, Wv, Wo):
        import jax, jax.numpy as jnp
        import numpy as np
        B, S, T, D, H = (4, 256, 256, 128, 16)
        HD = D // H
        b, s, d = src.shape
        t = tgt.shape[1]
        q = (tgt @ Wq.T).reshape(b, t, H, HD).transpose(0, 2, 1, 3)
        k = (src @ Wk.T).reshape(b, s, H, HD).transpose(0, 2, 1, 3)
        v = (src @ Wv.T).reshape(b, s, H, HD).transpose(0, 2, 1, 3)
        scores = jnp.einsum('bhtd,bhsd->bhts', q, k) / np.sqrt(HD)
        mask = attention_mask[:, None, None, :]
        scores = jnp.where(mask, scores, -jnp.inf)
        attn = jax.nn.softmax(scores, axis=-1)
        out = jnp.einsum('bhts,bhsd->bhtd', attn, v)
        out = out.transpose(0, 2, 1, 3).reshape(b, t, d)
        return out @ Wo.T

    def _L0_ffn_ref(hidden_states, gate_w, sh_gate, sh_up, sh_down, rt_gate, rt_up, rt_down):
        import jax, jax.numpy as jnp
        import numpy as np
        H = 128
        I = 256
        E = 8
        B, S = (2, 128)

        def _swiglu(x, wg, wu, wd):
            return jax.nn.silu(x @ wg) * (x @ wu) @ wd
        b, s, h = hidden_states.shape
        x = hidden_states.reshape(-1, h)
        logits = x @ gate_w
        top_val = jnp.max(logits, axis=-1, keepdims=True)
        top_id = jnp.argmax(logits, axis=-1)
        score = jax.nn.sigmoid(top_val)
        xs = x * score
        g = jnp.einsum('th,ehi->eti', xs, rt_gate)
        u = jnp.einsum('th,ehi->eti', xs, rt_up)
        act = jax.nn.silu(g) * u
        y = jnp.einsum('eti,eih->eth', act, rt_down)
        onehot = jax.nn.one_hot(top_id, E, dtype=x.dtype)
        routed = jnp.einsum('eth,te->th', y, onehot)
        shared = _swiglu(x, sh_gate, sh_up, sh_down)
        return (shared + routed).reshape(b, s, h)

    def _L1_xattn_ref(x, mem_seq, mem_mask, rms_scale, q_w, kv_w, out_w):
        import jax, jax.numpy as jnp
        import numpy as np
        NUM_HEADS, NUM_KV, HEAD_DIM, WIDTH = (4, 1, 32, 128)
        MASK_FILL = -2.3819763e+38

        def _apply_rope(x, positions, max_wavelength=10000.0):
            d = x.shape[-1]
            freq_exp = 2.0 / d * jnp.arange(d // 2, dtype=jnp.float32)
            timescale = max_wavelength ** freq_exp
            radians = positions[..., None].astype(jnp.float32) / timescale
            radians = radians[..., None, :]
            sin, cos = (jnp.sin(radians), jnp.cos(radians))
            x1, x2 = jnp.split(x, 2, axis=-1)
            out = jnp.concatenate([x1 * cos - x2 * sin, x2 * cos + x1 * sin], axis=-1)
            return out.astype(x.dtype)

        def _rmsnorm(x, scale):
            var = jnp.mean(jnp.square(x.astype(jnp.float32)), axis=-1, keepdims=True)
            normed = x * jax.lax.rsqrt(var + 1e-06)
            return (normed * (1 + scale)).astype(x.dtype)
        B, S, _ = mem_seq.shape
        T = x.shape[1]
        G = NUM_HEADS // NUM_KV
        xn = _rmsnorm(x, rms_scale)
        mn = _rmsnorm(mem_seq, rms_scale)
        q = jnp.einsum('BTD,NDH->BTNH', xn, q_w)
        kv = jnp.einsum('BSD,cKDH->cBSKH', mn, kv_w)
        k, v = (kv[0], kv[1])
        q_pos = jnp.broadcast_to(jnp.arange(S, T + S), (B, T))
        k_pos = jnp.broadcast_to(jnp.arange(S), (B, S))
        q = _apply_rope(q, q_pos) * HEAD_DIM ** (-0.5)
        k = _apply_rope(k, k_pos)
        q = q.reshape(B, T, NUM_KV, G, HEAD_DIM)
        logits = jnp.einsum('BTKGH,BSKH->BKGTS', q, k, preferred_element_type=jnp.float32)
        masked = jnp.where(mem_mask[:, None, None, None, :], logits, MASK_FILL)
        probs = jax.nn.softmax(masked, axis=-1).astype(x.dtype)
        enc = jnp.einsum('BKGTS,BSKH->BTKGH', probs, v).reshape(B, T, NUM_HEADS, HEAD_DIM)
        return jnp.einsum('BTNH,NHD->BTD', enc, out_w)

    def _L1_ffn_ref(x, gate_w, w1, b1, w2, b2):
        import jax, jax.numpy as jnp
        import numpy as np
        B, S, D, E, F, TOP_K = (4, 256, 128, 8, 512, 2)
        b, s, d = x.shape
        e = gate_w.shape[1]
        xf = x.reshape(-1, d)
        t = xf.shape[0]
        logits = xf @ gate_w
        top_w, top_idx = jax.lax.top_k(logits, TOP_K)
        top_w = jax.nn.softmax(top_w.astype(jnp.float32), axis=-1).astype(x.dtype)
        combine = jnp.zeros((t, e), x.dtype).at[jnp.arange(t)[:, None], top_idx].add(top_w)
        h = jax.nn.gelu(jnp.einsum('td,edf->tef', xf, w1) + b1, approximate=False)
        y = jnp.einsum('tef,efd->ted', h, w2) + b2
        out = jnp.einsum('ted,te->td', y, combine)
        return out.reshape(b, s, d)
    x = x + _L0_xattn_ref(ctx_1024, _layernorm(x, axis=-1), mask_BxS2_bk1, L0_xattn_Wq, L0_xattn_Wk, L0_xattn_Wv, L0_xattn_Wo)
    x = x + _L0_ffn_ref(_layernorm(x, axis=-1), L0_ffn_gate_w, L0_ffn_sh_gate, L0_ffn_sh_up, L0_ffn_sh_down, L0_ffn_rt_gate, L0_ffn_rt_up, L0_ffn_rt_down)
    x = x + _L1_xattn_ref(_layernorm(x, axis=-1), ctx_1024, mask_BxS2_bk0, L1_xattn_rms_scale, L1_xattn_q_w, L1_xattn_kv_w, L1_xattn_out_w)
    x = x + _L1_ffn_ref(_layernorm(x, axis=-1), L1_ffn_gate_w, L1_ffn_w1, L1_ffn_b1, L1_ffn_w2, L1_ffn_b2)
    return x

_drawn_inputs = setup_inputs


def setup_inputs(seed=0):
    import zlib

    import numpy as np

    out = dict(_drawn_inputs(seed))
    spreads = {'L1_ffn_b1': (0.0, 0.1), 'L1_ffn_b2': (0.0, 0.1)}
    factors = {}
    for name, (base, spread) in spreads.items():
        noise = np.random.default_rng([zlib.crc32(name.encode()), seed]).standard_normal(out[name].shape)
        drawn = base * np.exp(spread * noise) if base else spread * noise
        out[name] = jnp.asarray(drawn.astype(out[name].dtype))
    for name, factor in factors.items():
        out[name] = (out[name] * factor).astype(out[name].dtype)
    return out
```

```python
from contextlib import ExitStack

import numpy as np

import concourse.bass as bass
from concourse import mybir

ALU = mybir.AluOpType
ACT = mybir.ActivationFunctionType
F32 = mybir.dt.float32
F32R = mybir.dt.float32r
BF16 = mybir.dt.bfloat16
U8 = mybir.dt.uint8
U32 = mybir.dt.uint32
AX_X = mybir.AxisListType.X

P = 128
B, S, D = 2, 512, 128
T = S // P
SC = 32
H0, H1 = 16, 4
HD0, HD1 = D // H0, D // H1
E = 8
I0 = 256
C0 = I0 // P
F1 = 512
C1 = F1 // P
U0 = E + 1
W0C = 2 * I0 + C0 * D
W1C = F1 + C1 * D
RAW = 3
LAG0, LAG1 = 2, 2
HB, HR = 3, 4
N0, N1 = U0 * C0, E * C1
LN_EPS, RMS_EPS = 1e-5, 1e-6
MASKED0, MASKED1 = 3.0e38, 2.3819763e38

ATT0 = dict(stats=0, normed=1, turned=2, scores01=3, sub01=4, scores23=5, sub23=6, sums=7, probs01=9, probs23=10,
            out=11, add=12, normed2=13, turned2=14, logits=15, route=16, _n=N0)
ATT1 = dict(y=0, y_turned=1, add_y=2, normed=3, turned=4, queries=5, rotate=6, scores=7, softmax=8, probs=9, out=10,
            add=11, normed2=12, turned2=13, logits=14, route=15, weights=16, bias=17, _n=18)

PA_ = dict(ctxT=0, wkT=64, wvT=192, wq=320, woT=448, bm0=576, bm0s=592, ident=608, _end=736)
PB_ = dict(qw=0, kw=128, vw=160, ow=192, rms=320, gate0=321, gate1=329, b1=337, bm1=369, bm1s=373,
           cosk=377, sink=409, iota=441, _end=449)


def two_moe_layers(nc, x, pack_a, pack_b, selectors, b2_rows, rope_q, ctx, masks, w0, w1, out):
    with ExitStack() as stack:
        def sb(name, shape, dt=F32):
            return stack.enter_context(nc.sbuf_tensor(name, shape, dt))

        def sem(name):
            return stack.enter_context(nc.semaphore(name))

        bank = [stack.enter_context(nc.psum_tensor(f"bank{i}", [P, 512], F32)) for i in range(8)]

        def tiles(ap):
            return ap.rearrange("p (t d) -> p t d", t=T)

        X = sb("X", [P, B, T, D])
        pa = sb("pa", [P, PA_["_end"]])
        pb = sb("pb", [P, PB_["_end"]])
        b2 = sb("b2", [2 * E, D])
        rope = sb("rope", [P, 2, S])
        ctx_sb = sb("ctx_sb", [B * SC, D])
        mask_u8 = sb("mask_u8", [1, 2, B * SC], U8)
        maskb = sb("maskb", [1, 2, B * SC], BF16)
        ones1 = sb("ones1", [1, P], BF16)
        neg_half = sb("neg_half", [P, T])
        KVbd = sb("KVbd", [P, 2, B, H0, SC])
        Kbd, Vbd = KVbd[:, 0], KVbd[:, 1]
        M0 = sb("M0", [P, B, 512])
        VW0 = sb("VW0", [P, B, 4, D])
        zT = sb("zT", [P, S])
        Sc = sb("Sc", [P, T, H0, SC])
        PT = KVbd[:].rearrange("p k b h s -> p (k b h s)").rearrange("p (t c q) -> p t c q", t=T, c=4)
        mx0 = sb("mx0", [P, T, H0])
        sm0 = sb("sm0", [P, T, H0])
        rs0 = sb("rs0", [P, T, H0])
        csq = sb("csq", [B * SC, D])
        cms = sb("cms", [B * SC, 1])
        cve = sb("cve", [B * SC, 1])
        crs = sb("crs", [B * SC, 1])
        mn = sb("mn", [B * SC, D])
        mnT = sb("mnT", [P, B * SC])
        rms1 = sb("rms1", [P, 1])
        wq1 = sb("wq1", [P, H1, HD1])
        wq1s = sb("wq1s", [P, H1, HD1])
        wk1 = sb("wk1", [P, H1, HD1])
        wk1s = sb("wk1s", [P, H1, HD1])
        wv1 = sb("wv1", [P, H1, HD1])
        kr = sb("kr", [P, 3, B, SC])
        Kbd1 = sb("Kbd1", [P, B, H1, SC])
        Vbd1 = sb("Vbd1", [P, B, H1, SC])
        VW1 = sb("VW1", [P, B, D])
        qr = sb("qr", [P, 2, S])
        S1 = sb("S1", [P, T * H1, SC])
        P1T = sb("P1T", [P, T, P])
        mx1 = sb("mx1", [P, T * H1])
        sm1 = sb("sm1", [P, T * H1])
        rs1 = sb("rs1", [P, T * H1])
        st = sb("st", [P, T, 6])
        mv = sb("mv", [P, T, 2])
        ve = sb("ve", [P, T])
        rstd = sb("rstd", [P, T])
        ZA = sb("ZA", [P, T, D])
        ZF = sb("ZF", [P, B, T, D])
        zF32 = sb("zF32", [P, S])
        zhi = sb("zhi", [P, B, S], F32R)
        zlo = sb("zlo", [P, B, S], F32R)
        lg = sb("lg", [P, T, E])
        top = sb("top", [P, T, 8])
        ix = sb("ix", [P, T, 8], U32)
        ixf = sb("ixf", [P, T, 2])
        th = sb("th", [P, T])
        df = sb("df", [P, T])
        sc = sb("sc", [P, T, 2])
        oh = sb("oh", [P, T, E])
        oh2 = sb("oh2", [P, T, E])
        ohs = sb("ohs", [P, B, T, E])
        cmb = sb("cmb", [P, T, E])
        c16 = sb("c16", [P, T, 2 * E], F32R)
        cT16 = sb("cT16", [2 * E, B, S], F32R)
        selr = sb("selr", [2 * E, E, P], F32R)
        b2hi = sb("b2hi", [2 * E, D], F32R)
        b2lo = sb("b2lo", [2 * E, D], F32R)
        b2c = sb("b2c", [P, S])
        raw = sb("raw", [P, RAW, W1C])
        whi = sb("whi", [P, E * W1C], F32R)
        wlo = sb("wlo", [P, E * W1C], F32R)
        w0hi, w0lo = (w[:, 0:U0 * W0C].rearrange("p (u c) -> p u c", u=U0) for w in (whi, wlo))
        w1hi, w1lo = (w[:].rearrange("p (e c) -> p e c", e=E) for w in (whi, wlo))
        xm = sb("xm", [P, 2, T, D])
        xmhi = sb("xmhi", [P, 2, S], F32R)
        xmlo = sb("xmlo", [P, 2, S], F32R)
        sg = sb("sg", [P, 2, S])
        h = sb("h", [P, HB, S])
        hhi = sb("hhi", [P, HR, S], F32R)
        hlo = sb("hlo", [P, HR, S], F32R)
        yT = sb("yT", [P, S])
        cbs = sg
        ym = xm[:].rearrange("p k t d -> p k (t d)")
        sel = ym[0:2 * E].rearrange("p a b -> p (a b)")
        acc = sb("acc", [P, S])

        ident = pa[:, PA_["ident"]:PA_["ident"] + P]

        def a_(name, n):
            return pa[:, PA_[name]:PA_[name] + n]

        def b_(name, n):
            return pb[:, PB_[name]:PB_[name] + n]

        def over_rows(ap, n):
            return ap.unsqueeze(1).to_broadcast([ap.shape[0], n, ap.shape[1]])

        def over_cols(ap, n):
            return ap.unsqueeze(2).to_broadcast([ap.shape[0], ap.shape[1], n])

        names = """pa_in pb_in sel_in b2_in rope_in ctx_in mask_in out_stored
            const_set maskb_set kv0_psum kbd0_set m0_psum m0_set vbd0_set vw0_psum vw0_set
            csq_set cve_set crs_set mn_set mnT_psum mnT_set rms1_set wts1_set kv1_psum kr_parts kr_set kvbd1_set
            vw1_psum vw1_set sel_set b2hi_set b2lo_set
            stats_set aggr_set ve_set rstd_set za_set zf_set x_updated
            zaT_psum zaT_set s_psum mx0_set s_sub s_exp sm0_set rs0_set p_norm pT_psum pT_set o_psum
            zfT_psum zhi_set zlo_set zF32_set lg_psum lg_set top_set ix_set ixf_set oh_set th_set sc_set ohs_set
            yT_set yT_psum q_psum q_sin q_set l1_psum mx1_set s1_sub s1_exp sm1_set rs1_set p1_norm p1T_psum
            p1T_set o1_psum df_set sc1_set oh2_set ohw_set cmb_set c16hi_set c16_set cT_psum cT_set b2_psum b2c_set
            w0hi_set w1hi_set w_lo_set xm_set xmT_psum xmhi_set xmlo_set gu_psum silu_set h_set hhi_set hlo_set
            down0_done up_psum gelu_hi_set gelu_set hi1_set lo1_set down1_done cb_psum cbs_set ym_set acc_set
            accT_psum""".split()
        s = {n: sem(n) for n in names}
        x_in = [sem(f"x_in{g}") for g in range(B)]
        w_in = [sem(f"w_in{i}") for i in range(RAW)]

        X_ORDER = [("a", 0), ("a", 1), ("f", 0), ("b", 0), ("f", 1), ("b", 1), ("o", 0), ("o", 1)]
        LN_ORDER = [("a", 0), ("A", 0), ("a", 1), ("A", 1), ("b", 0), ("B", 0), ("b", 1), ("B", 1)]

        def x_count(stage, g):
            return X_ORDER.index((stage, g)) + 1

        def ln_count(stage, g):
            return LN_ORDER.index((stage, g)) + 1

        def r_count(layer, g):
            return layer * B + g + 1

        def gu_after(n):
            return 2 * C0 * ((n // E) * U0 + n % E + 2)

        def w1_free(e):
            units = min(U0, -(-(e + 1) * W1C // W0C))
            return N0 + units * C0

        W1_AT0 = {w1_free(e) - N0 + LAG0 + 1: e for e in range(E) if w1_free(e) - N0 + LAG0 + 1 < N0}
        W1_AT1 = {3 + 2 * k: e for k, e in enumerate(sorted(set(range(E)) - set(W1_AT0.values())))}

        x_d = x.rearrange("b (p t) d -> b p (t d)", t=T)
        out_d = out.rearrange("b (p t) d -> b p (t d)", t=T)

        block = stack.enter_context(nc.Block())

        @block.sync
        def _(sp):
            for g in range(B):
                sp.dma_start(X[:, g].rearrange("p t d -> p (t d)"), x_d[g]).then_inc(x_in[g], 16)
            for w in range(U0 + E):
                if w >= RAW:
                    sp.wait_ge(s["w_lo_set"], w - RAW + 1)
                if w < U0:
                    sp.dma_start(raw[:, w % RAW, 0:W0C], w0[w]).then_inc(w_in[w % RAW], 16)
                else:
                    sp.dma_start(raw[:, w % RAW, :], w1[w - U0]).then_inc(w_in[w % RAW], 16)
            for g in range(B):
                sp.wait_ge(s["x_updated"], x_count("o", g))
                sp.dma_start(out_d[g], X[:, g].rearrange("p t d -> p (t d)")).then_inc(s["out_stored"], 16)
            sp.wait_ge(s["out_stored"], 16 * B)

        @block.gpsimd
        def _(pool):
            nc.gpsimd.memset(neg_half[:], -0.5)
            nc.gpsimd.memset(ones1[:], 1.0).then_inc(s["const_set"], 1)
            pool.wait_ge(s["const_set"], 1)

            def power(stage, g):
                pool.wait_ge(s["ve_set"], ln_count(stage, g))
                nc.gpsimd.tensor_tensor(rstd[:], ve[:], neg_half[:], ALU.pow).then_inc(s["rstd_set"], 1)

            def context_power():
                pool.wait_ge(s["cve_set"], 1)
                nc.gpsimd.tensor_tensor(crs[:], cve[:], neg_half[0:B * SC, 0:1], ALU.pow).then_inc(s["crs_set"], 1)

            def weights_low(w):
                r = w % RAW
                if w < U0:
                    hi, lo, c = w0hi[:, w], w0lo[:, w], W0C
                    pool.wait_ge(s["w0hi_set"], w + 1)
                else:
                    hi, lo, c = w1hi[:, w - U0], w1lo[:, w - U0], W1C
                    pool.wait_ge(s["w1hi_set"], w - U0 + 1)
                pool.wait_ge(w_in[r], 16 * (w // RAW + 1))
                nc.gpsimd.tensor_tensor(lo, raw[:, r, 0:c], hi.bitcast(F32), ALU.subtract).then_inc(s["w_lo_set"], 1)

            def normalise0(g, t):
                pool.wait_ge(s["rs0_set"], g * T + t + 1)
                nc.gpsimd.tensor_tensor(Sc[:, t], Sc[:, t],
                                        over_cols(rs0[:, t], SC), ALU.mult).then_inc(s["p_norm"], 1)

            def attention0(g):
                for k in range(ATT0["_n"]):
                    if k == ATT0["stats"]:
                        power("a", g)
                    if k == ATT0["sums"]:
                        normalise0(g, 0)
                        normalise0(g, 1)
                    if k == ATT0["sums"] + 1:
                        normalise0(g, 2)
                        normalise0(g, 3)
                        if g == 0:
                            weights_low(0)
                            context_power()
                    if k == ATT0["add"]:
                        power("A", g)
                    yield

            def attention1(g):
                for k in range(ATT1["_n"]):
                    if k == ATT1["add_y"]:
                        power("b", g)
                    if k == ATT1["rotate"]:
                        pool.wait_ge(s["q_sin"], g + 1)
                        nc.gpsimd.tensor_tensor(qr[:, 0], qr[:, 0], qr[:, 1], ALU.add).then_inc(s["q_set"], 1)
                    if k == ATT1["softmax"]:
                        pool.wait_ge(s["rs1_set"], g + 1)
                        nc.gpsimd.tensor_tensor(S1[:], S1[:], over_cols(rs1[:], SC), ALU.mult).then_inc(s["p1_norm"], 1)
                    if k == ATT1["add"]:
                        power("B", g)
                    yield

            def mask_x(g, u):
                n = g * E + u - 1
                if n == 0:
                    pool.wait_ge(s["sel_set"], 1)
                pool.wait_ge(s["ohs_set"], g + 1)
                if n >= 2:
                    pool.wait_ge(s["xmT_psum"], n - 1)
                nc.gpsimd.tensor_tensor(xm[:, n % 2], ZF[:, g], over_cols(ohs[:, g, :, u - 1], D),
                                        ALU.mult).then_inc(s["xm_set"], 1)

            def add_y(n):
                g, e = divmod(n, E)
                pool.wait_ge(s["ym_set"], n + 1)
                if e == 0:
                    pool.wait_ge(s["b2c_set"], g + 1)
                    if g:
                        pool.wait_ge(s["accT_psum"], g)
                else:
                    pool.wait_ge(s["acc_set"], n)
                nc.gpsimd.tensor_tensor(acc[:], ym[:, n % 2], b2c[:] if e == 0 else acc[:],
                                        ALU.add).then_inc(s["acc_set"], 1)

            def beside():
                yield from attention0(1)
                yield
                yield
                yield from attention1(0)
                yield
                yield
                yield from attention1(1)

            for _ in attention0(0):
                pass
            weights_low(1)
            weights_low(2)
            side = beside()
            for g in range(B):
                for u in range(U0):
                    for c in range(C0):
                        if c == 0 and u + 1 < U0:
                            mask_x(g, u + 1)
                        if c == 1 and g == 0 and u + 3 < U0:
                            weights_low(u + 3)
                        if g == 1 and u * C0 + c in W1_AT0:
                            weights_low(U0 + W1_AT0[u * C0 + c])
                        next(side, None)
            for g in range(B):
                for e in range(E):
                    for c in range(C1):
                        if c == LAG1 + 1 and g * E + e >= 1:
                            add_y(g * E + e - 1)
                        if g == 0 and e * C1 + c in W1_AT1:
                            weights_low(U0 + W1_AT1[e * C1 + c])
                        next(side, None)
            add_y(B * E - 1)

        @block.scalar
        def _(act):
            act.dma_start(pa[:], pack_a).then_inc(s["pa_in"], 16)
            act.dma_start(mask_u8[:].rearrange("p a b -> p (a b)"), masks).then_inc(s["mask_in"], 16)
            act.dma_start(pb[:], pack_b).then_inc(s["pb_in"], 16)
            act.dma_start(ctx_sb[:], ctx).then_inc(s["ctx_in"], 16)
            act.dma_start(sel, selectors).then_inc(s["sel_in"], 16)
            act.dma_start(b2[:], b2_rows).then_inc(s["b2_in"], 16)
            act.dma_start(rope[:], rope_q).then_inc(s["rope_in"], 16)

            def copy(out_, in_):
                return nc.scalar.activation(out_, in_, ACT.Copy)

            def attention0(g):
                for k in range(ATT0["_n"]):
                    if k == ATT0["turned"]:
                        act.wait_ge(s["zaT_psum"], g + 1)
                        if g:
                            act.wait_ge(s["s_psum"], T * g)
                        copy(zT[:], bank[6][:]).then_inc(s["zaT_set"], 1)
                        if g == 0:
                            for b in range(B):
                                act.wait_ge(s["vw0_psum"], b + 1)
                                copy(VW0[:, b], tiles(bank[2 + b][:])).then_inc(s["vw0_set"], 1)
                    if k == ATT0["sub23"]:
                        for t in range(T):
                            act.wait_ge(s["s_sub"], g * T + t + 1)
                            nc.scalar.activation(Sc[:, t], Sc[:, t], ACT.Exp).then_inc(s["s_exp"], 1)
                    for kk, t0 in ((ATT0["probs01"], 0), (ATT0["probs23"], 2)):
                        if k == kk:
                            for t in (t0, t0 + 1):
                                act.wait_ge(s["pT_psum"], g * T + t + 1)
                                if g and t == 0:
                                    act.wait_ge(s["o_psum"], g)
                                copy(PT[:, t], tiles(bank[6 + t % 2][:])).then_inc(s["pT_set"], 1)
                    if k == ATT0["add"] and g == 0:
                        act.wait_ge(s["mnT_psum"], 1)
                        copy(mnT[:], bank[0][:, 0:B * SC]).then_inc(s["mnT_set"], 1)
                    if k == ATT0["turned2"]:
                        act.wait_ge(s["zfT_psum"], r_count(0, g))
                        copy(zhi[:, g], bank[7][:]).then_inc(s["zhi_set"], 1)
                    if k == ATT0["route"]:
                        act.wait_ge(s["top_set"], T * r_count(0, g))
                        nc.scalar.activation(th[:], top[:, :, 0], ACT.Tanh, scale=0.5).then_inc(s["th_set"], 1)
                    if k == 1 and g == 1:
                        act.wait_ge(s["vw1_psum"], 1)
                        copy(VW1[:], bank[6][:, 0:B * D].rearrange("p (b d) -> p b d", b=B)).then_inc(s["vw1_set"], 1)
                    yield

            def attention1(g):
                for k in range(ATT1["_n"]):
                    if k == ATT1["y"]:
                        act.wait_ge(s["down0_done"], (g + 1) * N0)
                        if g:
                            act.wait_ge(s["yT_psum"], g)
                        copy(yT[:], bank[4][:]).then_inc(s["yT_set"], 1)
                    if k == ATT1["turned"]:
                        act.wait_ge(s["zaT_psum"], B + g + 1)
                        if g:
                            act.wait_ge(s["q_psum"], 2 * g)
                        else:
                            act.wait_ge(s["s_psum"], T * B)
                        copy(zT[:], bank[7][:]).then_inc(s["zaT_set"], 1)
                    if k == ATT1["softmax"]:
                        act.wait_ge(s["s1_sub"], g + 1)
                        nc.scalar.activation(S1[:], S1[:], ACT.Exp).then_inc(s["s1_exp"], 1)
                    if k == ATT1["probs"]:
                        act.wait_ge(s["p1T_psum"], g + 1)
                        if g:
                            act.wait_ge(s["o1_psum"], g)
                        copy(P1T[:], tiles(bank[7][:])).then_inc(s["p1T_set"], 1)
                    if k == ATT1["turned2"]:
                        act.wait_ge(s["zfT_psum"], r_count(1, g))
                        act.wait_ge(s["gu_psum"], 2 * (g * N0 + C0))
                        copy(zhi[:, g], bank[7][:]).then_inc(s["zhi_set"], 1)
                    if k == ATT1["route"]:
                        act.wait_ge(s["df_set"], g + 1)
                        nc.scalar.activation(th[:], df[:], ACT.Tanh, scale=0.5).then_inc(s["th_set"], 1)
                    if k == ATT1["weights"]:
                        act.wait_ge(s["cT_psum"], g + 1)
                        copy(cT16[:, g], bank[7][0:2 * E, :]).then_inc(s["cT_set"], 1)
                    if k == ATT1["bias"]:
                        act.wait_ge(s["b2_psum"], g + 1)
                        if g:
                            act.wait_ge(s["acc_set"], 1)
                        copy(b2c[:], bank[6][:]).then_inc(s["b2c_set"], 1)
                    yield

            def beside():
                yield from attention0(1)
                yield
                yield
                yield from attention1(0)
                yield
                yield
                yield from attention1(1)

            def masked_high(n):
                act.wait_ge(s["xmT_psum"], n + 1)
                if n >= 2:
                    act.wait_ge(s["gu_psum"], gu_after(n - 2))
                copy(xmhi[:, n % 2], bank[5][:]).then_inc(s["xmhi_set"], 1)

            def hidden_high(i):
                act.wait_ge(s["h_set"], i + 1)
                if i >= HR:
                    act.wait_ge(s["down0_done"], i - HR + 1)
                copy(hhi[:, i % HR], h[:, i % HB]).then_inc(s["hhi_set"], 1)

            def weights1_high(e):
                w = U0 + e
                act.wait_ge(w_in[w % RAW], 16 * (w // RAW + 1))
                act.wait_ge(s["down0_done"], w1_free(e))
                copy(w1hi[:, e], raw[:, w % RAW, :]).then_inc(s["w1hi_set"], 1)

            for b in range(B):
                act.wait_ge(s["m0_psum"], b + 1)
                copy(M0[:, b], bank[b][:]).then_inc(s["m0_set"], 1)
            for _ in attention0(0):
                pass
            act.wait_ge(s["sel_in"], 16)
            copy(selr[:].rearrange("k e p -> k (e p)"), sel).then_inc(s["sel_set"], 1)
            act.wait_ge(s["b2_in"], 16)
            copy(b2hi[:], b2[:]).then_inc(s["b2hi_set"], 1)

            side = beside()
            for g in range(B):
                for u in range(U0):
                    for c in range(C0):
                        i = g * N0 + u * C0 + c
                        act.wait_ge(s["gu_psum"], 2 * i + 1)
                        if i >= 2:
                            act.wait_ge(s["h_set"], i - 1)
                        nc.scalar.activation(sg[:, i % 2], bank[2 * (i % 2)][:], ACT.Silu).then_inc(s["silu_set"], 1)
                        if c == 0 and u + 1 < U0:
                            masked_high(g * E + u)
                        if i:
                            hidden_high(i - 1)
                        if g == 1 and u * C0 + c in W1_AT0:
                            weights1_high(W1_AT0[u * C0 + c])
                        next(side, None)
            hidden_high(B * N0 - 1)
            for g in range(B):
                for e in range(E):
                    for c in range(C1):
                        j = g * N1 + e * C1 + c
                        act.wait_ge(s["up_psum"], j + 1)
                        if j >= HB:
                            act.wait_ge(s["lo1_set"], j - HB + 1)
                        else:
                            act.wait_ge(s["hlo_set"], B * N0 - HB + j + 1)
                        bias = pb[:, PB_["b1"] + e * C1 + c:PB_["b1"] + e * C1 + c + 1]
                        nc.scalar.activation(h[:, j % HB], bank[j % 3][:], ACT.Gelu, bias=bias).then_inc(s["gelu_set"], 1)
                        if j % 2:
                            if j >= HR:
                                act.wait_ge(s["down1_done"], j - HR + 1)
                            else:
                                act.wait_ge(s["down0_done"], B * N0 - HR + j + 1)
                            nc.scalar.activation(hhi[:, j % HR], bank[j % 3][:], ACT.Gelu,
                                                 bias=bias).then_inc(s["gelu_hi_set"], 1)
                        if c == 2:
                            n = g * E + e
                            act.wait_ge(s["cb_psum"], n + 1)
                            if n >= 2:
                                act.wait_ge(s["ym_set"], n - 1)
                            copy(cbs[:, n % 2], bank[5][:]).then_inc(s["cbs_set"], 1)
                        if g == 0 and e * C1 + c in W1_AT1:
                            weights1_high(W1_AT1[e * C1 + c])
                        next(side, None)

        @block.vector
        def _(dve):
            v = nc.vector

            def statistics(stage, g):
                n = ln_count(stage, g)
                for t in range(T):
                    v.bn_stats(st[:, t], X[:, g, t]).then_inc(s["stats_set"], 1)
                for t in range(T):
                    dve.wait_ge(s["stats_set"], (n - 1) * T + t + 1)
                    v.bn_aggr(mv[:, t], st[:, t]).then_inc(s["aggr_set"], 1)
                dve.wait_ge(s["aggr_set"], n * T)
                if stage == "b":
                    v.tensor_scalar(ve[:], mv[:, :, 1], 1.0 + RMS_EPS, RMS_EPS * LN_EPS, ALU.mult,
                                    ALU.add).then_inc(s["ve_set"], 1)
                else:
                    v.tensor_scalar(ve[:], mv[:, :, 1], LN_EPS, None, ALU.add).then_inc(s["ve_set"], 1)

            def normalise(stage, g, out_):
                dve.wait_ge(s["rstd_set"], ln_count(stage, g))
                for t in range(T):
                    last = v.tensor_scalar(out_[:, t], X[:, g, t], mv[:, t, 0:1], rstd[:, t:t + 1],
                                           ALU.subtract, ALU.mult)
                last.then_inc(s["za_set" if stage in "ab" else "zf_set"], 1)

            def setup0():
                dve.wait_ge(s["mask_in"], 16)
                for k, fill in enumerate((MASKED0, MASKED1)):
                    last = v.tensor_scalar(maskb[:, k], mask_u8[:, k], -1.0, fill, ALU.add, ALU.mult)
                last.then_inc(s["maskb_set"], 1)
                dve.wait_ge(s["kv0_psum"], 1)
                for b in range(B):
                    last = v.tensor_tensor(Kbd[:, b], over_rows(bank[7][:, b * SC:(b + 1) * SC], H0),
                                           over_cols(a_("bm0s", H0), SC), ALU.mult)
                last.then_inc(s["kbd0_set"], 1)
                for b in range(B):
                    last = v.tensor_tensor(Vbd[:, b], over_rows(bank[7][:, (B + b) * SC:(B + b + 1) * SC], H0),
                                           over_cols(a_("bm0", H0), SC), ALU.mult)
                last.then_inc(s["vbd0_set"], 1)

            def setup1_weights():
                dve.wait_ge(s["ctx_in"], 16)
                v.tensor_tensor(csq[:], ctx_sb[:], ctx_sb[:], ALU.mult).then_inc(s["csq_set"], 1)
                dve.wait_ge(s["csq_set"], 1)
                v.reduce_sum(cms[:], csq[:], AX_X).then_inc(s["csq_set"], 1)
                dve.wait_ge(s["csq_set"], 2)
                v.tensor_scalar(cve[:], cms[:], 1.0 / D, RMS_EPS, ALU.mult, ALU.add).then_inc(s["cve_set"], 1)
                dve.wait_ge(s["pb_in"], 16)
                v.tensor_scalar(rms1[:], b_("rms", 1), 1.0, None, ALU.add).then_inc(s["rms1_set"], 1)
                dve.wait_ge(s["rms1_set"], 1)
                q4 = b_("qw", P).rearrange("p (h d) -> p h d", h=H1)
                half = HD1 // 2
                v.tensor_scalar(wq1[:], q4, rms1[:], None, ALU.mult)
                v.tensor_scalar(wq1s[:, :, 0:half], q4[:, :, half:HD1], rms1[:], None, ALU.mult)
                v.tensor_scalar(wq1s[:, :, half:HD1], q4[:, :, 0:half], rms1[:], None, ALU.mult)
                kw = b_("kw", HD1)
                v.tensor_scalar(wk1[:], over_rows(kw, H1), rms1[:], None, ALU.mult)
                v.tensor_scalar(wk1s[:, :, 0:half], over_rows(kw[:, half:HD1], H1), rms1[:], None, ALU.mult)
                v.tensor_scalar(wk1s[:, :, half:HD1], over_rows(kw[:, 0:half], H1), rms1[:], None, ALU.mult)
                v.tensor_scalar(wv1[:], over_rows(b_("vw", HD1), H1), rms1[:], None,
                                ALU.mult).then_inc(s["wts1_set"], 1)

            def setup1_keys():
                dve.wait_ge(s["kv1_psum"], 1)
                kv = bank[2][:, 0:3 * B * SC].rearrange("p (k b s) -> p k b s", k=3, b=B)
                v.tensor_tensor(kr[:, 0], kv[:, 0], over_rows(b_("cosk", SC), B), ALU.mult)
                v.tensor_tensor(kr[:, 1], kv[:, 1], over_rows(b_("sink", SC), B), ALU.mult).then_inc(s["kr_parts"], 1)
                dve.wait_ge(s["kr_parts"], 1)
                v.tensor_tensor(kr[:, 2], kr[:, 0], kr[:, 1], ALU.add).then_inc(s["kr_set"], 1)
                for b in range(B):
                    v.tensor_tensor(Vbd1[:, b], over_rows(kv[:, 2, b], H1), over_cols(b_("bm1", H1), SC), ALU.mult)
                dve.wait_ge(s["kr_set"], 1)
                for b in range(B):
                    last = v.tensor_tensor(Kbd1[:, b], over_rows(kr[:, 2, b], H1), over_cols(b_("bm1s", H1), SC),
                                           ALU.mult)
                last.then_inc(s["kvbd1_set"], 1)

            def add_x(g, src):
                v.tensor_tensor(X[:, g], X[:, g], tiles(src), ALU.add).then_inc(s["x_updated"], 1)

            def weights_high(w):
                dve.wait_ge(w_in[w % RAW], 16 * (w // RAW + 1))
                v.tensor_copy(w0hi[:, w], raw[:, w % RAW, 0:W0C]).then_inc(s["w0hi_set"], 1)

            def split_rows(layer, g):
                n = r_count(layer, g)
                dve.wait_ge(s["zfT_psum"], n)
                if n > 1:
                    dve.wait_ge(s["lg_psum"], n - 1)
                dve.wait_ge(s["zhi_set"], n)
                v.tensor_copy(zF32[:], bank[7][:]).then_inc(s["zF32_set"], 1)
                v.tensor_tensor(zlo[:, g], bank[7][:], zhi[:, g].bitcast(F32), ALU.subtract).then_inc(s["zlo_set"], 1)

            def route(layer, g):
                n = r_count(layer, g)
                dve.wait_ge(s["lg_psum"], n)
                v.tensor_copy(lg[:], bank[6][:, 0:T * E].rearrange("p (t e) -> p t e", t=T)).then_inc(s["lg_set"], 1)
                dve.wait_ge(s["lg_set"], n)
                for t in range(T):
                    v.max(top[:, t], lg[:, t]).then_inc(s["top_set"], 1)
                for t in range(T):
                    dve.wait_ge(s["top_set"], (n - 1) * T + t + 1)
                    last = v.max_index(ix[:, t], top[:, t], lg[:, t])
                last.then_inc(s["ix_set"], 1)
                if layer:
                    v.tensor_tensor(df[:], top[:, :, 0], top[:, :, 1], ALU.subtract).then_inc(s["df_set"], 1)
                dve.wait_ge(s["ix_set"], n)
                v.tensor_copy(ixf[:], ix[:, :, 0:2]).then_inc(s["ixf_set"], 1)
                dve.wait_ge(s["ixf_set"], n)
                v.tensor_tensor(oh[:], over_rows(b_("iota", E), T), over_cols(ixf[:, :, 0], E),
                                ALU.is_equal).then_inc(s["oh_set"], 1)

            def less_maximum0(g, t):
                n = g * T + t
                dve.wait_ge(s["s_psum"], n + 1)
                scores = bank[6 + t % 2][:].rearrange("p (h s) -> p h s", h=H0)
                v.reduce_max(mx0[:, t], scores, AX_X).then_inc(s["mx0_set"], 1)
                dve.wait_ge(s["mx0_set"], n + 1)
                if g:
                    dve.wait_ge(s["pT_psum"], (g - 1) * T + t + 1)
                v.tensor_tensor(Sc[:, t], scores, over_cols(mx0[:, t], SC), ALU.subtract).then_inc(s["s_sub"], 1)

            def attention0(g):
                for k in range(ATT0["_n"]):
                    if k == ATT0["stats"]:
                        dve.wait_ge(x_in[g], 16)
                        statistics("a", g)
                    if k == ATT0["normed"]:
                        if g:
                            dve.wait_ge(s["zaT_psum"], g)
                        normalise("a", g, ZA)
                        if g == 0:
                            setup0()
                    for kk, t0 in ((ATT0["sub01"], 0), (ATT0["sub23"], 2)):
                        if k == kk:
                            less_maximum0(g, t0)
                            less_maximum0(g, t0 + 1)
                    if k == ATT0["sums"]:
                        for t in range(T):
                            n = g * T + t
                            dve.wait_ge(s["s_exp"], n + 1)
                            v.reduce_sum(sm0[:, t], Sc[:, t], AX_X).then_inc(s["sm0_set"], 1)
                            dve.wait_ge(s["sm0_set"], n + 1)
                            if g:
                                dve.wait_ge(s["p_norm"], (g - 1) * T + t + 1)
                            v.reciprocal(rs0[:, t], sm0[:, t]).then_inc(s["rs0_set"], 1)
                        if g == 0:
                            weights_high(0)
                            setup1_weights()
                            weights_high(1)
                            weights_high(2)
                    if k == ATT0["add"]:
                        dve.wait_ge(s["o_psum"], g + 1)
                        add_x(g, bank[6][:])
                        dve.wait_ge(s["x_updated"], x_count("a", g))
                        statistics("A", g)
                        if g == 0:
                            dve.wait_ge(s["crs_set"], 1)
                            v.tensor_scalar(mn[:], ctx_sb[:], crs[:], None, ALU.mult).then_inc(s["mn_set"], 1)
                    if k == ATT0["normed2"]:
                        normalise("A", g, ZF[:, g])
                    if k == ATT0["turned2"]:
                        split_rows(0, g)
                    if k == ATT0["route"]:
                        route(0, g)
                        dve.wait_ge(s["th_set"], r_count(0, g))
                        v.tensor_scalar(sc[:, :, 0], th[:], 0.5, 0.5, ALU.mult, ALU.add).then_inc(s["sc_set"], 1)
                        dve.wait_ge(s["sc_set"], g + 1)
                        dve.wait_ge(s["oh_set"], r_count(0, g))
                        v.tensor_tensor(ohs[:, g], oh[:], over_cols(sc[:, :, 0], E), ALU.mult).then_inc(s["ohs_set"], 1)
                        if g == 0:
                            setup1_keys()
                    yield

            def attention1(g):
                for k in range(ATT1["_n"]):
                    if k == ATT1["add_y"]:
                        dve.wait_ge(s["yT_psum"], g + 1)
                        add_x(g, bank[6][:])
                        dve.wait_ge(s["x_updated"], x_count("f", g))
                        statistics("b", g)
                    if k == ATT1["normed"]:
                        dve.wait_ge(s["zaT_psum"], B + g)
                        normalise("b", g, ZA)
                    if k == ATT1["rotate"]:
                        dve.wait_ge(s["q_psum"], 2 * g + 1)
                        dve.wait_ge(s["rope_in"], 16)
                        if g:
                            dve.wait_ge(s["l1_psum"], g)
                        v.tensor_tensor(qr[:, 0], bank[6][:], rope[:, 0], ALU.mult)
                        dve.wait_ge(s["q_psum"], 2 * g + 2)
                        v.tensor_tensor(qr[:, 1], bank[7][:], rope[:, 1], ALU.mult).then_inc(s["q_sin"], 1)
                    if k == ATT1["softmax"]:
                        dve.wait_ge(s["l1_psum"], g + 1)
                        logits = bank[6][:].rearrange("p (n s) -> p n s", s=SC)
                        v.reduce_max(mx1[:], logits, AX_X).then_inc(s["mx1_set"], 1)
                        dve.wait_ge(s["mx1_set"], g + 1)
                        if g:
                            dve.wait_ge(s["p1T_psum"], g)
                        v.tensor_tensor(S1[:], logits, over_cols(mx1[:], SC), ALU.subtract).then_inc(s["s1_sub"], 1)
                        dve.wait_ge(s["s1_exp"], g + 1)
                        v.reduce_sum(sm1[:], S1[:], AX_X).then_inc(s["sm1_set"], 1)
                        dve.wait_ge(s["sm1_set"], g + 1)
                        v.reciprocal(rs1[:], sm1[:]).then_inc(s["rs1_set"], 1)
                    if k == ATT1["add"]:
                        dve.wait_ge(s["o1_psum"], g + 1)
                        add_x(g, bank[6][:])
                        dve.wait_ge(s["x_updated"], x_count("b", g))
                        statistics("B", g)
                    if k == ATT1["normed2"]:
                        dve.wait_ge(s["xm_set"], (g + 1) * E)
                        normalise("B", g, ZF[:, g])
                    if k == ATT1["turned2"]:
                        dve.wait_ge(s["gu_psum"], 2 * (g * N0 + C0))
                        split_rows(1, g)
                    if k == ATT1["route"]:
                        route(1, g)
                        v.tensor_tensor(oh2[:], over_rows(b_("iota", E), T), over_cols(ixf[:, :, 1], E),
                                        ALU.is_equal).then_inc(s["oh2_set"], 1)
                        dve.wait_ge(s["th_set"], r_count(1, g))
                        v.tensor_scalar(sc[:, :, 0], th[:], 0.5, 0.5, ALU.mult, ALU.add)
                        v.tensor_scalar(sc[:, :, 1], th[:], -0.5, 0.5, ALU.mult, ALU.add).then_inc(s["sc1_set"], 1)
                        dve.wait_ge(s["sc1_set"], g + 1)
                        dve.wait_ge(s["oh2_set"], g + 1)
                        v.tensor_tensor(oh[:], oh[:], over_cols(sc[:, :, 0], E), ALU.mult)
                        v.tensor_tensor(oh2[:], oh2[:], over_cols(sc[:, :, 1], E), ALU.mult).then_inc(s["ohw_set"], 1)
                        dve.wait_ge(s["ohw_set"], g + 1)
                        v.tensor_tensor(cmb[:], oh[:], oh2[:], ALU.add).then_inc(s["cmb_set"], 1)
                        dve.wait_ge(s["cmb_set"], g + 1)
                        if g:
                            dve.wait_ge(s["cT_psum"], g)
                        v.tensor_copy(c16[:, :, 0:E], cmb[:]).then_inc(s["c16hi_set"], 1)
                        dve.wait_ge(s["c16hi_set"], g + 1)
                        v.tensor_tensor(c16[:, :, E:2 * E], cmb[:], c16[:, :, 0:E].bitcast(F32),
                                        ALU.subtract).then_inc(s["c16_set"], 1)
                    yield

            def last_add(g):
                dve.wait_ge(s["accT_psum"], g + 1)
                add_x(g, bank[6][:])

            def beside():
                yield from attention0(1)
                yield
                yield
                yield from attention1(0)
                yield
                yield
                yield from attention1(1)

            def masked_low(n):
                dve.wait_ge(s["xmhi_set"], n + 1)
                if n >= 2:
                    dve.wait_ge(s["gu_psum"], gu_after(n - 2))
                v.tensor_tensor(xmlo[:, n % 2], bank[5][:], xmhi[:, n % 2].bitcast(F32),
                                ALU.subtract).then_inc(s["xmlo_set"], 1)

            def hidden_low(i):
                dve.wait_ge(s["hhi_set"], i + 1)
                if i >= HR:
                    dve.wait_ge(s["down0_done"], i - HR + 1)
                v.tensor_tensor(hlo[:, i % HR], h[:, i % HB], hhi[:, i % HR].bitcast(F32),
                                ALU.subtract).then_inc(s["hlo_set"], 1)

            for _ in attention0(0):
                pass
            dve.wait_ge(s["b2hi_set"], 1)
            v.tensor_tensor(b2lo[:], b2[:], b2hi[:].bitcast(F32),
                            ALU.subtract).then_inc(s["b2lo_set"], 1)

            side = beside()
            for g in range(B):
                for u in range(U0):
                    for c in range(C0):
                        i = g * N0 + u * C0 + c
                        if c == 0 and g == 0 and u + 3 < U0:
                            weights_high(u + 3)
                        dve.wait_ge(s["silu_set"], i + 1)
                        dve.wait_ge(s["gu_psum"], 2 * i + 2)
                        if i >= HB:
                            dve.wait_ge(s["hhi_set"], i - HB + 1)
                            dve.wait_ge(s["hlo_set"], i - HB + 1)
                        v.tensor_tensor(h[:, i % HB], sg[:, i % 2], bank[2 * (i % 2) + 1][:],
                                        ALU.mult).then_inc(s["h_set"], 1)
                        if c == 0 and u + 1 < U0:
                            masked_low(g * E + u)
                        if i:
                            hidden_low(i - 1)
                        next(side, None)
            hidden_low(B * N0 - 1)

            def weigh_y(n):
                dve.wait_ge(s["down1_done"], C1 * (n + 1))
                dve.wait_ge(s["cbs_set"], n + 1)
                if n >= 2:
                    dve.wait_ge(s["acc_set"], n - 1)
                v.tensor_tensor(ym[:, n % 2], bank[3 + n % 2][:], cbs[:, n % 2], ALU.mult).then_inc(s["ym_set"], 1)

            for g in range(B):
                for e in range(E):
                    for c in range(C1):
                        j = g * N1 + e * C1 + c
                        dve.wait_ge(s["gelu_set"], j + 1)
                        if j >= HR:
                            dve.wait_ge(s["down1_done"], j - HR + 1)
                        else:
                            dve.wait_ge(s["down0_done"], B * N0 - HR + j + 1)
                        if j % 2:
                            dve.wait_ge(s["gelu_hi_set"], j // 2 + 1)
                        else:
                            v.tensor_copy(hhi[:, j % HR], h[:, j % HB]).then_inc(s["hi1_set"], 1)
                            dve.wait_ge(s["hi1_set"], j // 2 + 1)
                        v.tensor_tensor(hlo[:, j % HR], h[:, j % HB], hhi[:, j % HR].bitcast(F32),
                                        ALU.subtract).then_inc(s["lo1_set"], 1)
                        if c == LAG1 and g * E + e:
                            weigh_y(g * E + e - 1)
                        if g == 1 and e == 1 and c == C1 - 1:
                            last_add(0)
                        next(side, None)
            weigh_y(B * E - 1)
            last_add(1)

        @block.tensor
        def _(pe):
            mm, tr = nc.tensor.matmul, nc.tensor.transpose

            def product(out_, hi, lo, xhi, xlo, start, stop):
                mm(out_, hi, xhi, start=start, stop=False)
                mm(out_, hi, xlo, start=False, stop=False)
                return mm(out_, lo, xhi, start=False, stop=stop)

            def transpose_tiles(dst, src):
                for t in range(T):
                    last = tr(dst[:, t * P:(t + 1) * P], src[:, t], ident)
                return last

            def scores0(g, t):
                if t >= 2:
                    pe.wait_ge(s["s_sub"], g * T + t - 1)
                elif g and t == 1:
                    pe.wait_ge(s["zlo_set"], g)
                o = bank[6 + t % 2][:]
                mm(o, zT[:, t * P:(t + 1) * P], M0[:, g], start=True, stop=False)
                mm(o, ones1[:], over_rows(maskb[:, 0, g * SC:(g + 1) * SC], H0), start=False,
                   stop=True).then_inc(s["s_psum"], 1)

            def transpose_probs0(g, t):
                pe.wait_ge(s["p_norm"], g * T + t + 1)
                if t < 2:
                    pe.wait_ge(s["s_sub"], g * T + T)
                else:
                    pe.wait_ge(s["pT_set"], g * T + t - 1)
                for c in range(4):
                    last = tr(bank[6 + t % 2][:, c * P:(c + 1) * P], Sc[:, t, 4 * c:4 * c + 4].rearrange("p h s -> p (h s)"), ident)
                last.then_inc(s["pT_psum"], 1)

            def logits(layer, g):
                n = r_count(layer, g)
                pe.wait_ge(s["zF32_set"], n)
                pe.wait_ge(s["x_updated"], x_count("b" if layer else "a", g))
                for t in range(T):
                    last = mm(bank[6][:, t * E:(t + 1) * E], zF32[:, t * P:(t + 1) * P],
                              b_("gate1" if layer else "gate0", E), start=True, stop=True)
                last.then_inc(s["lg_psum"], 1)

            def attention0(g):
                for k in range(ATT0["_n"]):
                    if k == 1 and g == 1:
                        pe.wait_ge(s["kvbd1_set"], 1)
                        pe.wait_ge(s["lg_set"], 1)
                        for b in range(B):
                            last = mm(bank[6][:, b * D:(b + 1) * D], Vbd1[:, b].rearrange("p h s -> p (h s)"),
                                      b_("ow", D), start=True, stop=True)
                        last.then_inc(s["vw1_psum"], 1)
                    if k == ATT0["turned"]:
                        pe.wait_ge(s["za_set"], g + 1)
                        if g:
                            pe.wait_ge(s["vw1_set"], 1)
                        transpose_tiles(bank[6], ZA).then_inc(s["zaT_psum"], 1)
                        if g == 0:
                            setup0_values()
                    if k == ATT0["scores01"]:
                        pe.wait_ge(s["zaT_set"], g + 1)
                        if g == 0:
                            pe.wait_ge(s["m0_set"], B)
                            pe.wait_ge(s["maskb_set"], 1)
                            pe.wait_ge(s["const_set"], 1)
                        scores0(g, 0)
                        scores0(g, 1)
                    if k == ATT0["scores23"]:
                        scores0(g, 2)
                        scores0(g, 3)
                    if k == ATT0["probs01"]:
                        transpose_probs0(g, 0)
                        transpose_probs0(g, 1)
                    if k == ATT0["probs23"]:
                        transpose_probs0(g, 2)
                        transpose_probs0(g, 3)
                    if k == ATT0["out"]:
                        pe.wait_ge(s["vw0_set"], B)
                        pe.wait_ge(s["pT_set"], (g + 1) * T)
                        for t in range(T):
                            for c in range(4):
                                last = mm(bank[6][:, t * D:(t + 1) * D], PT[:, t, c], VW0[:, g, c], start=(c == 0),
                                          stop=(c == 3))
                        last.then_inc(s["o_psum"], 1)
                        if g == 0:
                            context1()
                    if k == ATT0["turned2"]:
                        pe.wait_ge(s["zf_set"], r_count(0, g))
                        transpose_tiles(bank[7], ZF[:, g]).then_inc(s["zfT_psum"], 1)
                    if k == ATT0["logits"]:
                        logits(0, g)
                    yield

            def setup0_keys():
                pe.wait_ge(s["pa_in"], 16)
                mm(bank[7][:, 0:B * SC], a_("wkT", D), a_("ctxT", B * SC), start=True, stop=True)
                mm(bank[7][:, B * SC:2 * B * SC], a_("wvT", D), a_("ctxT", B * SC), start=True,
                   stop=True).then_inc(s["kv0_psum"], 1)
                pe.wait_ge(s["kbd0_set"], 1)
                for b in range(B):
                    mm(bank[b][:], a_("wq", D), Kbd[:, b].rearrange("p h s -> p (h s)"), start=True,
                       stop=True).then_inc(s["m0_psum"], 1)

            def setup0_values():
                pe.wait_ge(s["vbd0_set"], 1)
                for b in range(B):
                    for c in range(4):
                        last = mm(bank[2 + b][:, c * D:(c + 1) * D],
                                  Vbd[:, b, 4 * c:4 * c + 4].rearrange("p h s -> p (h s)"), a_("woT", D),
                                  start=True, stop=True)
                    last.then_inc(s["vw0_psum"], 1)

            def context1():
                pe.wait_ge(s["mn_set"], 1)
                tr(bank[0][:, 0:B * SC], mn[:], ident[0:B * SC, 0:B * SC]).then_inc(s["mnT_psum"], 1)
                pe.wait_ge(s["mnT_set"], 1)
                pe.wait_ge(s["wts1_set"], 1)
                for k, w in enumerate((wk1, wk1s, wv1)):
                    last = mm(bank[2][:, k * B * SC:(k + 1) * B * SC], w[:].rearrange("p h d -> p (h d)"), mnT[:],
                              start=True, stop=True)
                last.then_inc(s["kv1_psum"], 1)

            def attention1(g):
                for k in range(ATT1["_n"]):
                    if k == ATT1["y_turned"]:
                        pe.wait_ge(s["yT_set"], g + 1)
                        if g:
                            pe.wait_ge(s["b2c_set"], g)
                        else:
                            pe.wait_ge(s["lg_set"], B)
                        for t in range(T):
                            last = tr(bank[6][:, t * P:(t + 1) * P], yT[:, t * P:(t + 1) * P], ident)
                        last.then_inc(s["yT_psum"], 1)
                    if k == ATT1["turned"]:
                        pe.wait_ge(s["za_set"], B + g + 1)
                        transpose_tiles(bank[7], ZA).then_inc(s["zaT_psum"], 1)
                    if k == ATT1["queries"]:
                        pe.wait_ge(s["zaT_set"], B + g + 1)
                        pe.wait_ge(s["x_updated"], x_count("f", g))
                        mm(bank[6][:], wq1[:].rearrange("p h d -> p (h d)"), zT[:], start=True,
                           stop=True).then_inc(s["q_psum"], 1)
                        mm(bank[7][:], wq1s[:].rearrange("p h d -> p (h d)"), zT[:], start=True,
                           stop=True).then_inc(s["q_psum"], 1)
                    if k == ATT1["scores"]:
                        pe.wait_ge(s["q_set"], g + 1)
                        for t in range(T):
                            o = bank[6][:, t * P:(t + 1) * P]
                            mm(o, qr[:, 0, t * P:(t + 1) * P], Kbd1[:, g].rearrange("p h s -> p (h s)"), start=True,
                               stop=False)
                            last = mm(o, ones1[:], over_rows(maskb[:, 1, g * SC:(g + 1) * SC], H1), start=False,
                                      stop=True)
                        last.then_inc(s["l1_psum"], 1)
                    if k == ATT1["probs"]:
                        pe.wait_ge(s["p1_norm"], g + 1)
                        for t in range(T):
                            last = tr(bank[7][:, t * P:(t + 1) * P],
                                      S1[:, t * H1:(t + 1) * H1].rearrange("p h s -> p (h s)"), ident)
                        last.then_inc(s["p1T_psum"], 1)
                    if k == ATT1["out"]:
                        pe.wait_ge(s["p1T_set"], g + 1)
                        for t in range(T):
                            last = mm(bank[6][:, t * D:(t + 1) * D], P1T[:, t], VW1[:, g], start=True, stop=True)
                        last.then_inc(s["o1_psum"], 1)
                    if k == ATT1["turned2"]:
                        pe.wait_ge(s["zf_set"], r_count(1, g))
                        transpose_tiles(bank[7], ZF[:, g]).then_inc(s["zfT_psum"], 1)
                    if k == ATT1["logits"]:
                        logits(1, g)
                    if k == ATT1["weights"]:
                        pe.wait_ge(s["c16_set"], g + 1)
                        pe.wait_ge(s["zlo_set"], r_count(1, g))
                        for t in range(T):
                            last = tr(bank[7][0:2 * E, t * P:(t + 1) * P], c16[:, t].bitcast(F32), ident)
                        last.then_inc(s["cT_psum"], 1)
                    if k == ATT1["bias"]:
                        pe.wait_ge(s["cT_set"], g + 1)
                        pe.wait_ge(s["b2lo_set"], 1)
                        mm(bank[6][:], b2hi[:], cT16[:, g], start=True, stop=False)
                        mm(bank[6][:], b2lo[:], cT16[:, g], start=False, stop=True).then_inc(s["b2_psum"], 1)
                    yield

            def beside():
                yield from attention0(1)
                yield
                yield
                yield from attention1(0)
                yield
                yield
                yield from attention1(1)

            def transpose_sum(g):
                pe.wait_ge(s["acc_set"], (g + 1) * E)
                if g == 0:
                    pe.wait_ge(s["b2c_set"], B)
                else:
                    pe.wait_ge(s["x_updated"], x_count("o", 0))
                for t in range(T):
                    last = tr(bank[6][:, t * P:(t + 1) * P], acc[:, t * P:(t + 1) * P], ident)
                last.then_inc(s["accT_psum"], 1)

            def transpose_masked(n):
                pe.wait_ge(s["xm_set"], n + 1)
                if n:
                    pe.wait_ge(s["xmlo_set"], n)
                transpose_tiles(bank[5], xm[:, n % 2]).then_inc(s["xmT_psum"], 1)

            def down0(i):
                g, r = divmod(i, N0)
                u, c = divmod(r, C0)
                pe.wait_ge(s["hlo_set"], i + 1)
                if r == 0 and g:
                    pe.wait_ge(s["yT_set"], g)
                o = 2 * I0 + c * D
                product(bank[4][:], w0hi[:, u, o:o + D], w0lo[:, u, o:o + D], hhi[:, i % HR], hlo[:, i % HR],
                        r == 0, r == N0 - 1).then_inc(s["down0_done"], 1)

            def down1(j):
                n, c = divmod(j, C1)
                pe.wait_ge(s["lo1_set"], j + 1)
                if c == 0:
                    if n >= 2:
                        pe.wait_ge(s["ym_set"], n - 1)
                    elif n == 1:
                        pe.wait_ge(s["yT_set"], B)
                o = F1 + c * D
                e = n % E
                product(bank[3 + n % 2][:], w1hi[:, e, o:o + D], w1lo[:, e, o:o + D], hhi[:, j % HR], hlo[:, j % HR],
                        c == 0, c == C1 - 1).then_inc(s["down1_done"], 1)

            setup0_keys()
            for _ in attention0(0):
                pass
            side = beside()
            for g in range(B):
                for u in range(U0):
                    for c in range(C0):
                        i = g * N0 + u * C0 + c
                        if c == 0 and g == 0:
                            pe.wait_ge(s["w_lo_set"], u + 1)
                        if c == 0 and u:
                            pe.wait_ge(s["xmlo_set"], g * E + u)
                        elif c == 0:
                            pe.wait_ge(s["zlo_set"], g + 1)
                        n = g * E + u - 1
                        xhi, xlo = (zhi[:, g], zlo[:, g]) if u == 0 else (xmhi[:, n % 2], xmlo[:, n % 2])
                        if i >= 2:
                            pe.wait_ge(s["h_set"], i - 1)
                        elif i == 1:
                            pe.wait_ge(s["kvbd1_set"], 1)
                        for k in range(2):
                            o = k * I0 + c * P
                            product(bank[2 * (i % 2) + k][:], w0hi[:, u, o:o + P], w0lo[:, u, o:o + P], xhi, xlo, True,
                                    True).then_inc(s["gu_psum"], 1)
                        if c == 0 and u + 1 < U0:
                            transpose_masked(g * E + u)
                        if i >= LAG0:
                            down0(i - LAG0)
                        next(side, None)
            for g in range(B):
                for e in range(E):
                    for c in range(C1):
                        j = g * N1 + e * C1 + c
                        n = g * E + e
                        if c == 0 and g == 0:
                            pe.wait_ge(s["w_lo_set"], U0 + e + 1)
                        if c == 0 and e == 0:
                            pe.wait_ge(s["zlo_set"], r_count(1, g))
                        if j >= 3:
                            pe.wait_ge(s["gelu_set"], j - 2)
                            if j % 2 == 0:
                                pe.wait_ge(s["gelu_hi_set"], (j - 3) // 2 + 1)
                        else:
                            pe.wait_ge(s["h_set"], B * N0 - (j < 2))
                        product(bank[j % 3][:], w1hi[:, e, c * P:(c + 1) * P], w1lo[:, e, c * P:(c + 1) * P], zhi[:, g],
                                zlo[:, g], True, True).then_inc(s["up_psum"], 1)
                        if j < LAG0:
                            down0(B * N0 - LAG0 + j)
                        if c == 2:
                            pe.wait_ge(s["cT_set"], g + 1)
                            pe.wait_ge(s["sel_set"], 1)
                            if n:
                                pe.wait_ge(s["cbs_set"], n)
                            else:
                                pe.wait_ge(s["xmlo_set"], B * E)
                            mm(bank[5][:], selr[:, e], cT16[:, g], start=True, stop=True).then_inc(s["cb_psum"], 1)
                        if j >= LAG1:
                            down1(j - LAG1)
                        if g == 1 and e == 1 and c == C1 - 1:
                            transpose_sum(0)
                        next(side, None)
            for j in range(B * N1 - LAG1, B * N1):
                down1(j)
            transpose_sum(1)


def kernel(**inputs):
    import concourse.bacc as bacc
    from concourse.bass_utils import run_bass_kernel_spmd

    f32 = np.float32
    a = {k: np.ascontiguousarray(v) for k, v in inputs.items()}

    o = np.arange(P)
    bm0 = (o[:, None] // HD0 == np.arange(H0)[None, :]).astype(f32)
    bm1 = (o[:, None] // HD1 == np.arange(H1)[None, :]).astype(f32)
    half = HD1 // 2
    timescale = (10000.0 ** (2.0 / HD1 * np.arange(half))).astype(f32)
    lane = o % HD1
    sign = np.where(lane < half, -1.0, 1.0).astype(f32)

    def rotation(pos):
        radians = pos.astype(f32)[None, :] / timescale[lane % half][:, None]
        return np.cos(radians).astype(f32), (np.sin(radians) * sign[:, None]).astype(f32)

    cosk, sink = rotation(np.arange(SC))
    column = np.arange(S)
    cosq, sinq = rotation(SC + T * (column % P) + column // P)
    sel = (np.arange(2 * E)[:, None, None] % E == np.arange(E)[None, :, None]) * np.ones((1, 1, P))

    def cols(parts, layout):
        whole = np.concatenate([np.asarray(p_, f32).reshape(parts[0].shape[0], -1) for p_ in parts], axis=1)
        assert whole.shape[1] == layout["_end"]
        return whole

    ctx = a["ctx_1024"].reshape(B * SC, D)
    pack_a = cols([ctx.T, a["L0_xattn_Wk"].T, a["L0_xattn_Wv"].T, a["L0_xattn_Wq"], a["L0_xattn_Wo"].T, bm0,
                   bm0 * f32(HD0 ** -0.5), np.eye(P, dtype=f32)], PA_)
    qw = a["L1_xattn_q_w"].transpose(1, 0, 2).reshape(D, H1 * HD1)
    kvw = a["L1_xattn_kv_w"][:, 0]
    pack_b = cols([qw, kvw[0], kvw[1], a["L1_xattn_out_w"].reshape(H1 * HD1, D), a["L1_xattn_rms_scale"][:, None],
                   a["L0_ffn_gate_w"], a["L1_ffn_gate_w"], a["L1_ffn_b1"].reshape(E, C1, P).transpose(2, 0, 1), bm1,
                   bm1 * f32(HD1 ** -0.5), cosk, sink, np.tile(np.arange(E, dtype=f32), (P, 1))], PB_)
    selectors = sel.astype(f32).reshape(2 * E, E * P)
    b2_rows = np.concatenate([a["L1_ffn_b2"]] * 2)
    rope_q = np.stack([cosq, sinq], axis=1)
    masks = np.concatenate([a["mask_BxS2_bk1"].reshape(1, -1), a["mask_BxS2_bk0"].reshape(1, -1)],
                           axis=1)

    def rows(w, c):
        return w.reshape(c, P, -1).transpose(1, 0, 2).reshape(P, -1)

    w0 = np.stack([np.concatenate([g_, u_, rows(d_, C0)], axis=1) for g_, u_, d_ in
                   [(a["L0_ffn_sh_gate"], a["L0_ffn_sh_up"], a["L0_ffn_sh_down"])]
                   + [(a["L0_ffn_rt_gate"][e], a["L0_ffn_rt_up"][e], a["L0_ffn_rt_down"][e]) for e in range(E)]])
    w1 = np.stack([np.concatenate([a["L1_ffn_w1"][e], rows(a["L1_ffn_w2"][e], C1)], axis=1) for e in range(E)])

    nc = bacc.Bacc("TRN2", target_bir_lowering=False, num_devices=1)
    arrays, args = {}, []
    for name, v in dict(x=a["x"], pack_a=pack_a, pack_b=pack_b, selectors=selectors, b2_rows=b2_rows, rope_q=rope_q, ctx=ctx, masks=masks,
                        w0=w0, w1=w1).items():
        v = np.ascontiguousarray(v)
        arrays[f"in_{name}"] = v
        args.append(nc.dram_tensor(f"in_{name}", v.shape, mybir.dt.from_np(v.dtype), kind="ExternalInput").ap())
    out = nc.dram_tensor("out_0", (B, S, D), F32, kind="ExternalOutput").ap()
    two_moe_layers(nc, *args, out)
    r = run_bass_kernel_spmd(nc, [arrays], core_ids=[0])
    return r.results[0]["out_0"]
```

```python
from contextlib import ExitStack

import numpy as np

import concourse.bass as bass
from concourse import mybir

ALU = mybir.AluOpType
ACT = mybir.ActivationFunctionType
F32 = mybir.dt.float32
F32R = mybir.dt.float32r
BF16 = mybir.dt.bfloat16
U8 = mybir.dt.uint8
U32 = mybir.dt.uint32
AX_X = mybir.AxisListType.X

P = 128
B, S, D = 2, 512, 128
T = S // P
SC = 32
H0, H1 = 16, 4
HD0, HD1 = D // H0, D // H1
E = 8
I0 = 256
C0 = I0 // P
F1 = 512
C1 = F1 // P
U0 = E + 1
W0C = 2 * I0 + C0 * D
W1C = F1 + C1 * D
RAW = 3
LAG0, LAG1 = 3, 3
HB, HR = 3, 4
N0, N1 = U0 * C0, E * C1
LN_EPS, RMS_EPS = 1e-5, 1e-6
MASKED0, MASKED1 = 3.0e38, 2.3819763e38

ATT0 = dict(stats=0, normed=1, turned=2, scores01=2, sub01=3, scores23=3, sub23=4, sums=5, probs01=6, probs23=7,
            out=8, add=9, normed2=10, turned2=11, logits=11, route=12, _n=13)
ATT1 = dict(y=0, add_y=1, normed=2, turned=3, queries=3, rotate=4, scores=4, softmax=5, sums=6, probs=6, out=7,
            add=8, normed2=9, turned2=10, logits=10, route=11, weights=12, bias=13, _n=15)
BESIDE = {(0, 0): (0, 1), (0, 1): (2, 1), (1, 0): (2, 2)}

PA_ = dict(ctxT=0, wkT=64, wvT=192, wq=320, woT=448, bm0=576, bm0s=592, ident=608, _end=736)
PB_ = dict(qw=0, kw=128, vw=160, ow=192, rms=320, gate0=321, gate1=329, b1=337, bm1=369, bm1s=373,
           cosk=377, sink=409, iota=441, _end=449)


def two_moe_layers(nc, x, pack_a, pack_b, selectors, b2_rows, rope_q, ctx, masks, w0, w1, out):
    with ExitStack() as stack:
        def sb(name, shape, dt=F32):
            return stack.enter_context(nc.sbuf_tensor(name, shape, dt))

        def sem(name):
            return stack.enter_context(nc.semaphore(name))

        bank = [stack.enter_context(nc.psum_tensor(f"bank{i}", [P, 512], F32)) for i in range(8)]

        def tiles(ap):
            return ap.rearrange("p (t d) -> p t d", t=T)

        X = sb("X", [P, B, T, D])
        pa = sb("pa", [P, PA_["_end"]])
        pb = sb("pb", [P, PB_["_end"]])
        b2 = sb("b2", [2 * E, D])
        rope = sb("rope", [P, 2, S])
        ctx_sb = sb("ctx_sb", [B * SC, D])
        mask_u8 = sb("mask_u8", [1, 2, B * SC], U8)
        maskb = sb("maskb", [1, 2, B * SC], BF16)
        ones1 = sb("ones1", [1, P], BF16)
        neg_half = sb("neg_half", [P, T])
        KVbd = sb("KVbd", [P, 2, B, H0, SC])
        Kbd, Vbd = KVbd[:, 0], KVbd[:, 1]
        M0 = sb("M0", [P, B, 512])
        VW0 = sb("VW0", [P, B, 4, D])
        zT = sb("zT", [P, S])
        Sc = sb("Sc", [P, T, H0, SC])
        PT = KVbd[:].rearrange("p k b h s -> p (k b h s)").rearrange("p (t c q) -> p t c q", t=T, c=4)
        mx0 = sb("mx0", [P, T, H0])
        sm0 = sb("sm0", [P, T, H0])
        rs0 = sb("rs0", [P, T, H0])
        csq = sb("csq", [B * SC, D])
        cms = sb("cms", [B * SC, 1])
        cve = sb("cve", [B * SC, 1])
        crs = sb("crs", [B * SC, 1])
        mn = sb("mn", [B * SC, D])
        mnT = sb("mnT", [P, B * SC])
        rms1 = sb("rms1", [P, 1])
        wq1 = sb("wq1", [P, H1, HD1])
        wq1s = sb("wq1s", [P, H1, HD1])
        wk1 = sb("wk1", [P, H1, HD1])
        wk1s = sb("wk1s", [P, H1, HD1])
        wv1 = sb("wv1", [P, H1, HD1])
        kr = sb("kr", [P, 3, B, SC])
        Kbd1 = sb("Kbd1", [P, B, H1, SC])
        Vbd1 = sb("Vbd1", [P, B, H1, SC])
        VW1 = sb("VW1", [P, B, D])
        qr = sb("qr", [P, 2, S])
        S1 = sb("S1", [P, T * H1, SC])
        P1T = sb("P1T", [P, T, P])
        mx1 = sb("mx1", [P, T * H1])
        sm1 = sb("sm1", [P, T * H1])
        rs1 = sb("rs1", [P, T * H1])
        st = sb("st", [P, T, 6])
        mv = sb("mv", [P, T, 2])
        ve = sb("ve", [P, T])
        rstd = sb("rstd", [P, T])
        ZA = sb("ZA", [P, T, D])
        ZF = sb("ZF", [P, B, T, D])
        gates = sb("gates", [P, 2, 2, E], F32R)
        zhi = sb("zhi", [P, B, S], F32R)
        zlo = sb("zlo", [P, B, S], F32R)
        lg = sb("lg", [P, T, E])
        top = sb("top", [P, T, 8])
        ix = sb("ix", [P, T, 8], U32)
        ixf = sb("ixf", [P, T, 2])
        th = sb("th", [P, T])
        df = sb("df", [P, T])
        sc = sb("sc", [P, T, 2])
        oh = sb("oh", [P, T, E])
        oh2 = sb("oh2", [P, T, E])
        ohs = sb("ohs", [P, B, T, E])
        cmb = sb("cmb", [P, T, E])
        c16 = sb("c16", [P, T, 2 * E], F32R)
        cT16 = sb("cT16", [2 * E, B, S], F32R)
        selr = sb("selr", [2 * E, E, P], F32R)
        b2hi = sb("b2hi", [2 * E, D], F32R)
        b2lo = sb("b2lo", [2 * E, D], F32R)
        b2c = sb("b2c", [P, S])
        raw = sb("raw", [P, RAW, W1C])
        whi = sb("whi", [P, E * W1C], F32R)
        wlo = sb("wlo", [P, E * W1C], F32R)
        w0hi, w0lo = (w[:, 0:U0 * W0C].rearrange("p (u c) -> p u c", u=U0) for w in (whi, wlo))
        w1hi, w1lo = (w[:].rearrange("p (e c) -> p e c", e=E) for w in (whi, wlo))
        xm = sb("xm", [P, 2, T, D])
        xmhi = sb("xmhi", [P, 2, S], F32R)
        xmlo = sb("xmlo", [P, 2, S], F32R)
        sg = sb("sg", [P, 2, S])
        h = sb("h", [P, HB, S])
        hhi = sb("hhi", [P, HR, S], F32R)
        hlo = sb("hlo", [P, HR, S], F32R)
        yT = sb("yT", [P, S])
        cbs = sg
        ym = xm[:].rearrange("p k t d -> p k (t d)")
        sel = ym[0:2 * E].rearrange("p a b -> p (a b)")
        acc = sb("acc", [P, S])

        ident = pa[:, PA_["ident"]:PA_["ident"] + P]

        def a_(name, n):
            return pa[:, PA_[name]:PA_[name] + n]

        def b_(name, n):
            return pb[:, PB_[name]:PB_[name] + n]

        def over_rows(ap, n):
            return ap.unsqueeze(1).to_broadcast([ap.shape[0], n, ap.shape[1]])

        def over_cols(ap, n):
            return ap.unsqueeze(2).to_broadcast([ap.shape[0], ap.shape[1], n])

        names = """pa_in pb_in sel_in b2_in rope_in ctx_in mask_in out_stored
            const_set maskb_set kv0_psum kbd0_set m0_psum m0_set vbd0_set vw0_psum vw0_set
            csq_set cve_set crs_set mn_set mnT_psum mnT_set rms1_set wts1_set kv1_psum kr_parts kr_set kvbd1_set
            vw1_psum vw1_set sel_set b2hi_set b2lo_set
            stats_set aggr_set ve_set rstd_set za_set zf_set x_updated
            zaT_psum zaT_set s_psum mx0_set s_sub s_exp sm0_set rs0_set pT_psum pT_set o_psum
            zfT_psum zhi_set zlo_set gates_hi_set gates_set lg_psum lg_set top_set ix_set ixf_set oh_set th_set sc_set ohs_set
            yT_set yT_psum q_psum q_sin q_set l1_psum mx1_set s1_sub s1_exp sm1_set rs1_set p1_norm p1T_psum
            p1T_set o1_psum df_set sc1_set oh2_set ohw_set cmb_set c16hi_set c16_set cT_psum cT_set b2_psum b2c_set
            w0hi_set w1hi_set w_lo_set xm_set xmT_psum xmhi_set xmlo_set gu_psum silu_set h_set hhi_set hlo_set
            down0_done up_psum gelu_hi_set gelu_set hi1_set lo1_set down1_done cb_psum cbs_set ym_set acc_set
            accT_psum""".split()
        s = {n: sem(n) for n in names}
        x_in = [sem(f"x_in{g}") for g in range(B)]
        p_norm = [sem(f"p_norm{t}") for t in range(T)]
        w_in = [sem(f"w_in{i}") for i in range(RAW)]

        X_ORDER = [("a", 0), ("a", 1), ("f", 0), ("b", 0), ("f", 1), ("b", 1), ("o", 0), ("o", 1)]
        LN_ORDER = [("a", 0), ("A", 0), ("a", 1), ("A", 1), ("b", 0), ("B", 0), ("b", 1), ("B", 1)]

        def x_count(stage, g):
            return T * (X_ORDER.index((stage, g)) + 1)

        def ln_count(stage, g):
            return LN_ORDER.index((stage, g)) + 1

        def scores_bank(g, t):
            return bank[6 + t % 2 if g else 4 + t]

        def out_tile(g, t):
            return (bank[6] if g else bank[t])[:, t * D:(t + 1) * D]

        def r_count(layer, g):
            return layer * B + g + 1

        def gu_after(n):
            return 2 * C0 * ((n // E) * U0 + n % E + 2)

        def w1_free(e):
            units = min(U0, -(-(e + 1) * W1C // W0C))
            return N0 + units * C0

        W1_AT0 = {w1_free(e) - N0 + LAG0 + 1: e for e in range(E) if w1_free(e) - N0 + LAG0 + 1 < N0}
        W1_AT1 = {3 + 2 * k: e for k, e in enumerate(sorted(set(range(E)) - set(W1_AT0.values())))}

        def turns_masked(g, u, c):
            return u + 1 < U0 and c == (1 if g == u == 0 else 0)

        def tick(side, layer, g, slot, behind=0):
            first, every = BESIDE.get((layer, g), (slot + 1, 1))
            first += behind if every > 1 else 0
            if slot >= first and (slot - first) % every == 0:
                next(side, None)

        x_d = x.rearrange("b (p t) d -> b p (t d)", t=T)
        out_d = out.rearrange("b (p t) d -> b p (t d)", t=T)

        block = stack.enter_context(nc.Block())

        @block.sync
        def _(sp):
            sp.dma_start(X[:, 0].rearrange("p t d -> p (t d)"), x_d[0]).then_inc(x_in[0], 16)
            sp.wait_ge(s["pa_in"], 16)
            for w in range(U0 + E):
                if w == 2:
                    sp.dma_start(X[:, 1].rearrange("p t d -> p (t d)"), x_d[1]).then_inc(x_in[1], 16)
                if w >= RAW:
                    sp.wait_ge(s["w_lo_set"], w - RAW + 1)
                if w < U0:
                    sp.dma_start(raw[:, w % RAW, 0:W0C], w0[w]).then_inc(w_in[w % RAW], 16)
                else:
                    sp.dma_start(raw[:, w % RAW, :], w1[w - U0]).then_inc(w_in[w % RAW], 16)
            for g in range(B):
                sp.wait_ge(s["x_updated"], x_count("o", g))
                sp.dma_start(out_d[g], X[:, g].rearrange("p t d -> p (t d)")).then_inc(s["out_stored"], 16)
            sp.wait_ge(s["out_stored"], 16 * B)

        @block.gpsimd
        def _(pool):
            nc.gpsimd.memset(neg_half[:], -0.5)
            nc.gpsimd.memset(ones1[:], 1.0).then_inc(s["const_set"], 1)
            pool.wait_ge(s["const_set"], 1)

            def power(stage, g):
                pool.wait_ge(s["ve_set"], ln_count(stage, g))
                nc.gpsimd.tensor_tensor(rstd[:], ve[:], neg_half[:], ALU.pow).then_inc(s["rstd_set"], 1)

            def context_power():
                pool.wait_ge(s["cve_set"], 1)
                nc.gpsimd.tensor_tensor(crs[:], cve[:], neg_half[0:B * SC, 0:1], ALU.pow).then_inc(s["crs_set"], 1)

            def weights_low(w):
                r = w % RAW
                if w < U0:
                    hi, lo, c = w0hi[:, w], w0lo[:, w], W0C
                    pool.wait_ge(s["w0hi_set"], w + 1)
                else:
                    hi, lo, c = w1hi[:, w - U0], w1lo[:, w - U0], W1C
                    pool.wait_ge(s["w1hi_set"], w - U0 + 1)
                pool.wait_ge(w_in[r], 16 * (w // RAW + 1))
                nc.gpsimd.tensor_tensor(lo, raw[:, r, 0:c], hi.bitcast(F32), ALU.subtract).then_inc(s["w_lo_set"], 1)

            def normalise0(g, t):
                pool.wait_ge(s["rs0_set"], g * T + t + 1)
                nc.gpsimd.tensor_tensor(Sc[:, t], Sc[:, t],
                                        over_cols(rs0[:, t], SC), ALU.mult).then_inc(p_norm[t], 1)

            def attention0(g):
                for k in range(ATT0["_n"]):
                    if k == ATT0["stats"]:
                        power("a", g)
                    if k == ATT0["sums"]:
                        for t in range(T if g else T - 1):
                            normalise0(g, t)
                        if g == 0:
                            context_power()
                            weights_low(0)
                    if k == ATT0["add"]:
                        power("A", g)
                    yield

            def attention1(g):
                for k in range(ATT1["_n"]):
                    if k == ATT1["add_y"]:
                        power("b", g)
                    if k == ATT1["rotate"]:
                        pool.wait_ge(s["q_sin"], g + 1)
                        nc.gpsimd.tensor_tensor(qr[:, 0], qr[:, 0], qr[:, 1], ALU.add).then_inc(s["q_set"], 1)
                    if k == ATT1["sums"]:
                        pool.wait_ge(s["rs1_set"], g + 1)
                        nc.gpsimd.tensor_tensor(S1[:], S1[:], over_cols(rs1[:], SC), ALU.mult).then_inc(s["p1_norm"], 1)
                    if k == ATT1["add"]:
                        power("B", g)
                    yield

            def mask_x(n):
                g, e = divmod(n, E)
                if n == 0:
                    pool.wait_ge(s["sel_set"], 1)
                pool.wait_ge(s["ohs_set"], g + 1)
                if n >= 2:
                    pool.wait_ge(s["xmT_psum"], n - 1)
                nc.gpsimd.tensor_tensor(xm[:, n % 2], ZF[:, g], over_cols(ohs[:, g, :, e], D),
                                        ALU.mult).then_inc(s["xm_set"], 1)

            def add_y(n):
                g, e = divmod(n, E)
                pool.wait_ge(s["ym_set"], n + 1)
                if e == 0:
                    pool.wait_ge(s["b2c_set"], g + 1)
                    if g:
                        pool.wait_ge(s["accT_psum"], g)
                else:
                    pool.wait_ge(s["acc_set"], n)
                nc.gpsimd.tensor_tensor(acc[:], ym[:, n % 2], b2c[:] if e == 0 else acc[:],
                                        ALU.add).then_inc(s["acc_set"], 1)

            for _ in attention0(0):
                pass
            weights_low(1)
            weights_low(2)
            mask_x(0)
            for g in range(B):
                side = attention1(0) if g else attention0(1)
                for u in range(U0):
                    for c in range(C0):
                        tick(side, 0, g, u * C0 + c)
                        n = g * E + u + 1
                        if c == 0 and u < E and n < B * E:
                            mask_x(n)
                        if c == 1 and g == 0 and u + 3 < U0:
                            weights_low(u + 3)
                        if g == 1 and u * C0 + c in W1_AT0:
                            weights_low(U0 + W1_AT0[u * C0 + c])
            for g in range(B):
                side = attention1(1) if g == 0 else None
                for e in range(E):
                    for c in range(C1):
                        tick(side, 1, g, e * C1 + c)
                        if c == C1 - 1 and g * E + e >= 1:
                            add_y(g * E + e - 1)
                        if g == 0 and e * C1 + c in W1_AT1:
                            weights_low(U0 + W1_AT1[e * C1 + c])
            add_y(B * E - 1)

        @block.scalar
        def _(act):
            act.dma_start(pa[:], pack_a).then_inc(s["pa_in"], 16)
            act.dma_start(mask_u8[:].rearrange("p a b -> p (a b)"), masks).then_inc(s["mask_in"], 16)
            act.dma_start(pb[:], pack_b).then_inc(s["pb_in"], 16)
            act.dma_start(ctx_sb[:], ctx).then_inc(s["ctx_in"], 16)
            act.dma_start(sel, selectors).then_inc(s["sel_in"], 16)
            act.dma_start(b2[:], b2_rows).then_inc(s["b2_in"], 16)
            act.dma_start(rope[:], rope_q).then_inc(s["rope_in"], 16)

            def copy(out_, in_):
                return nc.scalar.activation(out_, in_, ACT.Copy)

            def attention0(g):
                for k in range(ATT0["_n"]):
                    if k == ATT0["turned"]:
                        act.wait_ge(s["zaT_psum"], g + 1)
                        if g:
                            act.wait_ge(s["s_psum"], T * g)
                        copy(zT[:], bank[6][:]).then_inc(s["zaT_set"], 1)
                    if k == ATT0["sub23"]:
                        for t in range(T):
                            if g == 0 and t == T - 1:
                                setup_products()
                            act.wait_ge(s["s_sub"], g * T + t + 1)
                            nc.scalar.activation(Sc[:, t], Sc[:, t], ACT.Exp).then_inc(s["s_exp"], 1)
                        if g:
                            nc.scalar.preload_act_table(ACT.Silu)
                    for kk, t0 in ((ATT0["probs01"] + 1, 0), (ATT0["probs23"] + 1, 2)):
                        if k == kk:
                            for t in (t0, t0 + 1):
                                act.wait_ge(s["pT_psum"], g * T + t + 1)
                                if g and t == 0:
                                    act.wait_ge(s["o_psum"], g * T)
                                copy(PT[:, t], tiles(scores_bank(g, t)[:])).then_inc(s["pT_set"], 1)
                    if k == ATT0["add"] and g == 0:
                        act.wait_ge(s["mnT_psum"], 1)
                        copy(mnT[:], bank[4][:, 0:B * SC]).then_inc(s["mnT_set"], 1)
                        nc.scalar.preload_act_table(ACT.Silu)
                        setup_later()
                    if k == ATT0["turned2"]:
                        act.wait_ge(s["zfT_psum"], r_count(0, g))
                        copy(zhi[:, g], bank[7][:]).then_inc(s["zhi_set"], 1)
                    if k == ATT0["route"]:
                        act.wait_ge(s["top_set"], T * r_count(0, g))
                        nc.scalar.activation(th[:], top[:, :, 0], ACT.Tanh, scale=0.5).then_inc(s["th_set"], 1)
                    if k == 1 and g == 1:
                        act.wait_ge(s["vw1_psum"], 1)
                        copy(VW1[:], bank[6][:, 0:B * D].rearrange("p (b d) -> p b d", b=B)).then_inc(s["vw1_set"], 1)
                    yield

            def attention1(g):
                for k in range(ATT1["_n"]):
                    if k == ATT1["y"]:
                        act.wait_ge(s["down0_done"], (g + 1) * N0)
                        if g:
                            act.wait_ge(s["yT_psum"], g)
                        copy(yT[:], bank[4][:]).then_inc(s["yT_set"], 1)
                    if k == ATT1["turned"]:
                        act.wait_ge(s["zaT_psum"], B + g + 1)
                        if g:
                            act.wait_ge(s["q_psum"], 2 * g)
                        else:
                            act.wait_ge(s["s_psum"], T * B)
                        copy(zT[:], bank[7][:]).then_inc(s["zaT_set"], 1)
                    if k == ATT1["softmax"]:
                        act.wait_ge(s["s1_sub"], g + 1)
                        nc.scalar.activation(S1[:], S1[:], ACT.Exp).then_inc(s["s1_exp"], 1)
                        nc.scalar.preload_act_table(ACT.Gelu if g else ACT.Silu)
                    if k == ATT1["probs"] + 1:
                        act.wait_ge(s["p1T_psum"], g + 1)
                        if g:
                            act.wait_ge(s["o1_psum"], g)
                        copy(P1T[:], tiles(bank[7][:])).then_inc(s["p1T_set"], 1)
                    if k == ATT1["turned2"]:
                        act.wait_ge(s["zfT_psum"], r_count(1, g))
                        act.wait_ge(s["gu_psum"], 2 * (g * N0 + C0))
                        copy(zhi[:, g], bank[7][:]).then_inc(s["zhi_set"], 1)
                    if k == ATT1["route"]:
                        act.wait_ge(s["df_set"], g + 1)
                        nc.scalar.activation(th[:], df[:], ACT.Tanh, scale=0.5).then_inc(s["th_set"], 1)
                    if k == ATT1["weights"] + 1:
                        act.wait_ge(s["cT_psum"], g + 1)
                        copy(cT16[:, g], bank[7][0:2 * E, :]).then_inc(s["cT_set"], 1)
                    if k == ATT1["bias"] + 1:
                        act.wait_ge(s["b2_psum"], g + 1)
                        if g:
                            act.wait_ge(s["acc_set"], 1)
                        copy(b2c[:], bank[6][:]).then_inc(s["b2c_set"], 1)
                    yield

            def masked_high(n):
                act.wait_ge(s["xmT_psum"], n + 1)
                if n >= 2:
                    act.wait_ge(s["gu_psum"], gu_after(n - 2))
                copy(xmhi[:, n % 2], bank[5][:]).then_inc(s["xmhi_set"], 1)

            def hidden_high(i):
                act.wait_ge(s["h_set"], i + 1)
                if i >= HR:
                    act.wait_ge(s["down0_done"], i - HR + 1)
                copy(hhi[:, i % HR], h[:, i % HB]).then_inc(s["hhi_set"], 1)

            def weights1_high(e):
                w = U0 + e
                act.wait_ge(w_in[w % RAW], 16 * (w // RAW + 1))
                act.wait_ge(s["down0_done"], w1_free(e))
                copy(w1hi[:, e], raw[:, w % RAW, :]).then_inc(s["w1hi_set"], 1)

            def weights0_high(w):
                act.wait_ge(w_in[w % RAW], 16 * (w // RAW + 1))
                copy(w0hi[:, w], raw[:, w % RAW, 0:W0C]).then_inc(s["w0hi_set"], 1)

            def folded_keys(b):
                act.wait_ge(s["m0_psum"], b + 1)
                copy(M0[:, b], bank[b][:]).then_inc(s["m0_set"], 1)

            def setup_products():
                folded_keys(1)
                for b in range(B):
                    act.wait_ge(s["vw0_psum"], b + 1)
                    copy(VW0[:, b], tiles(bank[2 + b][:])).then_inc(s["vw0_set"], 1)

            def setup_later():
                act.wait_ge(s["sel_in"], 16)
                copy(selr[:].rearrange("k e p -> k (e p)"), sel).then_inc(s["sel_set"], 1)
                act.wait_ge(s["b2_in"], 16)
                copy(b2hi[:], b2[:]).then_inc(s["b2hi_set"], 1)

            folded_keys(0)
            for _ in attention0(0):
                pass

            for g in range(B):
                side = attention1(0) if g else attention0(1)
                for u in range(U0):
                    for c in range(C0):
                        i = g * N0 + u * C0 + c
                        tick(side, 0, g, u * C0 + c)
                        act.wait_ge(s["gu_psum"], 2 * i + 1)
                        if i >= 2:
                            act.wait_ge(s["h_set"], i - 1)
                        nc.scalar.activation(sg[:, i % 2], bank[2 * (i % 2)][:], ACT.Silu).then_inc(s["silu_set"], 1)
                        if turns_masked(g, u, c):
                            masked_high(g * E + u)
                        if i:
                            hidden_high(i - 1)
                        if c == 1 and g == 0 and u + 3 < U0:
                            weights0_high(u + 3)
                        if g == 1 and u * C0 + c in W1_AT0:
                            weights1_high(W1_AT0[u * C0 + c])
            hidden_high(B * N0 - 1)
            nc.scalar.preload_act_table(ACT.Gelu)
            for g in range(B):
                side = attention1(1) if g == 0 else None
                for e in range(E):
                    for c in range(C1):
                        j = g * N1 + e * C1 + c
                        tick(side, 1, g, e * C1 + c)
                        act.wait_ge(s["up_psum"], j + 1)
                        if j >= HB:
                            act.wait_ge(s["lo1_set"], j - HB + 1)
                        else:
                            act.wait_ge(s["hlo_set"], B * N0 - HB + j + 1)
                        bias = pb[:, PB_["b1"] + e * C1 + c:PB_["b1"] + e * C1 + c + 1]
                        nc.scalar.activation(h[:, j % HB], bank[j % 3][:], ACT.Gelu, bias=bias).then_inc(s["gelu_set"], 1)
                        if j % 2:
                            if j >= HR:
                                act.wait_ge(s["down1_done"], j - HR + 1)
                            else:
                                act.wait_ge(s["down0_done"], B * N0 - HR + j + 1)
                            nc.scalar.activation(hhi[:, j % HR], bank[j % 3][:], ACT.Gelu,
                                                 bias=bias).then_inc(s["gelu_hi_set"], 1)
                        if c == 2:
                            n = g * E + e
                            act.wait_ge(s["cb_psum"], n + 1)
                            if n >= 2:
                                act.wait_ge(s["ym_set"], n - 1)
                            copy(cbs[:, n % 2], bank[5][:]).then_inc(s["cbs_set"], 1)
                        if g == 0 and e * C1 + c in W1_AT1:
                            weights1_high(W1_AT1[e * C1 + c])

        @block.vector
        def _(dve):
            v = nc.vector

            def statistics(stage, g, added=False):
                n = ln_count(stage, g)
                for t in range(T + 1 if added else T):
                    if added and t < T:
                        dve.wait_ge(s["o_psum"], g * T + t + 1)
                        v.tensor_tensor(X[:, g, t], X[:, g, t], out_tile(g, t),
                                        ALU.add).then_inc(s["x_updated"], 1)
                    if added and t:
                        dve.wait_ge(s["x_updated"], x_count("a", g) - T + t)
                        v.bn_stats(st[:, t - 1], X[:, g, t - 1]).then_inc(s["stats_set"], 1)
                    if not added:
                        v.bn_stats(st[:, t], X[:, g, t]).then_inc(s["stats_set"], 1)
                for t in range(T):
                    dve.wait_ge(s["stats_set"], (n - 1) * T + t + 1)
                    v.bn_aggr(mv[:, t], st[:, t]).then_inc(s["aggr_set"], 1)
                dve.wait_ge(s["aggr_set"], n * T)
                if stage == "b":
                    v.tensor_scalar(ve[:], mv[:, :, 1], 1.0 + RMS_EPS, RMS_EPS * LN_EPS, ALU.mult,
                                    ALU.add).then_inc(s["ve_set"], 1)
                else:
                    v.tensor_scalar(ve[:], mv[:, :, 1], LN_EPS, None, ALU.add).then_inc(s["ve_set"], 1)

            def normalise(stage, g, out_):
                dve.wait_ge(s["rstd_set"], ln_count(stage, g))
                for t in range(T):
                    last = v.tensor_scalar(out_[:, t], X[:, g, t], mv[:, t, 0:1], rstd[:, t:t + 1],
                                           ALU.subtract, ALU.mult)
                last.then_inc(s["za_set" if stage in "ab" else "zf_set"], 1)

            def setup0():
                dve.wait_ge(s["mask_in"], 16)
                for k, fill in enumerate((MASKED0, MASKED1)):
                    last = v.tensor_scalar(maskb[:, k], mask_u8[:, k], -1.0, fill, ALU.add, ALU.mult)
                last.then_inc(s["maskb_set"], 1)
                dve.wait_ge(s["kv0_psum"], 1)
                blocks_of_keys(0)

            def blocks_of_keys(b):
                v.tensor_tensor(Kbd[:, b], over_rows(bank[7][:, b * SC:(b + 1) * SC], H0),
                                over_cols(a_("bm0s", H0), SC), ALU.mult).then_inc(s["kbd0_set"], 1)

            def setup0_rest():
                blocks_of_keys(1)
                for b in range(B):
                    last = v.tensor_tensor(Vbd[:, b], over_rows(bank[7][:, (B + b) * SC:(B + b + 1) * SC], H0),
                                           over_cols(a_("bm0", H0), SC), ALU.mult)
                last.then_inc(s["vbd0_set"], 1)

            def setup1_weights():
                dve.wait_ge(s["ctx_in"], 16)
                v.tensor_tensor(csq[:], ctx_sb[:], ctx_sb[:], ALU.mult).then_inc(s["csq_set"], 1)
                dve.wait_ge(s["csq_set"], 1)
                v.reduce_sum(cms[:], csq[:], AX_X).then_inc(s["csq_set"], 1)
                dve.wait_ge(s["csq_set"], 2)
                v.tensor_scalar(cve[:], cms[:], 1.0 / D, RMS_EPS, ALU.mult, ALU.add).then_inc(s["cve_set"], 1)
                dve.wait_ge(s["pb_in"], 16)
                both = b_("gate0", 2 * E).rearrange("p (l e) -> p l e", l=2)
                v.tensor_copy(gates[:, :, 0], both).then_inc(s["gates_hi_set"], 1)
                dve.wait_ge(s["gates_hi_set"], 1)
                v.tensor_tensor(gates[:, :, 1], both, gates[:, :, 0].bitcast(F32),
                                ALU.subtract).then_inc(s["gates_set"], 1)
                v.tensor_scalar(rms1[:], b_("rms", 1), 1.0, None, ALU.add).then_inc(s["rms1_set"], 1)
                dve.wait_ge(s["rms1_set"], 1)
                q4 = b_("qw", P).rearrange("p (h d) -> p h d", h=H1)
                half = HD1 // 2
                v.tensor_scalar(wq1[:], q4, rms1[:], None, ALU.mult)
                v.tensor_scalar(wq1s[:, :, 0:half], q4[:, :, half:HD1], rms1[:], None, ALU.mult)
                v.tensor_scalar(wq1s[:, :, half:HD1], q4[:, :, 0:half], rms1[:], None, ALU.mult)
                kw = b_("kw", HD1)
                v.tensor_scalar(wk1[:], over_rows(kw, H1), rms1[:], None, ALU.mult)
                v.tensor_scalar(wk1s[:, :, 0:half], over_rows(kw[:, half:HD1], H1), rms1[:], None, ALU.mult)
                v.tensor_scalar(wk1s[:, :, half:HD1], over_rows(kw[:, 0:half], H1), rms1[:], None, ALU.mult)
                v.tensor_scalar(wv1[:], over_rows(b_("vw", HD1), H1), rms1[:], None,
                                ALU.mult).then_inc(s["wts1_set"], 1)

            def setup1_keys():
                dve.wait_ge(s["kv1_psum"], 1)
                kv = bank[5][:, 0:3 * B * SC].rearrange("p (k b s) -> p k b s", k=3, b=B)
                v.tensor_tensor(kr[:, 0], kv[:, 0], over_rows(b_("cosk", SC), B), ALU.mult)
                v.tensor_tensor(kr[:, 1], kv[:, 1], over_rows(b_("sink", SC), B), ALU.mult).then_inc(s["kr_parts"], 1)
                dve.wait_ge(s["kr_parts"], 1)
                v.tensor_tensor(kr[:, 2], kr[:, 0], kr[:, 1], ALU.add).then_inc(s["kr_set"], 1)
                for b in range(B):
                    v.tensor_tensor(Vbd1[:, b], over_rows(kv[:, 2, b], H1), over_cols(b_("bm1", H1), SC), ALU.mult)
                dve.wait_ge(s["kr_set"], 1)
                for b in range(B):
                    last = v.tensor_tensor(Kbd1[:, b], over_rows(kr[:, 2, b], H1), over_cols(b_("bm1s", H1), SC),
                                           ALU.mult)
                last.then_inc(s["kvbd1_set"], 1)

            def add_x(g, src):
                v.tensor_tensor(X[:, g], X[:, g], tiles(src), ALU.add).then_inc(s["x_updated"], T)

            def weights_high(w):
                dve.wait_ge(w_in[w % RAW], 16 * (w // RAW + 1))
                v.tensor_copy(w0hi[:, w], raw[:, w % RAW, 0:W0C]).then_inc(s["w0hi_set"], 1)

            def split_rows(layer, g):
                n = r_count(layer, g)
                dve.wait_ge(s["zhi_set"], n)
                v.tensor_tensor(zlo[:, g], bank[7][:], zhi[:, g].bitcast(F32), ALU.subtract).then_inc(s["zlo_set"], 1)

            def route(layer, g):
                n = r_count(layer, g)
                dve.wait_ge(s["lg_psum"], n)
                parts = bank[6][:, 0:2 * T * E].rearrange("p (t k e) -> p t k e", t=T, k=2)
                v.reduce_sum(lg[:], parts.rearrange("p t k e -> p t e k"), AX_X).then_inc(s["lg_set"], 1)
                dve.wait_ge(s["lg_set"], n)
                for t in range(T):
                    v.max(top[:, t], lg[:, t]).then_inc(s["top_set"], 1)
                for t in range(T):
                    dve.wait_ge(s["top_set"], (n - 1) * T + t + 1)
                    last = v.max_index(ix[:, t], top[:, t], lg[:, t])
                last.then_inc(s["ix_set"], 1)
                if layer:
                    v.tensor_tensor(df[:], top[:, :, 0], top[:, :, 1], ALU.subtract).then_inc(s["df_set"], 1)
                dve.wait_ge(s["ix_set"], n)
                v.tensor_copy(ixf[:], ix[:, :, 0:2]).then_inc(s["ixf_set"], 1)
                dve.wait_ge(s["ixf_set"], n)
                v.tensor_tensor(oh[:], over_rows(b_("iota", E), T), over_cols(ixf[:, :, 0], E),
                                ALU.is_equal).then_inc(s["oh_set"], 1)

            def less_maximum0(g, t):
                n = g * T + t
                dve.wait_ge(s["s_psum"], n + 1)
                scores = scores_bank(g, t)[:].rearrange("p (h s) -> p h s", h=H0)
                v.reduce_max(mx0[:, t], scores, AX_X).then_inc(s["mx0_set"], 1)
                dve.wait_ge(s["mx0_set"], n + 1)
                if g:
                    dve.wait_ge(s["pT_psum"], (g - 1) * T + t + 1)
                v.tensor_tensor(Sc[:, t], scores, over_cols(mx0[:, t], SC), ALU.subtract).then_inc(s["s_sub"], 1)

            def sums0(g, t):
                n = g * T + t
                dve.wait_ge(s["s_exp"], n + 1)
                v.reduce_sum(sm0[:, t], Sc[:, t], AX_X).then_inc(s["sm0_set"], 1)
                dve.wait_ge(s["sm0_set"], n + 1)
                if g:
                    dve.wait_ge(p_norm[t], g)
                v.reciprocal(rs0[:, t], sm0[:, t]).then_inc(s["rs0_set"], 1)

            def attention0(g):
                for k in range(ATT0["_n"]):
                    if k == ATT0["stats"]:
                        dve.wait_ge(x_in[g], 16)
                        statistics("a", g)
                        if g == 0:
                            setup0()
                    if k == ATT0["normed"]:
                        if g:
                            dve.wait_ge(s["zaT_psum"], g)
                        normalise("a", g, ZA)
                        if g == 0:
                            setup0_rest()
                    if k == ATT0["sub01"]:
                        less_maximum0(g, 0)
                        less_maximum0(g, 1)
                    if k == ATT0["sub23"]:
                        less_maximum0(g, 2)
                        if g == 0:
                            sums0(g, 0)
                            sums0(g, 1)
                        less_maximum0(g, 3)
                    if k == ATT0["sums"]:
                        for t in range(0 if g else 2, T):
                            sums0(g, t)
                        if g == 0:
                            dve.wait_ge(s["rs0_set"], T)
                            v.tensor_tensor(Sc[:, T - 1], Sc[:, T - 1], over_cols(rs0[:, T - 1], SC),
                                            ALU.mult).then_inc(p_norm[T - 1], 1)
                            weights_high(0)
                            setup1_weights()
                    if k == ATT0["add"]:
                        if g == 0:
                            dve.wait_ge(s["crs_set"], 1)
                            v.tensor_scalar(mn[:], ctx_sb[:], crs[:], None, ALU.mult).then_inc(s["mn_set"], 1)
                            statistics("A", g, added=True)
                            weights_high(1)
                            weights_high(2)
                        else:
                            dve.wait_ge(s["o_psum"], (g + 1) * T)
                            add_x(g, bank[6][:])
                            dve.wait_ge(s["x_updated"], x_count("a", g))
                            statistics("A", g)
                    if k == ATT0["normed2"]:
                        normalise("A", g, ZF[:, g])
                        if g == 0:
                            setup1_keys()
                    if k == ATT0["turned2"]:
                        split_rows(0, g)
                    if k == ATT0["route"]:
                        route(0, g)
                        dve.wait_ge(s["th_set"], r_count(0, g))
                        v.tensor_scalar(sc[:, :, 0], th[:], 0.5, 0.5, ALU.mult, ALU.add).then_inc(s["sc_set"], 1)
                        dve.wait_ge(s["sc_set"], g + 1)
                        dve.wait_ge(s["oh_set"], r_count(0, g))
                        v.tensor_tensor(ohs[:, g], oh[:], over_cols(sc[:, :, 0], E), ALU.mult).then_inc(s["ohs_set"], 1)
                    yield

            def attention1(g):
                for k in range(ATT1["_n"]):
                    if k == ATT1["add_y"]:
                        dve.wait_ge(s["yT_psum"], g + 1)
                        add_x(g, bank[6][:])
                        dve.wait_ge(s["x_updated"], x_count("f", g))
                        statistics("b", g)
                    if k == ATT1["normed"]:
                        dve.wait_ge(s["zaT_psum"], B + g)
                        normalise("b", g, ZA)
                    if k == ATT1["rotate"]:
                        dve.wait_ge(s["q_psum"], 2 * g + 1)
                        dve.wait_ge(s["rope_in"], 16)
                        if g:
                            dve.wait_ge(s["l1_psum"], g)
                        v.tensor_tensor(qr[:, 0], bank[6][:], rope[:, 0], ALU.mult)
                        dve.wait_ge(s["q_psum"], 2 * g + 2)
                        v.tensor_tensor(qr[:, 1], bank[7][:], rope[:, 1], ALU.mult).then_inc(s["q_sin"], 1)
                    if k == ATT1["softmax"]:
                        dve.wait_ge(s["l1_psum"], g + 1)
                        logits = bank[6][:].rearrange("p (n s) -> p n s", s=SC)
                        v.reduce_max(mx1[:], logits, AX_X).then_inc(s["mx1_set"], 1)
                        dve.wait_ge(s["mx1_set"], g + 1)
                        if g:
                            dve.wait_ge(s["p1T_psum"], g)
                        v.tensor_tensor(S1[:], logits, over_cols(mx1[:], SC), ALU.subtract).then_inc(s["s1_sub"], 1)
                    if k == ATT1["sums"]:
                        dve.wait_ge(s["s1_exp"], g + 1)
                        v.reduce_sum(sm1[:], S1[:], AX_X).then_inc(s["sm1_set"], 1)
                        dve.wait_ge(s["sm1_set"], g + 1)
                        v.reciprocal(rs1[:], sm1[:]).then_inc(s["rs1_set"], 1)
                    if k == ATT1["add"]:
                        dve.wait_ge(s["o1_psum"], g + 1)
                        add_x(g, bank[6][:])
                        dve.wait_ge(s["x_updated"], x_count("b", g))
                        statistics("B", g)
                    if k == ATT1["normed2"]:
                        dve.wait_ge(s["xm_set"], (g + 1) * E)
                        normalise("B", g, ZF[:, g])
                    if k == ATT1["turned2"]:
                        dve.wait_ge(s["gu_psum"], 2 * (g * N0 + C0))
                        split_rows(1, g)
                    if k == ATT1["route"]:
                        route(1, g)
                        v.tensor_tensor(oh2[:], over_rows(b_("iota", E), T), over_cols(ixf[:, :, 1], E),
                                        ALU.is_equal).then_inc(s["oh2_set"], 1)
                        dve.wait_ge(s["th_set"], r_count(1, g))
                        v.tensor_scalar(sc[:, :, 0], th[:], 0.5, 0.5, ALU.mult, ALU.add)
                        v.tensor_scalar(sc[:, :, 1], th[:], -0.5, 0.5, ALU.mult, ALU.add).then_inc(s["sc1_set"], 1)
                        dve.wait_ge(s["sc1_set"], g + 1)
                        dve.wait_ge(s["oh2_set"], g + 1)
                        v.tensor_tensor(oh[:], oh[:], over_cols(sc[:, :, 0], E), ALU.mult)
                        v.tensor_tensor(oh2[:], oh2[:], over_cols(sc[:, :, 1], E), ALU.mult).then_inc(s["ohw_set"], 1)
                        dve.wait_ge(s["ohw_set"], g + 1)
                        v.tensor_tensor(cmb[:], oh[:], oh2[:], ALU.add).then_inc(s["cmb_set"], 1)
                        dve.wait_ge(s["cmb_set"], g + 1)
                        if g:
                            dve.wait_ge(s["cT_psum"], g)
                        v.tensor_copy(c16[:, :, 0:E], cmb[:]).then_inc(s["c16hi_set"], 1)
                        dve.wait_ge(s["c16hi_set"], g + 1)
                        v.tensor_tensor(c16[:, :, E:2 * E], cmb[:], c16[:, :, 0:E].bitcast(F32),
                                        ALU.subtract).then_inc(s["c16_set"], 1)
                    yield

            def last_add(g):
                dve.wait_ge(s["accT_psum"], g + 1)
                add_x(g, bank[6][:])

            def masked_low(n):
                dve.wait_ge(s["xmhi_set"], n + 1)
                if n >= 2:
                    dve.wait_ge(s["gu_psum"], gu_after(n - 2))
                v.tensor_tensor(xmlo[:, n % 2], bank[5][:], xmhi[:, n % 2].bitcast(F32),
                                ALU.subtract).then_inc(s["xmlo_set"], 1)

            def hidden_low(i):
                dve.wait_ge(s["hhi_set"], i + 1)
                if i >= HR:
                    dve.wait_ge(s["down0_done"], i - HR + 1)
                v.tensor_tensor(hlo[:, i % HR], h[:, i % HB], hhi[:, i % HR].bitcast(F32),
                                ALU.subtract).then_inc(s["hlo_set"], 1)

            for _ in attention0(0):
                pass
            dve.wait_ge(s["b2hi_set"], 1)
            v.tensor_tensor(b2lo[:], b2[:], b2hi[:].bitcast(F32),
                            ALU.subtract).then_inc(s["b2lo_set"], 1)

            for g in range(B):
                side = attention1(0) if g else attention0(1)
                for u in range(U0):
                    for c in range(C0):
                        i = g * N0 + u * C0 + c
                        tick(side, 0, g, u * C0 + c)
                        dve.wait_ge(s["silu_set"], i + 1)
                        dve.wait_ge(s["gu_psum"], 2 * i + 2)
                        if i >= HB:
                            dve.wait_ge(s["hhi_set"], i - HB + 1)
                            dve.wait_ge(s["hlo_set"], i - HB + 1)
                        v.tensor_tensor(h[:, i % HB], sg[:, i % 2], bank[2 * (i % 2) + 1][:],
                                        ALU.mult).then_inc(s["h_set"], 1)
                        if turns_masked(g, u, c):
                            masked_low(g * E + u)
                        if i:
                            hidden_low(i - 1)
            hidden_low(B * N0 - 1)

            def weigh_y(n):
                dve.wait_ge(s["down1_done"], C1 * (n + 1))
                dve.wait_ge(s["cbs_set"], n + 1)
                if n >= 2:
                    dve.wait_ge(s["acc_set"], n - 1)
                v.tensor_tensor(ym[:, n % 2], bank[3 + n % 2][:], cbs[:, n % 2], ALU.mult).then_inc(s["ym_set"], 1)

            for g in range(B):
                side = attention1(1) if g == 0 else None
                for e in range(E):
                    for c in range(C1):
                        j = g * N1 + e * C1 + c
                        tick(side, 1, g, e * C1 + c)
                        dve.wait_ge(s["gelu_set"], j + 1)
                        if j >= HR:
                            dve.wait_ge(s["down1_done"], j - HR + 1)
                        else:
                            dve.wait_ge(s["down0_done"], B * N0 - HR + j + 1)
                        if j % 2:
                            dve.wait_ge(s["gelu_hi_set"], j // 2 + 1)
                        else:
                            v.tensor_copy(hhi[:, j % HR], h[:, j % HB]).then_inc(s["hi1_set"], 1)
                            dve.wait_ge(s["hi1_set"], j // 2 + 1)
                        v.tensor_tensor(hlo[:, j % HR], h[:, j % HB], hhi[:, j % HR].bitcast(F32),
                                        ALU.subtract).then_inc(s["lo1_set"], 1)
                        if c == LAG1 and g * E + e:
                            weigh_y(g * E + e - 1)
                        if g == 1 and e == 1 and c == C1 - 1:
                            last_add(0)
            weigh_y(B * E - 1)
            last_add(1)

        @block.tensor
        def _(pe):
            mm, tr = nc.tensor.matmul, nc.tensor.transpose

            def product(out_, hi, lo, xhi, xlo, start, stop):
                mm(out_, hi, xhi, start=start, stop=False)
                mm(out_, hi, xlo, start=False, stop=False)
                return mm(out_, lo, xhi, start=False, stop=stop)

            def transpose_tiles(dst, src):
                for t in range(T):
                    last = tr(dst[:, t * P:(t + 1) * P], src[:, t], ident)
                return last

            def scores0(g, t):
                if g and t >= 2:
                    pe.wait_ge(s["s_sub"], g * T + t - 1)
                elif g == 0 and t == 3:
                    pe.wait_ge(s["vbd0_set"], 1)
                elif g and t == 1:
                    pe.wait_ge(s["zlo_set"], g)
                o = scores_bank(g, t)[:]
                mm(o, zT[:, t * P:(t + 1) * P], M0[:, g], start=True, stop=False)
                mm(o, ones1[:], over_rows(maskb[:, 0, g * SC:(g + 1) * SC], H0), start=False,
                   stop=True).then_inc(s["s_psum"], 1)

            def transpose_probs0(g, t):
                pe.wait_ge(p_norm[t], g + 1)
                if t < 2 or g == 0:
                    pe.wait_ge(s["s_sub"], g * T + T)
                else:
                    pe.wait_ge(s["pT_set"], g * T + t - 1)
                for c in range(4):
                    last = tr(scores_bank(g, t)[:, c * P:(c + 1) * P], Sc[:, t, 4 * c:4 * c + 4].rearrange("p h s -> p (h s)"), ident)
                last.then_inc(s["pT_psum"], 1)

            def output0(g, t):
                pe.wait_ge(s["vw0_set"], B)
                pe.wait_ge(s["m0_set"], B)
                pe.wait_ge(s["pT_set"], g * T + t + 1)
                if g and t == 0:
                    pe.wait_ge(s["pT_set"], (g + 1) * T)
                for c in range(4):
                    last = mm(out_tile(g, t), PT[:, t, c], VW0[:, g, c], start=(c == 0),
                              stop=(c == 3))
                last.then_inc(s["o_psum"], 1)

            def logits(layer, g):
                n = r_count(layer, g)
                pe.wait_ge(s["zlo_set"], n)
                pe.wait_ge(s["gates_set"], 1)
                pe.wait_ge(s["x_updated"], x_count("b" if layer else "a", g))
                for t in range(T):
                    hi, lo = (z[:, g, t * P:(t + 1) * P] for z in (zhi, zlo))
                    o = bank[6][:, 2 * t * E:2 * (t + 1) * E]
                    mm(o, hi, gates[:, layer].rearrange("p k e -> p (k e)"), start=True, stop=False)
                    last = mm(o[:, 0:E], lo, gates[:, layer, 0], start=False, stop=True)
                last.then_inc(s["lg_psum"], 1)

            def attention0(g):
                for k in range(ATT0["_n"]):
                    if k == 0 and g == 1:
                        pe.wait_ge(s["kvbd1_set"], 1)
                        pe.wait_ge(s["lg_set"], 1)
                        for b in range(B):
                            last = mm(bank[6][:, b * D:(b + 1) * D], Vbd1[:, b].rearrange("p h s -> p (h s)"),
                                      b_("ow", D), start=True, stop=True)
                        last.then_inc(s["vw1_psum"], 1)
                    if k == ATT0["normed"]:
                        pe.wait_ge(s["za_set"], g + 1)
                        if g:
                            pe.wait_ge(s["vw1_set"], 1)
                        transpose_tiles(bank[6], ZA).then_inc(s["zaT_psum"], 1)
                        if g == 0:
                            keep_busy(3)
                    if k == ATT0["scores01"]:
                        pe.wait_ge(s["zaT_set"], g + 1)
                        if g == 0:
                            pe.wait_ge(s["m0_set"], 1)
                            pe.wait_ge(s["maskb_set"], 1)
                            pe.wait_ge(s["const_set"], 1)
                        scores0(g, 0)
                        scores0(g, 1)
                    if k == ATT0["scores23"]:
                        scores0(g, 2)
                        scores0(g, 3)
                        if g == 0:
                            fold_keys(1)
                            fold_values()
                    if k == ATT0["probs01"]:
                        transpose_probs0(g, 0)
                        transpose_probs0(g, 1)
                    if k == ATT0["probs23"]:
                        transpose_probs0(g, 2)
                        if g == 0:
                            output0(g, 0)
                        transpose_probs0(g, 3)
                    if k == ATT0["out"]:
                        for t in range(0 if g else 1, T):
                            output0(g, t)
                        if g == 0:
                            context1()
                    if k == ATT0["normed2"]:
                        pe.wait_ge(s["zf_set"], r_count(0, g))
                        transpose_tiles(bank[7], ZF[:, g]).then_inc(s["zfT_psum"], 1)
                    if k == ATT0["logits"]:
                        logits(0, g)
                    yield

            def keep_busy(n):
                for _ in range(n):
                    mm(bank[5][:], ones1[:], over_rows(ones1[:], T), start=True, stop=True)

            def setup0_keys():
                pe.wait_ge(s["pa_in"], 16)
                mm(bank[7][:, 0:B * SC], a_("wkT", D), a_("ctxT", B * SC), start=True, stop=True)
                mm(bank[7][:, B * SC:2 * B * SC], a_("wvT", D), a_("ctxT", B * SC), start=True,
                   stop=True).then_inc(s["kv0_psum"], 1)
                keep_busy(3)
                fold_keys(0)

            def fold_keys(b):
                pe.wait_ge(s["kbd0_set"], b + 1)
                mm(bank[b][:], a_("wq", D), Kbd[:, b].rearrange("p h s -> p (h s)"), start=True,
                   stop=True).then_inc(s["m0_psum"], 1)

            def fold_values():
                pe.wait_ge(s["vbd0_set"], 1)
                for b in range(B):
                    for c in range(4):
                        last = mm(bank[2 + b][:, c * D:(c + 1) * D],
                                  Vbd[:, b, 4 * c:4 * c + 4].rearrange("p h s -> p (h s)"), a_("woT", D),
                                  start=True, stop=True)
                    last.then_inc(s["vw0_psum"], 1)

            def context1():
                pe.wait_ge(s["mn_set"], 1)
                tr(bank[4][:, 0:B * SC], mn[:], ident[0:B * SC, 0:B * SC]).then_inc(s["mnT_psum"], 1)
                pe.wait_ge(s["mnT_set"], 1)
                pe.wait_ge(s["wts1_set"], 1)
                for k, w in enumerate((wk1, wk1s, wv1)):
                    last = mm(bank[5][:, k * B * SC:(k + 1) * B * SC], w[:].rearrange("p h d -> p (h d)"), mnT[:],
                              start=True, stop=True)
                last.then_inc(s["kv1_psum"], 1)

            def attention1(g):
                for k in range(ATT1["_n"]):
                    if k == ATT1["y"]:
                        pe.wait_ge(s["yT_set"], g + 1)
                        if g:
                            pe.wait_ge(s["b2c_set"], g)
                        else:
                            pe.wait_ge(s["lg_set"], B)
                        for t in range(T):
                            last = tr(bank[6][:, t * P:(t + 1) * P], yT[:, t * P:(t + 1) * P], ident)
                        last.then_inc(s["yT_psum"], 1)
                    if k == ATT1["normed"]:
                        pe.wait_ge(s["za_set"], B + g + 1)
                        transpose_tiles(bank[7], ZA).then_inc(s["zaT_psum"], 1)
                    if k == ATT1["queries"]:
                        pe.wait_ge(s["zaT_set"], B + g + 1)
                        pe.wait_ge(s["x_updated"], x_count("f", g))
                        mm(bank[6][:], wq1[:].rearrange("p h d -> p (h d)"), zT[:], start=True,
                           stop=True).then_inc(s["q_psum"], 1)
                        mm(bank[7][:], wq1s[:].rearrange("p h d -> p (h d)"), zT[:], start=True,
                           stop=True).then_inc(s["q_psum"], 1)
                    if k == ATT1["scores"]:
                        pe.wait_ge(s["q_set"], g + 1)
                        for t in range(T):
                            o = bank[6][:, t * P:(t + 1) * P]
                            mm(o, qr[:, 0, t * P:(t + 1) * P], Kbd1[:, g].rearrange("p h s -> p (h s)"), start=True,
                               stop=False)
                            last = mm(o, ones1[:], over_rows(maskb[:, 1, g * SC:(g + 1) * SC], H1), start=False,
                                      stop=True)
                        last.then_inc(s["l1_psum"], 1)
                    if k == ATT1["probs"]:
                        pe.wait_ge(s["p1_norm"], g + 1)
                        for t in range(T):
                            last = tr(bank[7][:, t * P:(t + 1) * P],
                                      S1[:, t * H1:(t + 1) * H1].rearrange("p h s -> p (h s)"), ident)
                        last.then_inc(s["p1T_psum"], 1)
                    if k == ATT1["out"]:
                        pe.wait_ge(s["p1T_set"], g + 1)
                        for t in range(T):
                            last = mm(bank[6][:, t * D:(t + 1) * D], P1T[:, t], VW1[:, g], start=True, stop=True)
                        last.then_inc(s["o1_psum"], 1)
                    if k == ATT1["normed2"]:
                        pe.wait_ge(s["zf_set"], r_count(1, g))
                        transpose_tiles(bank[7], ZF[:, g]).then_inc(s["zfT_psum"], 1)
                    if k == ATT1["logits"]:
                        logits(1, g)
                    if k == ATT1["weights"]:
                        pe.wait_ge(s["c16_set"], g + 1)
                        pe.wait_ge(s["zlo_set"], r_count(1, g))
                        for t in range(T):
                            last = tr(bank[7][0:2 * E, t * P:(t + 1) * P], c16[:, t].bitcast(F32), ident)
                        last.then_inc(s["cT_psum"], 1)
                    if k == ATT1["bias"]:
                        pe.wait_ge(s["cT_set"], g + 1)
                        pe.wait_ge(s["b2lo_set"], 1)
                        mm(bank[6][:], b2hi[:], cT16[:, g], start=True, stop=False)
                        mm(bank[6][:], b2lo[:], cT16[:, g], start=False, stop=True).then_inc(s["b2_psum"], 1)
                    yield

            def transpose_sum(g):
                pe.wait_ge(s["acc_set"], (g + 1) * E)
                if g == 0:
                    pe.wait_ge(s["b2c_set"], B)
                else:
                    pe.wait_ge(s["x_updated"], x_count("o", 0))
                for t in range(T):
                    last = tr(bank[6][:, t * P:(t + 1) * P], acc[:, t * P:(t + 1) * P], ident)
                last.then_inc(s["accT_psum"], 1)

            def transpose_masked(n):
                pe.wait_ge(s["xm_set"], n + 1)
                if n:
                    pe.wait_ge(s["xmlo_set"], n)
                else:
                    pe.wait_ge(s["kvbd1_set"], 1)
                transpose_tiles(bank[5], xm[:, n % 2]).then_inc(s["xmT_psum"], 1)

            def down0(i):
                g, r = divmod(i, N0)
                u, c = divmod(r, C0)
                pe.wait_ge(s["hlo_set"], i + 1)
                if r == 0 and g:
                    pe.wait_ge(s["yT_set"], g)
                o = 2 * I0 + c * D
                product(bank[4][:], w0hi[:, u, o:o + D], w0lo[:, u, o:o + D], hhi[:, i % HR], hlo[:, i % HR],
                        r == 0, r == N0 - 1).then_inc(s["down0_done"], 1)

            def down1(j):
                n, c = divmod(j, C1)
                pe.wait_ge(s["lo1_set"], j + 1)
                if c == 0:
                    if n >= 2:
                        pe.wait_ge(s["ym_set"], n - 1)
                    elif n == 1:
                        pe.wait_ge(s["yT_set"], B)
                o = F1 + c * D
                e = n % E
                product(bank[3 + n % 2][:], w1hi[:, e, o:o + D], w1lo[:, e, o:o + D], hhi[:, j % HR], hlo[:, j % HR],
                        c == 0, c == C1 - 1).then_inc(s["down1_done"], 1)

            pe.wait_ge(s["const_set"], 1)
            keep_busy(8)
            setup0_keys()
            for _ in attention0(0):
                pass
            pe.wait_ge(s["m0_set"], B)
            pe.wait_ge(s["vw0_set"], B)
            for g in range(B):
                side = attention1(0) if g else attention0(1)
                for u in range(U0):
                    for c in range(C0):
                        i = g * N0 + u * C0 + c
                        if c == 0 and g == 0:
                            pe.wait_ge(s["w_lo_set"], u + 1)
                        if c == 0 and u:
                            pe.wait_ge(s["xmlo_set"], g * E + u)
                        elif c == 0:
                            pe.wait_ge(s["zlo_set"], g + 1)
                        n = g * E + u - 1
                        xhi, xlo = (zhi[:, g], zlo[:, g]) if u == 0 else (xmhi[:, n % 2], xmlo[:, n % 2])
                        if i >= 2:
                            pe.wait_ge(s["h_set"], i - 1)
                        for k in range(2):
                            o = k * I0 + c * P
                            product(bank[2 * (i % 2) + k][:], w0hi[:, u, o:o + P], w0lo[:, u, o:o + P], xhi, xlo, True,
                                    True).then_inc(s["gu_psum"], 1)
                        if turns_masked(g, u, c):
                            transpose_masked(g * E + u)
                        if i >= LAG0:
                            down0(i - LAG0)
                        tick(side, 0, g, u * C0 + c)
            for g in range(B):
                side = attention1(1) if g == 0 else None
                for e in range(E):
                    for c in range(C1):
                        j = g * N1 + e * C1 + c
                        n = g * E + e
                        if c == 0 and g == 0:
                            pe.wait_ge(s["w_lo_set"], U0 + e + 1)
                        if c == 0 and e == 0:
                            pe.wait_ge(s["zlo_set"], r_count(1, g))
                        if j >= 3:
                            pe.wait_ge(s["gelu_set"], j - 2)
                            if j % 2 == 0:
                                pe.wait_ge(s["gelu_hi_set"], (j - 3) // 2 + 1)
                        else:
                            pe.wait_ge(s["h_set"], B * N0 - (j < 2))
                        product(bank[j % 3][:], w1hi[:, e, c * P:(c + 1) * P], w1lo[:, e, c * P:(c + 1) * P], zhi[:, g],
                                zlo[:, g], True, True).then_inc(s["up_psum"], 1)
                        if j < LAG0:
                            down0(B * N0 - LAG0 + j)
                        if c == 2:
                            pe.wait_ge(s["cT_set"], g + 1)
                            pe.wait_ge(s["sel_set"], 1)
                            if n:
                                pe.wait_ge(s["cbs_set"], n)
                            else:
                                pe.wait_ge(s["xmlo_set"], B * E)
                            mm(bank[5][:], selr[:, e], cT16[:, g], start=True, stop=True).then_inc(s["cb_psum"], 1)
                        if j >= LAG1:
                            down1(j - LAG1)
                        if g == 1 and e == 1 and c == C1 - 1:
                            transpose_sum(0)
                        tick(side, 1, g, e * C1 + c, behind=1)
            for j in range(B * N1 - LAG1, B * N1):
                down1(j)
            transpose_sum(1)


def kernel(**inputs):
    import concourse.bacc as bacc
    from concourse.bass_utils import run_bass_kernel_spmd

    f32 = np.float32
    a = {k: np.ascontiguousarray(v) for k, v in inputs.items()}

    o = np.arange(P)
    bm0 = (o[:, None] // HD0 == np.arange(H0)[None, :]).astype(f32)
    bm1 = (o[:, None] // HD1 == np.arange(H1)[None, :]).astype(f32)
    half = HD1 // 2
    timescale = (10000.0 ** (2.0 / HD1 * np.arange(half))).astype(f32)
    lane = o % HD1
    sign = np.where(lane < half, -1.0, 1.0).astype(f32)

    def rotation(pos):
        radians = pos.astype(f32)[None, :] / timescale[lane % half][:, None]
        return np.cos(radians).astype(f32), (np.sin(radians) * sign[:, None]).astype(f32)

    cosk, sink = rotation(np.arange(SC))
    column = np.arange(S)
    cosq, sinq = rotation(SC + T * (column % P) + column // P)
    sel = (np.arange(2 * E)[:, None, None] % E == np.arange(E)[None, :, None]) * np.ones((1, 1, P))

    def cols(parts, layout):
        whole = np.concatenate([np.asarray(p_, f32).reshape(parts[0].shape[0], -1) for p_ in parts], axis=1)
        assert whole.shape[1] == layout["_end"]
        return whole

    ctx = a["ctx_1024"].reshape(B * SC, D)
    pack_a = cols([ctx.T, a["L0_xattn_Wk"].T, a["L0_xattn_Wv"].T, a["L0_xattn_Wq"], a["L0_xattn_Wo"].T, bm0,
                   bm0 * f32(HD0 ** -0.5), np.eye(P, dtype=f32)], PA_)
    qw = a["L1_xattn_q_w"].transpose(1, 0, 2).reshape(D, H1 * HD1)
    kvw = a["L1_xattn_kv_w"][:, 0]
    pack_b = cols([qw, kvw[0], kvw[1], a["L1_xattn_out_w"].reshape(H1 * HD1, D), a["L1_xattn_rms_scale"][:, None],
                   a["L0_ffn_gate_w"], a["L1_ffn_gate_w"], a["L1_ffn_b1"].reshape(E, C1, P).transpose(2, 0, 1), bm1,
                   bm1 * f32(HD1 ** -0.5), cosk, sink, np.tile(np.arange(E, dtype=f32), (P, 1))], PB_)
    selectors = sel.astype(f32).reshape(2 * E, E * P)
    b2_rows = np.concatenate([a["L1_ffn_b2"]] * 2)
    rope_q = np.stack([cosq, sinq], axis=1)
    masks = np.concatenate([a["mask_BxS2_bk1"].reshape(1, -1), a["mask_BxS2_bk0"].reshape(1, -1)],
                           axis=1)

    def rows(w, c):
        return w.reshape(c, P, -1).transpose(1, 0, 2).reshape(P, -1)

    w0 = np.stack([np.concatenate([g_, u_, rows(d_, C0)], axis=1) for g_, u_, d_ in
                   [(a["L0_ffn_sh_gate"], a["L0_ffn_sh_up"], a["L0_ffn_sh_down"])]
                   + [(a["L0_ffn_rt_gate"][e], a["L0_ffn_rt_up"][e], a["L0_ffn_rt_down"][e]) for e in range(E)]])
    w1 = np.stack([np.concatenate([a["L1_ffn_w1"][e], rows(a["L1_ffn_w2"][e], C1)], axis=1) for e in range(E)])

    nc = bacc.Bacc("TRN2", target_bir_lowering=False, num_devices=1)
    arrays, args = {}, []
    for name, v in dict(x=a["x"], pack_a=pack_a, pack_b=pack_b, selectors=selectors, b2_rows=b2_rows, rope_q=rope_q, ctx=ctx, masks=masks,
                        w0=w0, w1=w1).items():
        v = np.ascontiguousarray(v)
        arrays[f"in_{name}"] = v
        args.append(nc.dram_tensor(f"in_{name}", v.shape, mybir.dt.from_np(v.dtype), kind="ExternalInput").ap())
    out = nc.dram_tensor("out_0", (B, S, D), F32, kind="ExternalOutput").ap()
    two_moe_layers(nc, *args, out)
    r = run_bass_kernel_spmd(nc, [arrays], core_ids=[0])
    return r.results[0]["out_0"]
```

```python
from contextlib import ExitStack

import numpy as np

import concourse.bass as bass
from concourse import mybir

ALU = mybir.AluOpType
ACT = mybir.ActivationFunctionType
F32 = mybir.dt.float32
F32R = mybir.dt.float32r
BF16 = mybir.dt.bfloat16
U8 = mybir.dt.uint8
U32 = mybir.dt.uint32
AX_X = mybir.AxisListType.X

P = 128
B, S, D = 2, 512, 128
T = S // P
SC = 32
H0, H1 = 16, 4
HD0, HD1 = D // H0, D // H1
E = 8
I0 = 256
C0 = I0 // P
F1 = 512
C1 = F1 // P
U0 = E + 1
W0C = 2 * I0 + C0 * D
W1C = F1 + C1 * D
RAW = 3
LAG0, LAG1 = 4, 3
OUT_PARTS = (1, 2)
EARLY = 5
HB, HR = 3, 6
N0, N1 = U0 * C0, E * C1
LN_EPS, RMS_EPS = 1e-5, 1e-6
MASKED0, MASKED1 = 3.0e38, 2.3819763e38

ATT0 = dict(stats=0, normed=1, turned=3, sub01=4, sub23=6, exp=6, sums=8, pt01=10, pt23=11, add=13, normed2=14,
            turned2=16, route=17)
ATT0_PE = dict(normed=2, scores01=3, scores23=5, probs01=9, probs23=10, out=12, normed2=15, logits=16)
ATT1 = [dict(y=3, add_y=4, normed=5, turned=7, rotate=8, softmax=10, exp=10, sums=11, pt=13, add=14, normed2=15,
             turned2=17, route=18, ct=21, b2c=22),
        dict(y=4, add_y=6, normed=8, turned=11, rotate=13, softmax=16, exp=17, sums=18, pt=21, add=24, normed2=26,
             turned2=29, route=32, ct=35, b2c=37)]
ATT1_PE = [dict(y=3, normed=6, queries=7, scores=9, probs=12, out=13, normed2=16, logits=17, weights=20, bias=21),
           dict(y=5, normed=10, queries=12, scores=15, probs=20, out=23, normed2=28, logits=31, weights=34, bias=36)]

PA_ = dict(ctxT=0, wkT=64, wvT=192, bm0s=320, bm0=336, wq=352, ident=480, woT=608, _end=736)
PA_KEYS = PA_["wq"]
PB_ = dict(qw=0, kw=128, vw=160, ow=192, rms=320, gate0=321, gate1=329, b1=337, bm1=369, bm1s=373,
           cosk=377, sink=409, iota=441, _end=449)


def two_moe_layers(nc, x, pack_a, pack_b, selectors, b2_rows, rope_q, ctx, masks, w0, w1, out):
    with ExitStack() as stack:
        def sb(name, shape, dt=F32):
            return stack.enter_context(nc.sbuf_tensor(name, shape, dt))

        def sem(name):
            return stack.enter_context(nc.semaphore(name))

        bank = [stack.enter_context(nc.psum_tensor(f"bank{i}", [P, 512], F32)) for i in range(8)]

        def tiles(ap):
            return ap.rearrange("p (t d) -> p t d", t=T)

        X = sb("X", [P, B, T, D])
        pa = sb("pa", [P, PA_["_end"]])
        pb = sb("pb", [P, PB_["_end"]])
        b2 = sb("b2", [2 * E, D])
        rope = sb("rope", [P, 2, S])
        ctx_sb = sb("ctx_sb", [B * SC, D])
        mask_u8 = sb("mask_u8", [1, 2, B * SC], U8)
        maskb = sb("maskb", [1, 2, B * SC], BF16)
        ones1 = sb("ones1", [1, P], BF16)
        neg_half = sb("neg_half", [P, T])
        KVbd = sb("KVbd", [P, 2, B, H0, SC])
        Kbd, Vbd = KVbd[:, 0], KVbd[:, 1]
        M0 = sb("M0", [P, B, 512])
        VW0 = sb("VW0", [P, B, 4, D])
        zT = sb("zT", [P, S])
        Sc = sb("Sc", [P, T, H0, SC])
        PT = KVbd[:].rearrange("p k b h s -> p (k b h s)").rearrange("p (t c q) -> p t c q", t=T, c=4)
        mx0 = sb("mx0", [P, T, H0])
        sm0 = sb("sm0", [P, T, H0])
        rs0 = sb("rs0", [P, T, H0])
        csq = sb("csq", [B * SC, D])
        cms = sb("cms", [B * SC, 1])
        cve = sb("cve", [B * SC, 1])
        crs = sb("crs", [B * SC, 1])
        mn = sb("mn", [B * SC, D])
        mnT = sb("mnT", [P, B * SC])
        rms1 = sb("rms1", [P, 1])
        wq1 = sb("wq1", [P, H1, HD1])
        wq1s = sb("wq1s", [P, H1, HD1])
        wk1 = sb("wk1", [P, H1, HD1])
        wk1s = sb("wk1s", [P, H1, HD1])
        wv1 = sb("wv1", [P, H1, HD1])
        kr = sb("kr", [P, 3, B, SC])
        Kbd1 = sb("Kbd1", [P, B, H1, SC])
        Vbd1 = sb("Vbd1", [P, B, H1, SC])
        VW1 = sb("VW1", [P, B, D])
        later = Sc[:].rearrange("p t h s -> p (t h s)")
        qr = later[:, 0:2 * S].rearrange("p (k s) -> p k s", k=2)
        S1 = later[:, 2 * S:3 * S].rearrange("p (n s) -> p n s", s=SC)
        P1T = later[:, 3 * S:4 * S].rearrange("p (t q) -> p t q", t=T)
        mx1 = sb("mx1", [P, T * H1])
        sm1 = sb("sm1", [P, T * H1])
        rs1 = sb("rs1", [P, T * H1])
        st = sb("st", [P, T, 6])
        mv = sb("mv", [P, T, 2])
        ve = sb("ve", [P, T])
        rstd = sb("rstd", [P, T])
        ZA = sb("ZA", [P, T, D])
        ZF = sb("ZF", [P, B, T, D])
        gates = sb("gates", [P, 2, 2, E], F32R)
        zhi = sb("zhi", [P, B, S], F32R)
        zlo = sb("zlo", [P, B, S], F32R)
        lg = sb("lg", [P, T, E])
        top = sb("top", [P, T, 8])
        ix = sb("ix", [P, T, 8], U32)
        ixf = sb("ixf", [P, T, 2])
        th = sb("th", [P, T])
        df = sb("df", [P, T])
        sc = sb("sc", [P, T, 2])
        oh = sb("oh", [P, T, E])
        oh2 = sb("oh2", [P, T, E])
        ohs = sb("ohs", [P, B, T, E])
        cmb = sb("cmb", [P, T, E])
        c16 = sb("c16", [P, T, 2 * E], F32R)
        cT16 = sb("cT16", [2 * E, B, S], F32R)
        selr = sb("selr", [2 * E, E, P], F32R)
        b2hi = sb("b2hi", [2 * E, D], F32R)
        b2lo = sb("b2lo", [2 * E, D], F32R)
        b2c = sb("b2c", [P, S])
        raw = sb("raw", [P, RAW, W1C])
        whi = sb("whi", [P, E * W1C], F32R)
        wlo = sb("wlo", [P, E * W1C], F32R)
        w0hi, w0lo = (w[:, 0:U0 * W0C].rearrange("p (u c) -> p u c", u=U0) for w in (whi, wlo))
        w1hi, w1lo = (w[:].rearrange("p (e c) -> p e c", e=E) for w in (whi, wlo))
        xm = sb("xm", [P, 2, T, D])
        xmhi = sb("xmhi", [P, 2, S], F32R)
        xmlo = sb("xmlo", [P, 2, S], F32R)
        sg = sb("sg", [P, 2, S])
        h = sb("h", [P, HB, S])
        hhi = sb("hhi", [P, HR, S], F32R)
        hlo = sb("hlo", [P, HR, S], F32R)
        yT = sb("yT", [P, S])
        cbs = sg
        ym = xm[:].rearrange("p k t d -> p k (t d)")
        sel = ym[0:2 * E].rearrange("p a b -> p (a b)")
        acc = sb("acc", [P, S])

        ident = pa[:, PA_["ident"]:PA_["ident"] + P]

        def a_(name, n):
            return pa[:, PA_[name]:PA_[name] + n]

        def b_(name, n):
            return pb[:, PB_[name]:PB_[name] + n]

        def over_rows(ap, n):
            return ap.unsqueeze(1).to_broadcast([ap.shape[0], n, ap.shape[1]])

        def over_cols(ap, n):
            return ap.unsqueeze(2).to_broadcast([ap.shape[0], ap.shape[1], n])

        names = """keys_in pa_in pb_in sel_in b2_in rope_in ctx_in mask_in out_stored
            const_set maskb_set kv0_psum kbd0_set m0_psum m0_set vbd0_set vw0_psum vw0_set
            csq_set cve_set crs_set mn_set mnT_psum mnT_set rms1_set wts1_set kv1_psum kr_parts kr_set kvbd1_set
            vw1_psum vw1_set sel_set b2hi_set b2lo_set
            stats_set aggr_set ve_set rstd_set za_set zf_set x_updated
            zaT_psum zaT_set s_psum mx0_set s_sub s_exp sm0_set rs0_set pT_psum pT_set o_psum
            zfT_psum zhi_set zlo_set gates_hi_set gates_set lg_psum lg_set top_set ix_set ixf_set oh_set th_set
            sc_set ohs_set
            yT_set yT_psum q_psum q_sin q_set l1_psum mx1_set s1_sub s1_exp sm1_set rs1_set p1_norm p1T_psum
            p1T_set o1_psum df_set sc1_set oh2_set ohw_set cmb_set c16hi_set c16_set cT_psum cT_set b2_psum b2c_set
            w0hi_set w1hi_set w_lo_set xm_set xmT_psum xmhi_set xmlo_set gu_psum silu_set h_set hhi_set hlo_set
            down0_done up_psum gelu_hi_set gelu_set hi1_set lo1_set down1_done cb_psum cbs_set ym_set acc_set
            accT_psum last_psum""".split()
        s = {n: sem(n) for n in names}
        x_in = [sem(f"x_in{g}") for g in range(B)]
        p_norm = [sem(f"p_norm{t}") for t in range(T)]
        w_in = [sem(f"w_in{i}") for i in range(RAW)]

        X_ORDER = [("a", 0), ("a", 1), ("f", 0), ("b", 0), ("f", 1), ("b", 1), ("o", 0), ("o", 1)]
        LN_ORDER = [("a", 0), ("A", 0), ("a", 1), ("A", 1), ("b", 0), ("B", 0), ("b", 1), ("B", 1)]

        def x_count(stage, g):
            return T * (X_ORDER.index((stage, g)) + 1)

        def ln_count(stage, g):
            return LN_ORDER.index((stage, g)) + 1

        def scores_bank(g, t):
            return bank[6 + t % 2 if g else 4 + t]

        def out_tile(g, t):
            return (bank[6] if g else bank[t])[:, t * D:(t + 1) * D]

        def last_bank(t):
            return bank[(6, 7, 1, 2)[t]]

        def r_count(layer, g):
            return layer * B + g + 1

        def gu_after(n):
            return 2 * C0 * ((n // E) * U0 + n % E + 2)

        def w1_free(e):
            units = min(U0, -(-(e + 1) * W1C // W0C))
            return N0 + units * C0

        W1_AT0 = {w1_free(e) - N0 + LAG0 + 1: e for e in range(E) if w1_free(e) - N0 + LAG0 + 1 < N0}
        W1_AT1 = {3 + 2 * k: e for k, e in enumerate(sorted(set(range(E)) - set(W1_AT0.values())))}

        def tick(*sides):
            for side in sides:
                next(side, None)

        x_d = x.rearrange("b (p t) d -> b p (t d)", t=T)
        out_d = out.rearrange("b (p t) d -> b p (t d)", t=T)

        block = stack.enter_context(nc.Block())

        @block.sync
        def _(sp):
            sp.dma_start(X[:, 0].rearrange("p t d -> p (t d)"), x_d[0]).then_inc(x_in[0], 16)
            sp.dma_start(pa[:, PA_KEYS:], pack_a[:, PA_KEYS:]).then_inc(s["pa_in"], 16)
            sp.wait_ge(s["pa_in"], 16)
            for w in range(U0 + E):
                if w == 2:
                    sp.dma_start(X[:, 1].rearrange("p t d -> p (t d)"), x_d[1]).then_inc(x_in[1], 16)
                if w >= RAW:
                    sp.wait_ge(s["w_lo_set"], w - RAW + 1)
                if w < U0:
                    sp.dma_start(raw[:, w % RAW, 0:W0C], w0[w]).then_inc(w_in[w % RAW], 16)
                else:
                    sp.dma_start(raw[:, w % RAW, :], w1[w - U0]).then_inc(w_in[w % RAW], 16)
            for g in range(B):
                parts = OUT_PARTS[g]
                for k in range(parts):
                    n = T // parts
                    sp.wait_ge(s["x_updated"], x_count("o", g) - T + (k + 1) * n)
                    sp.dma_start(out_d[g][:, k * n * D:(k + 1) * n * D],
                                 X[:, g, k * n:(k + 1) * n].rearrange("p t d -> p (t d)")).then_inc(s["out_stored"], 16)
            sp.wait_ge(s["out_stored"], 16 * sum(OUT_PARTS))

        @block.gpsimd
        def _(pool):
            nc.gpsimd.memset(neg_half[:], -0.5)
            nc.gpsimd.memset(ones1[:], 1.0).then_inc(s["const_set"], 1)
            pool.wait_ge(s["const_set"], 1)

            def power(stage, g):
                pool.wait_ge(s["ve_set"], ln_count(stage, g))
                nc.gpsimd.tensor_tensor(rstd[:], ve[:], neg_half[:], ALU.pow).then_inc(s["rstd_set"], 1)

            def context_power():
                pool.wait_ge(s["cve_set"], 1)
                nc.gpsimd.tensor_tensor(crs[:], cve[:], neg_half[0:B * SC, 0:1], ALU.pow).then_inc(s["crs_set"], 1)

            def weights_low(w):
                r = w % RAW
                if w < U0:
                    hi, lo, c = w0hi[:, w], w0lo[:, w], W0C
                    pool.wait_ge(s["w0hi_set"], w + 1)
                else:
                    hi, lo, c = w1hi[:, w - U0], w1lo[:, w - U0], W1C
                    pool.wait_ge(s["w1hi_set"], w - U0 + 1)
                pool.wait_ge(w_in[r], 16 * (w // RAW + 1))
                nc.gpsimd.tensor_tensor(lo, raw[:, r, 0:c], hi.bitcast(F32), ALU.subtract).then_inc(s["w_lo_set"], 1)

            def normalise0(g, t):
                pool.wait_ge(s["rs0_set"], g * T + t + 1)
                nc.gpsimd.tensor_tensor(Sc[:, t], Sc[:, t],
                                        over_cols(rs0[:, t], SC), ALU.mult).then_inc(p_norm[t], 1)

            def attention0(g):
                at = ATT0
                for k in range(max(at.values()) + 1):
                    if k == at["stats"]:
                        power("a", g)
                    if k == at["sums"]:
                        if g == 0:
                            weights_low(0)
                            weights_low(1)
                        for t in range(T if g else T - 1):
                            normalise0(g, t)
                        if g == 0:
                            context_power()
                            weights_low(2)
                    if k == at["add"]:
                        power("A", g)
                    yield

            def attention1(g):
                at = ATT1[g]
                for k in range(max(at.values()) + 1):
                    if k == at["add_y"]:
                        power("b", g)
                    if k == at["rotate"]:
                        pool.wait_ge(s["q_sin"], g + 1)
                        nc.gpsimd.tensor_tensor(qr[:, 0], qr[:, 0], qr[:, 1], ALU.add).then_inc(s["q_set"], 1)
                    if k == at["add"]:
                        power("B", g)
                    yield

            def mask_x(n):
                g, e = divmod(n, E)
                if n == 0:
                    pool.wait_ge(s["sel_set"], 1)
                pool.wait_ge(s["ohs_set"], g + 1)
                if n >= 2:
                    pool.wait_ge(s["xmT_psum"], n - 1)
                nc.gpsimd.tensor_tensor(xm[:, n % 2], ZF[:, g], over_cols(ohs[:, g, :, e], D),
                                        ALU.mult).then_inc(s["xm_set"], 1)

            def add_y(n):
                g, e = divmod(n, E)
                pool.wait_ge(s["ym_set"], n + 1)
                if e == 0:
                    pool.wait_ge(s["b2c_set"], g + 1)
                    if g:
                        pool.wait_ge(s["accT_psum"], g)
                else:
                    pool.wait_ge(s["acc_set"], n)
                nc.gpsimd.tensor_tensor(acc[:], ym[:, n % 2], b2c[:] if e == 0 else acc[:],
                                        ALU.add).then_inc(s["acc_set"], 1)

            for _ in attention0(0):
                pass
            for w in range(3, EARLY):
                weights_low(w)
            mask_x(0)
            beside = [attention0(1), attention1(0), attention1(1)]
            for g in range(B):
                for u in range(U0):
                    for c in range(C0):
                        tick(beside[g])
                        n = g * E + u + 1
                        if c == 0 and u < E and n < B * E:
                            mask_x(n)
                        if c == 1 and g == 0 and u + EARLY < U0:
                            weights_low(u + EARLY)
                        if g == 1 and u * C0 + c in W1_AT0:
                            weights_low(U0 + W1_AT0[u * C0 + c])
            for g in range(B):
                for e in range(E):
                    for c in range(C1):
                        tick(*beside[1 + g:])
                        if c == C1 - 1 and 1 <= g * E + e < B * E - 1:
                            add_y(g * E + e - 1)
                        if g == 0 and e * C1 + c in W1_AT1:
                            weights_low(U0 + W1_AT1[e * C1 + c])

        @block.scalar
        def _(act):
            act.dma_start(pa[:, 0:PA_KEYS], pack_a[:, 0:PA_KEYS]).then_inc(s["keys_in"], 16)
            act.dma_start(mask_u8[:].rearrange("p a b -> p (a b)"), masks).then_inc(s["mask_in"], 16)
            act.dma_start(pb[:], pack_b).then_inc(s["pb_in"], 16)
            act.dma_start(ctx_sb[:], ctx).then_inc(s["ctx_in"], 16)
            act.dma_start(sel, selectors).then_inc(s["sel_in"], 16)
            act.dma_start(b2[:], b2_rows).then_inc(s["b2_in"], 16)
            act.dma_start(rope[:], rope_q).then_inc(s["rope_in"], 16)

            def copy(out_, in_):
                return nc.scalar.activation(out_, in_, ACT.Copy)

            def attention0(g):
                at = ATT0
                for k in range(max(at.values()) + 1):
                    if k == at["turned"]:
                        act.wait_ge(s["zaT_psum"], g + 1)
                        if g:
                            act.wait_ge(s["s_psum"], T * g)
                        copy(zT[:], bank[6][:]).then_inc(s["zaT_set"], 1)
                        if g == 0:
                            weights0_high(0)
                            weights0_high(1)
                    if k == at["exp"]:
                        for t in range(T):
                            if g == 0 and t == T - 1:
                                setup_products()
                            act.wait_ge(s["s_sub"], g * T + t + 1)
                            nc.scalar.activation(Sc[:, t], Sc[:, t], ACT.Exp).then_inc(s["s_exp"], 1)
                        if g:
                            nc.scalar.preload_act_table(ACT.Silu)
                    for kk, t0 in ((at["pt01"], 0), (at["pt23"], 2)):
                        if k == kk:
                            for t in (t0, t0 + 1):
                                act.wait_ge(s["pT_psum"], g * T + t + 1)
                                if g and t == 0:
                                    act.wait_ge(s["o_psum"], g * T)
                                copy(PT[:, t], tiles(scores_bank(g, t)[:])).then_inc(s["pT_set"], 1)
                            if g == 0 and t0 == 0:
                                weights0_high(2)
                    if k == at["add"] and g == 0:
                        act.wait_ge(s["mnT_psum"], 1)
                        copy(mnT[:], bank[4][:, 0:B * SC]).then_inc(s["mnT_set"], 1)
                        nc.scalar.preload_act_table(ACT.Silu)
                        setup_later()
                        for w in range(3, EARLY):
                            weights0_high(w)
                    if k == at["turned2"]:
                        act.wait_ge(s["zfT_psum"], r_count(0, g))
                        copy(zhi[:, g], bank[7][:]).then_inc(s["zhi_set"], 1)
                    if k == at["route"]:
                        act.wait_ge(s["top_set"], T * r_count(0, g))
                        nc.scalar.activation(th[:], top[:, :, 0], ACT.Tanh, scale=0.5).then_inc(s["th_set"], 1)
                    if k == 1 and g == 1:
                        act.wait_ge(s["vw1_psum"], 1)
                        copy(VW1[:], bank[6][:, 0:B * D].rearrange("p (b d) -> p b d", b=B)).then_inc(s["vw1_set"], 1)
                    yield

            def attention1(g):
                at = ATT1[g]
                for k in range(max(at.values()) + 1):
                    if k == at["y"]:
                        act.wait_ge(s["down0_done"], (g + 1) * N0)
                        if g:
                            act.wait_ge(s["yT_psum"], g)
                        copy(yT[:], bank[4][:]).then_inc(s["yT_set"], 1)
                    if k == at["turned"]:
                        act.wait_ge(s["zaT_psum"], B + g + 1)
                        if g:
                            act.wait_ge(s["q_psum"], 2 * g)
                        else:
                            act.wait_ge(s["s_psum"], T * B)
                        copy(zT[:], bank[7][:]).then_inc(s["zaT_set"], 1)
                    if k == at["exp"]:
                        act.wait_ge(s["s1_sub"], g + 1)
                        nc.scalar.activation(S1[:], S1[:], ACT.Exp).then_inc(s["s1_exp"], 1)
                        nc.scalar.preload_act_table(ACT.Gelu if g else ACT.Silu)
                    if k == at["pt"]:
                        act.wait_ge(s["p1T_psum"], g + 1)
                        if g:
                            act.wait_ge(s["o1_psum"], g)
                        copy(P1T[:], tiles(bank[7][:])).then_inc(s["p1T_set"], 1)
                    if k == at["turned2"]:
                        act.wait_ge(s["zfT_psum"], r_count(1, g))
                        act.wait_ge(s["gu_psum"], 2 * (g * N0 + C0))
                        copy(zhi[:, g], bank[7][:]).then_inc(s["zhi_set"], 1)
                    if k == at["route"]:
                        act.wait_ge(s["df_set"], g + 1)
                        nc.scalar.activation(th[:], df[:], ACT.Tanh, scale=0.5).then_inc(s["th_set"], 1)
                    if k == at["ct"]:
                        act.wait_ge(s["cT_psum"], g + 1)
                        copy(cT16[:, g], bank[7][0:2 * E, :]).then_inc(s["cT_set"], 1)
                    if k == at["b2c"]:
                        act.wait_ge(s["b2_psum"], g + 1)
                        if g:
                            act.wait_ge(s["acc_set"], 1)
                        copy(b2c[:], bank[6][:]).then_inc(s["b2c_set"], 1)
                    yield

            def masked_high(n):
                act.wait_ge(s["xmT_psum"], n + 1)
                if n >= 2:
                    act.wait_ge(s["gu_psum"], gu_after(n - 2))
                copy(xmhi[:, n % 2], bank[5][:]).then_inc(s["xmhi_set"], 1)

            def hidden_high(i):
                act.wait_ge(s["h_set"], i + 1)
                if i >= HR:
                    act.wait_ge(s["down0_done"], i - HR + 1)
                copy(hhi[:, i % HR], h[:, i % HB]).then_inc(s["hhi_set"], 1)

            def weights1_high(e):
                w = U0 + e
                act.wait_ge(w_in[w % RAW], 16 * (w // RAW + 1))
                act.wait_ge(s["down0_done"], w1_free(e))
                copy(w1hi[:, e], raw[:, w % RAW, :]).then_inc(s["w1hi_set"], 1)

            def weights0_high(w):
                act.wait_ge(w_in[w % RAW], 16 * (w // RAW + 1))
                copy(w0hi[:, w], raw[:, w % RAW, 0:W0C]).then_inc(s["w0hi_set"], 1)

            def folded_keys(b):
                act.wait_ge(s["m0_psum"], b + 1)
                copy(M0[:, b], bank[b][:]).then_inc(s["m0_set"], 1)

            def copy_weights(n):
                act.wait_ge(s["cb_psum"], n + 1)
                if n >= 2:
                    act.wait_ge(s["ym_set"], n - 1)
                copy(cbs[:, n % 2], bank[5][:]).then_inc(s["cbs_set"], 1)

            def setup_products():
                folded_keys(1)
                for b in range(B):
                    act.wait_ge(s["vw0_psum"], b + 1)
                    copy(VW0[:, b], tiles(bank[2 + b][:])).then_inc(s["vw0_set"], 1)

            def setup_later():
                act.wait_ge(s["sel_in"], 16)
                copy(selr[:].rearrange("k e p -> k (e p)"), sel).then_inc(s["sel_set"], 1)
                act.wait_ge(s["b2_in"], 16)
                copy(b2hi[:], b2[:]).then_inc(s["b2hi_set"], 1)

            folded_keys(0)
            for _ in attention0(0):
                pass

            beside = [attention0(1), attention1(0), attention1(1)]
            for g in range(B):
                for u in range(U0):
                    for c in range(C0):
                        i = g * N0 + u * C0 + c
                        tick(beside[g])
                        act.wait_ge(s["gu_psum"], 2 * i + 1)
                        if i >= 2:
                            act.wait_ge(s["h_set"], i - 1)
                        nc.scalar.activation(sg[:, i % 2], bank[2 * (i % 2)][:], ACT.Silu).then_inc(s["silu_set"], 1)
                        if c == 0 and u + 1 < U0:
                            masked_high(g * E + u)
                        if i:
                            hidden_high(i - 1)
                        if c == 1 and g == 0 and u + EARLY < U0:
                            weights0_high(u + EARLY)
                        if g == 1 and u * C0 + c in W1_AT0:
                            weights1_high(W1_AT0[u * C0 + c])
            hidden_high(B * N0 - 1)
            nc.scalar.preload_act_table(ACT.Gelu)
            for g in range(B):
                for e in range(E):
                    for c in range(C1):
                        j = g * N1 + e * C1 + c
                        exps = j == ATT1[1]["exp"]
                        if not exps:
                            tick(*beside[1 + g:])
                        act.wait_ge(s["up_psum"], j + 1)
                        if j >= HB:
                            act.wait_ge(s["lo1_set"], j - HB + 1)
                        else:
                            act.wait_ge(s["hlo_set"], B * N0 - HB + j + 1)
                        bias = pb[:, PB_["b1"] + e * C1 + c:PB_["b1"] + e * C1 + c + 1]
                        nc.scalar.activation(h[:, j % HB], bank[j % 3][:], ACT.Gelu,
                                             bias=bias).then_inc(s["gelu_set"], 1)
                        if j % 2:
                            if j >= HR:
                                act.wait_ge(s["down1_done"], j - HR + 1)
                            else:
                                act.wait_ge(s["down0_done"], B * N0 - HR + j + 1)
                            nc.scalar.activation(hhi[:, j % HR], bank[j % 3][:], ACT.Gelu,
                                                 bias=bias).then_inc(s["gelu_hi_set"], 1)
                        if exps:
                            tick(*beside[1 + g:])
                        if c == 0 and g * E + e:
                            copy_weights(g * E + e - 1)
                        if g == 0 and e * C1 + c in W1_AT1:
                            weights1_high(W1_AT1[e * C1 + c])
            copy_weights(B * E - 1)

        @block.vector
        def _(dve):
            v = nc.vector

            def statistics(stage, g, added=False):
                n = ln_count(stage, g)
                for t in range(T + 1 if added else T):
                    if added and t < T:
                        dve.wait_ge(s["o_psum"], g * T + t + 1)
                        v.tensor_tensor(X[:, g, t], X[:, g, t], out_tile(g, t),
                                        ALU.add).then_inc(s["x_updated"], 1)
                    if added and t:
                        dve.wait_ge(s["x_updated"], x_count("a", g) - T + t)
                        v.bn_stats(st[:, t - 1], X[:, g, t - 1]).then_inc(s["stats_set"], 1)
                    if not added:
                        v.bn_stats(st[:, t], X[:, g, t]).then_inc(s["stats_set"], 1)
                for t in range(T):
                    dve.wait_ge(s["stats_set"], (n - 1) * T + t + 1)
                    v.bn_aggr(mv[:, t], st[:, t]).then_inc(s["aggr_set"], 1)
                dve.wait_ge(s["aggr_set"], n * T)
                if stage == "b":
                    v.tensor_scalar(ve[:], mv[:, :, 1], 1.0 + RMS_EPS, RMS_EPS * LN_EPS, ALU.mult,
                                    ALU.add).then_inc(s["ve_set"], 1)
                else:
                    v.tensor_scalar(ve[:], mv[:, :, 1], LN_EPS, None, ALU.add).then_inc(s["ve_set"], 1)

            def normalise(stage, g, out_):
                dve.wait_ge(s["rstd_set"], ln_count(stage, g))
                for t in range(T):
                    v.tensor_scalar(out_[:, t], X[:, g, t], mv[:, t, 0:1], rstd[:, t:t + 1], ALU.subtract,
                                    ALU.mult).then_inc(s["za_set" if stage in "ab" else "zf_set"], 1)

            def setup0():
                dve.wait_ge(s["mask_in"], 16)
                for k, fill in enumerate((MASKED0, MASKED1)):
                    last = v.tensor_scalar(maskb[:, k], mask_u8[:, k], -1.0, fill, ALU.add, ALU.mult)
                last.then_inc(s["maskb_set"], 1)
                dve.wait_ge(s["kv0_psum"], 1)
                blocks_of_keys(0)

            def blocks_of_keys(b):
                v.tensor_tensor(Kbd[:, b], over_rows(bank[7][:, b * SC:(b + 1) * SC], H0),
                                over_cols(a_("bm0s", H0), SC), ALU.mult).then_inc(s["kbd0_set"], 1)

            def setup0_rest():
                blocks_of_keys(1)
                for b in range(B):
                    last = v.tensor_tensor(Vbd[:, b], over_rows(bank[7][:, (B + b) * SC:(B + b + 1) * SC], H0),
                                           over_cols(a_("bm0", H0), SC), ALU.mult)
                last.then_inc(s["vbd0_set"], 1)

            def setup1_weights():
                dve.wait_ge(s["ctx_in"], 16)
                v.tensor_tensor(csq[:], ctx_sb[:], ctx_sb[:], ALU.mult).then_inc(s["csq_set"], 1)
                dve.wait_ge(s["csq_set"], 1)
                v.reduce_sum(cms[:], csq[:], AX_X).then_inc(s["csq_set"], 1)
                dve.wait_ge(s["csq_set"], 2)
                v.tensor_scalar(cve[:], cms[:], 1.0 / D, RMS_EPS, ALU.mult, ALU.add).then_inc(s["cve_set"], 1)
                dve.wait_ge(s["pb_in"], 16)
                both = b_("gate0", 2 * E).rearrange("p (l e) -> p l e", l=2)
                v.tensor_copy(gates[:, :, 0], both).then_inc(s["gates_hi_set"], 1)
                dve.wait_ge(s["gates_hi_set"], 1)
                v.tensor_tensor(gates[:, :, 1], both, gates[:, :, 0].bitcast(F32),
                                ALU.subtract).then_inc(s["gates_set"], 1)
                v.tensor_scalar(rms1[:], b_("rms", 1), 1.0, None, ALU.add).then_inc(s["rms1_set"], 1)
                dve.wait_ge(s["rms1_set"], 1)
                q4 = b_("qw", P).rearrange("p (h d) -> p h d", h=H1)
                half = HD1 // 2
                v.tensor_scalar(wq1[:], q4, rms1[:], None, ALU.mult)
                v.tensor_scalar(wq1s[:, :, 0:half], q4[:, :, half:HD1], rms1[:], None, ALU.mult)
                v.tensor_scalar(wq1s[:, :, half:HD1], q4[:, :, 0:half], rms1[:], None, ALU.mult)
                kw = b_("kw", HD1)
                v.tensor_scalar(wk1[:], over_rows(kw, H1), rms1[:], None, ALU.mult)
                v.tensor_scalar(wk1s[:, :, 0:half], over_rows(kw[:, half:HD1], H1), rms1[:], None, ALU.mult)
                v.tensor_scalar(wk1s[:, :, half:HD1], over_rows(kw[:, 0:half], H1), rms1[:], None, ALU.mult)
                v.tensor_scalar(wv1[:], over_rows(b_("vw", HD1), H1), rms1[:], None,
                                ALU.mult).then_inc(s["wts1_set"], 1)

            def setup1_keys():
                dve.wait_ge(s["kv1_psum"], 1)
                kv = bank[5][:, 0:3 * B * SC].rearrange("p (k b s) -> p k b s", k=3, b=B)
                v.tensor_tensor(kr[:, 0], kv[:, 0], over_rows(b_("cosk", SC), B), ALU.mult)
                v.tensor_tensor(kr[:, 1], kv[:, 1], over_rows(b_("sink", SC), B), ALU.mult).then_inc(s["kr_parts"], 1)
                dve.wait_ge(s["kr_parts"], 1)
                v.tensor_tensor(kr[:, 2], kr[:, 0], kr[:, 1], ALU.add).then_inc(s["kr_set"], 1)
                for b in range(B):
                    v.tensor_tensor(Vbd1[:, b], over_rows(kv[:, 2, b], H1), over_cols(b_("bm1", H1), SC), ALU.mult)
                dve.wait_ge(s["kr_set"], 1)
                for b in range(B):
                    last = v.tensor_tensor(Kbd1[:, b], over_rows(kr[:, 2, b], H1), over_cols(b_("bm1s", H1), SC),
                                           ALU.mult)
                last.then_inc(s["kvbd1_set"], 1)

            def add_x(g, src):
                v.tensor_tensor(X[:, g], X[:, g], tiles(src), ALU.add).then_inc(s["x_updated"], T)

            def split_rows(layer, g):
                n = r_count(layer, g)
                dve.wait_ge(s["zhi_set"], n)
                v.tensor_tensor(zlo[:, g], bank[7][:], zhi[:, g].bitcast(F32), ALU.subtract).then_inc(s["zlo_set"], 1)

            def route(layer, g):
                n = r_count(layer, g)
                dve.wait_ge(s["lg_psum"], n)
                parts = bank[6][:, 0:2 * T * E].rearrange("p (t k e) -> p t k e", t=T, k=2)
                v.reduce_sum(lg[:], parts.rearrange("p t k e -> p t e k"), AX_X).then_inc(s["lg_set"], 1)
                dve.wait_ge(s["lg_set"], n)
                for t in range(T):
                    v.max(top[:, t], lg[:, t]).then_inc(s["top_set"], 1)
                for t in range(T):
                    dve.wait_ge(s["top_set"], (n - 1) * T + t + 1)
                    last = v.max_index(ix[:, t], top[:, t], lg[:, t])
                last.then_inc(s["ix_set"], 1)
                if layer:
                    v.tensor_tensor(df[:], top[:, :, 0], top[:, :, 1], ALU.subtract).then_inc(s["df_set"], 1)
                dve.wait_ge(s["ix_set"], n)
                v.tensor_copy(ixf[:], ix[:, :, 0:2]).then_inc(s["ixf_set"], 1)
                dve.wait_ge(s["ixf_set"], n)
                v.tensor_tensor(oh[:], over_rows(b_("iota", E), T), over_cols(ixf[:, :, 0], E),
                                ALU.is_equal).then_inc(s["oh_set"], 1)

            def less_maximum0(g, t):
                n = g * T + t
                dve.wait_ge(s["s_psum"], n + 1)
                scores = scores_bank(g, t)[:].rearrange("p (h s) -> p h s", h=H0)
                v.reduce_max(mx0[:, t], scores, AX_X).then_inc(s["mx0_set"], 1)
                dve.wait_ge(s["mx0_set"], n + 1)
                if g:
                    dve.wait_ge(s["pT_psum"], (g - 1) * T + t + 1)
                v.tensor_tensor(Sc[:, t], scores, over_cols(mx0[:, t], SC), ALU.subtract).then_inc(s["s_sub"], 1)

            def sums0(g, t):
                n = g * T + t
                dve.wait_ge(s["s_exp"], n + 1)
                v.reduce_sum(sm0[:, t], Sc[:, t], AX_X).then_inc(s["sm0_set"], 1)
                dve.wait_ge(s["sm0_set"], n + 1)
                if g:
                    dve.wait_ge(p_norm[t], g)
                v.reciprocal(rs0[:, t], sm0[:, t]).then_inc(s["rs0_set"], 1)

            def attention0(g):
                at = ATT0
                for k in range(max(at.values()) + 1):
                    if k == at["stats"]:
                        dve.wait_ge(x_in[g], 16)
                        statistics("a", g)
                        if g == 0:
                            setup0()
                    if k == at["normed"]:
                        if g:
                            dve.wait_ge(s["zaT_psum"], g)
                        normalise("a", g, ZA)
                        if g == 0:
                            setup0_rest()
                    if k == at["sub01"]:
                        less_maximum0(g, 0)
                        less_maximum0(g, 1)
                    if k == at["sub23"]:
                        less_maximum0(g, 2)
                        if g == 0:
                            sums0(g, 0)
                            sums0(g, 1)
                        less_maximum0(g, 3)
                    if k == at["sums"]:
                        for t in range(0 if g else 2, T):
                            sums0(g, t)
                        if g == 0:
                            dve.wait_ge(s["rs0_set"], T)
                            v.tensor_tensor(Sc[:, T - 1], Sc[:, T - 1], over_cols(rs0[:, T - 1], SC),
                                            ALU.mult).then_inc(p_norm[T - 1], 1)
                            setup1_weights()
                    if k == at["add"]:
                        if g == 0:
                            dve.wait_ge(s["crs_set"], 1)
                            v.tensor_scalar(mn[:], ctx_sb[:], crs[:], None, ALU.mult).then_inc(s["mn_set"], 1)
                            statistics("A", g, added=True)
                        else:
                            dve.wait_ge(s["o_psum"], (g + 1) * T)
                            add_x(g, bank[6][:])
                            dve.wait_ge(s["x_updated"], x_count("a", g))
                            statistics("A", g)
                    if k == at["normed2"]:
                        normalise("A", g, ZF[:, g])
                        if g == 0:
                            setup1_keys()
                    if k == at["turned2"]:
                        split_rows(0, g)
                    if k == at["route"]:
                        route(0, g)
                        dve.wait_ge(s["th_set"], r_count(0, g))
                        v.tensor_scalar(sc[:, :, 0], th[:], 0.5, 0.5, ALU.mult, ALU.add).then_inc(s["sc_set"], 1)
                        dve.wait_ge(s["sc_set"], g + 1)
                        dve.wait_ge(s["oh_set"], r_count(0, g))
                        v.tensor_tensor(ohs[:, g], oh[:], over_cols(sc[:, :, 0], E), ALU.mult).then_inc(s["ohs_set"], 1)
                    yield

            def attention1(g):
                at = ATT1[g]
                for k in range(max(at.values()) + 1):
                    if k == at["add_y"]:
                        dve.wait_ge(s["yT_psum"], g + 1)
                        add_x(g, bank[6][:])
                        dve.wait_ge(s["x_updated"], x_count("f", g))
                        statistics("b", g)
                    if k == at["normed"]:
                        dve.wait_ge(s["zaT_psum"], B + g)
                        normalise("b", g, ZA)
                    if k == at["rotate"]:
                        dve.wait_ge(s["q_psum"], 2 * g + 1)
                        dve.wait_ge(s["rope_in"], 16)
                        if g:
                            dve.wait_ge(s["l1_psum"], g)
                        v.tensor_tensor(qr[:, 0], bank[6][:], rope[:, 0], ALU.mult)
                        dve.wait_ge(s["q_psum"], 2 * g + 2)
                        v.tensor_tensor(qr[:, 1], bank[7][:], rope[:, 1], ALU.mult).then_inc(s["q_sin"], 1)
                    if k == at["softmax"]:
                        dve.wait_ge(s["l1_psum"], g + 1)
                        logits = bank[6][:].rearrange("p (n s) -> p n s", s=SC)
                        v.reduce_max(mx1[:], logits, AX_X).then_inc(s["mx1_set"], 1)
                        dve.wait_ge(s["mx1_set"], g + 1)
                        if g:
                            dve.wait_ge(s["p1T_psum"], g)
                        v.tensor_tensor(S1[:], logits, over_cols(mx1[:], SC), ALU.subtract).then_inc(s["s1_sub"], 1)
                    if k == at["sums"]:
                        dve.wait_ge(s["s1_exp"], g + 1)
                        v.reduce_sum(sm1[:], S1[:], AX_X).then_inc(s["sm1_set"], 1)
                        dve.wait_ge(s["sm1_set"], g + 1)
                        v.reciprocal(rs1[:], sm1[:]).then_inc(s["rs1_set"], 1)
                        dve.wait_ge(s["rs1_set"], g + 1)
                        v.tensor_tensor(S1[:], S1[:], over_cols(rs1[:], SC), ALU.mult).then_inc(s["p1_norm"], 1)
                    if k == at["add"]:
                        dve.wait_ge(s["o1_psum"], g + 1)
                        add_x(g, bank[6][:])
                        dve.wait_ge(s["x_updated"], x_count("b", g))
                        statistics("B", g)
                    if k == at["normed2"]:
                        dve.wait_ge(s["xm_set"], (g + 1) * E)
                        normalise("B", g, ZF[:, g])
                    if k == at["turned2"]:
                        dve.wait_ge(s["gu_psum"], 2 * (g * N0 + C0))
                        split_rows(1, g)
                    if k == at["route"]:
                        route(1, g)
                        v.tensor_tensor(oh2[:], over_rows(b_("iota", E), T), over_cols(ixf[:, :, 1], E),
                                        ALU.is_equal).then_inc(s["oh2_set"], 1)
                        dve.wait_ge(s["th_set"], r_count(1, g))
                        v.tensor_scalar(sc[:, :, 0], th[:], 0.5, 0.5, ALU.mult, ALU.add)
                        v.tensor_scalar(sc[:, :, 1], th[:], -0.5, 0.5, ALU.mult, ALU.add).then_inc(s["sc1_set"], 1)
                        dve.wait_ge(s["sc1_set"], g + 1)
                        dve.wait_ge(s["oh2_set"], g + 1)
                        v.tensor_tensor(oh[:], oh[:], over_cols(sc[:, :, 0], E), ALU.mult)
                        v.tensor_tensor(oh2[:], oh2[:], over_cols(sc[:, :, 1], E), ALU.mult).then_inc(s["ohw_set"], 1)
                        dve.wait_ge(s["ohw_set"], g + 1)
                        v.tensor_tensor(cmb[:], oh[:], oh2[:], ALU.add).then_inc(s["cmb_set"], 1)
                        dve.wait_ge(s["cmb_set"], g + 1)
                        if g:
                            dve.wait_ge(s["cT_psum"], g)
                        v.tensor_copy(c16[:, :, 0:E], cmb[:]).then_inc(s["c16hi_set"], 1)
                        dve.wait_ge(s["c16hi_set"], g + 1)
                        v.tensor_tensor(c16[:, :, E:2 * E], cmb[:], c16[:, :, 0:E].bitcast(F32),
                                        ALU.subtract).then_inc(s["c16_set"], 1)
                    yield

            def last_add():
                for t in range(T):
                    dve.wait_ge(s["last_psum"], t + 1)
                    v.tensor_tensor(X[:, 1, t], X[:, 1, t], last_bank(t)[:, 0:D],
                                    ALU.add).then_inc(s["x_updated"], 1)

            def masked_low(n):
                dve.wait_ge(s["xmhi_set"], n + 1)
                if n >= 2:
                    dve.wait_ge(s["gu_psum"], gu_after(n - 2))
                v.tensor_tensor(xmlo[:, n % 2], bank[5][:], xmhi[:, n % 2].bitcast(F32),
                                ALU.subtract).then_inc(s["xmlo_set"], 1)

            def hidden_low(i):
                dve.wait_ge(s["hhi_set"], i + 1)
                if i >= HR:
                    dve.wait_ge(s["down0_done"], i - HR + 1)
                v.tensor_tensor(hlo[:, i % HR], h[:, i % HB], hhi[:, i % HR].bitcast(F32),
                                ALU.subtract).then_inc(s["hlo_set"], 1)

            for _ in attention0(0):
                pass
            dve.wait_ge(s["b2hi_set"], 1)
            v.tensor_tensor(b2lo[:], b2[:], b2hi[:].bitcast(F32),
                            ALU.subtract).then_inc(s["b2lo_set"], 1)

            beside = [attention0(1), attention1(0), attention1(1)]
            for g in range(B):
                for u in range(U0):
                    for c in range(C0):
                        i = g * N0 + u * C0 + c
                        tick(beside[g])
                        dve.wait_ge(s["silu_set"], i + 1)
                        dve.wait_ge(s["gu_psum"], 2 * i + 2)
                        if i >= HB:
                            dve.wait_ge(s["hhi_set"], i - HB + 1)
                            dve.wait_ge(s["hlo_set"], i - HB + 1)
                        v.tensor_tensor(h[:, i % HB], sg[:, i % 2], bank[2 * (i % 2) + 1][:],
                                        ALU.mult).then_inc(s["h_set"], 1)
                        if c == 0 and u + 1 < U0:
                            masked_low(g * E + u)
                        if i:
                            hidden_low(i - 1)
            hidden_low(B * N0 - 1)

            def weigh_y(n):
                dve.wait_ge(s["down1_done"], C1 * (n + 1))
                dve.wait_ge(s["cbs_set"], n + 1)
                if n >= 2:
                    dve.wait_ge(s["acc_set"], n - 1)
                v.tensor_tensor(ym[:, n % 2], bank[3 + n % 2][:], cbs[:, n % 2], ALU.mult).then_inc(s["ym_set"], 1)

            for g in range(B):
                for e in range(E):
                    for c in range(C1):
                        j = g * N1 + e * C1 + c
                        tick(*beside[1 + g:])
                        dve.wait_ge(s["gelu_set"], j + 1)
                        if j >= HR:
                            dve.wait_ge(s["down1_done"], j - HR + 1)
                        else:
                            dve.wait_ge(s["down0_done"], B * N0 - HR + j + 1)
                        if j % 2:
                            dve.wait_ge(s["gelu_hi_set"], j // 2 + 1)
                        else:
                            v.tensor_copy(hhi[:, j % HR], h[:, j % HB]).then_inc(s["hi1_set"], 1)
                            dve.wait_ge(s["hi1_set"], j // 2 + 1)
                        v.tensor_tensor(hlo[:, j % HR], h[:, j % HB], hhi[:, j % HR].bitcast(F32),
                                        ALU.subtract).then_inc(s["lo1_set"], 1)
                        if c == LAG1 and g * E + e:
                            weigh_y(g * E + e - 1)
                        if g == 1 and e == 2 and c == 2:
                            dve.wait_ge(s["accT_psum"], 1)
                            add_x(0, bank[6][:])
            weigh_y(B * E - 1)
            last_add()

        @block.tensor
        def _(pe):
            mm, tr = nc.tensor.matmul, nc.tensor.transpose

            def product(out_, hi, lo, xhi, xlo, start, stop):
                mm(out_, hi, xhi, start=start, stop=False)
                mm(out_, hi, xlo, start=False, stop=False)
                return mm(out_, lo, xhi, start=False, stop=stop)

            def transpose_tiles(dst, src, rows_set=None, n=0):
                for t in range(T):
                    if rows_set:
                        pe.wait_ge(s[rows_set], (n - 1) * T + t + 1)
                    last = tr(dst[:, t * P:(t + 1) * P], src[:, t], ident)
                return last

            def bias0(g, t):
                mm(scores_bank(g, t)[:], ones1[:], over_rows(maskb[:, 0, g * SC:(g + 1) * SC], H0), start=True,
                   stop=False)

            def scores0(g, t):
                if g and t >= 2:
                    pe.wait_ge(s["s_sub"], g * T + t - 1)
                elif g == 0 and t == 3:
                    pe.wait_ge(s["vbd0_set"], 1)
                elif g and t == 1:
                    pe.wait_ge(s["zlo_set"], g)
                o = scores_bank(g, t)[:]
                if g or t >= 2:
                    bias0(g, t)
                mm(o, zT[:, t * P:(t + 1) * P], M0[:, g], start=False, stop=True).then_inc(s["s_psum"], 1)

            def transpose_probs0(g, t):
                pe.wait_ge(p_norm[t], g + 1)
                if t < 2 or g == 0:
                    pe.wait_ge(s["s_sub"], g * T + T)
                else:
                    pe.wait_ge(s["pT_set"], g * T + t - 1)
                for c in range(4):
                    heads = Sc[:, t, 4 * c:4 * c + 4].rearrange("p h s -> p (h s)")
                    last = tr(scores_bank(g, t)[:, c * P:(c + 1) * P], heads, ident)
                last.then_inc(s["pT_psum"], 1)

            def output0(g, t):
                pe.wait_ge(s["vw0_set"], B)
                pe.wait_ge(s["m0_set"], B)
                pe.wait_ge(s["pT_set"], g * T + t + 1)
                if g and t == 0:
                    pe.wait_ge(s["pT_set"], (g + 1) * T)
                for c in range(4):
                    last = mm(out_tile(g, t), PT[:, t, c], VW0[:, g, c], start=(c == 0),
                              stop=(c == 3))
                last.then_inc(s["o_psum"], 1)

            def logits(layer, g):
                n = r_count(layer, g)
                pe.wait_ge(s["zlo_set"], n)
                pe.wait_ge(s["gates_set"], 1)
                pe.wait_ge(s["x_updated"], x_count("b" if layer else "a", g))
                for t in range(T):
                    hi, lo = (z[:, g, t * P:(t + 1) * P] for z in (zhi, zlo))
                    o = bank[6][:, 2 * t * E:2 * (t + 1) * E]
                    mm(o, hi, gates[:, layer].rearrange("p k e -> p (k e)"), start=True, stop=False)
                    last = mm(o[:, 0:E], lo, gates[:, layer, 0], start=False, stop=True)
                last.then_inc(s["lg_psum"], 1)

            def attention0(g):
                at = ATT0_PE
                for k in range(max(at.values()) + 1):
                    if k == 0 and g == 1:
                        pe.wait_ge(s["kvbd1_set"], 1)
                        pe.wait_ge(s["lg_set"], 1)
                        for b in range(B):
                            last = mm(bank[6][:, b * D:(b + 1) * D], Vbd1[:, b].rearrange("p h s -> p (h s)"),
                                      b_("ow", D), start=True, stop=True)
                        last.then_inc(s["vw1_psum"], 1)
                    if k == at["normed"]:
                        if g:
                            pe.wait_ge(s["vw1_set"], 1)
                        transpose_tiles(bank[6], ZA, "za_set", g + 1).then_inc(s["zaT_psum"], 1)
                        if g == 0:
                            pe.wait_ge(s["maskb_set"], 1)
                            pe.wait_ge(s["const_set"], 1)
                            bias0(0, 0)
                            bias0(0, 1)
                    if k == at["scores01"]:
                        pe.wait_ge(s["zaT_set"], g + 1)
                        if g == 0:
                            pe.wait_ge(s["m0_set"], 1)
                        scores0(g, 0)
                        scores0(g, 1)
                    if k == at["scores23"]:
                        scores0(g, 2)
                        scores0(g, 3)
                        if g == 0:
                            fold_keys(1)
                            fold_values()
                    if k == at["probs01"]:
                        transpose_probs0(g, 0)
                        transpose_probs0(g, 1)
                    if k == at["probs23"]:
                        if g == 0:
                            output0(g, 0)
                        transpose_probs0(g, 2)
                        if g == 0:
                            output0(g, 1)
                        transpose_probs0(g, 3)
                    if k == at["out"]:
                        for t in range(0 if g else 2, T):
                            output0(g, t)
                        if g == 0:
                            context1()
                    if k == at["normed2"]:
                        transpose_tiles(bank[7], ZF[:, g], "zf_set", r_count(0, g)).then_inc(s["zfT_psum"], 1)
                    if k == at["logits"]:
                        logits(0, g)
                    yield

            def setup0_keys():
                pe.wait_ge(s["keys_in"], 16)
                mm(bank[7][:, 0:B * SC], a_("wkT", D), a_("ctxT", B * SC), start=True, stop=True)
                mm(bank[7][:, B * SC:2 * B * SC], a_("wvT", D), a_("ctxT", B * SC), start=True,
                   stop=True).then_inc(s["kv0_psum"], 1)
                fold_keys(0)

            def fold_keys(b):
                pe.wait_ge(s["pa_in"], 16)
                pe.wait_ge(s["kbd0_set"], b + 1)
                mm(bank[b][:], a_("wq", D), Kbd[:, b].rearrange("p h s -> p (h s)"), start=True,
                   stop=True).then_inc(s["m0_psum"], 1)

            def fold_values():
                pe.wait_ge(s["vbd0_set"], 1)
                for b in range(B):
                    for c in range(4):
                        last = mm(bank[2 + b][:, c * D:(c + 1) * D],
                                  Vbd[:, b, 4 * c:4 * c + 4].rearrange("p h s -> p (h s)"), a_("woT", D),
                                  start=True, stop=True)
                    last.then_inc(s["vw0_psum"], 1)

            def context1():
                pe.wait_ge(s["mn_set"], 1)
                tr(bank[4][:, 0:B * SC], mn[:], ident[0:B * SC, 0:B * SC]).then_inc(s["mnT_psum"], 1)
                pe.wait_ge(s["mnT_set"], 1)
                pe.wait_ge(s["wts1_set"], 1)
                for k, w in enumerate((wk1, wk1s, wv1)):
                    last = mm(bank[5][:, k * B * SC:(k + 1) * B * SC], w[:].rearrange("p h d -> p (h d)"), mnT[:],
                              start=True, stop=True)
                last.then_inc(s["kv1_psum"], 1)

            def attention1(g):
                at = ATT1_PE[g]
                for k in range(max(at.values()) + 1):
                    if k == at["y"]:
                        pe.wait_ge(s["yT_set"], g + 1)
                        if g:
                            pe.wait_ge(s["b2c_set"], g)
                        else:
                            pe.wait_ge(s["lg_set"], B)
                        for t in range(T):
                            last = tr(bank[6][:, t * P:(t + 1) * P], yT[:, t * P:(t + 1) * P], ident)
                        last.then_inc(s["yT_psum"], 1)
                    if k == at["normed"]:
                        transpose_tiles(bank[7], ZA, "za_set", B + g + 1).then_inc(s["zaT_psum"], 1)
                    if k == at["queries"]:
                        pe.wait_ge(s["zaT_set"], B + g + 1)
                        pe.wait_ge(s["x_updated"], x_count("f", g))
                        mm(bank[6][:], wq1[:].rearrange("p h d -> p (h d)"), zT[:], start=True,
                           stop=True).then_inc(s["q_psum"], 1)
                        mm(bank[7][:], wq1s[:].rearrange("p h d -> p (h d)"), zT[:], start=True,
                           stop=True).then_inc(s["q_psum"], 1)
                    if k == at["scores"]:
                        pe.wait_ge(s["q_set"], g + 1)
                        for t in range(T):
                            o = bank[6][:, t * P:(t + 1) * P]
                            mm(o, qr[:, 0, t * P:(t + 1) * P], Kbd1[:, g].rearrange("p h s -> p (h s)"), start=True,
                               stop=False)
                            last = mm(o, ones1[:], over_rows(maskb[:, 1, g * SC:(g + 1) * SC], H1), start=False,
                                      stop=True)
                        last.then_inc(s["l1_psum"], 1)
                    if k == at["probs"]:
                        pe.wait_ge(s["p1_norm"], g + 1)
                        for t in range(T):
                            last = tr(bank[7][:, t * P:(t + 1) * P],
                                      S1[:, t * H1:(t + 1) * H1].rearrange("p h s -> p (h s)"), ident)
                        last.then_inc(s["p1T_psum"], 1)
                    if k == at["out"]:
                        pe.wait_ge(s["p1T_set"], g + 1)
                        for t in range(T):
                            last = mm(bank[6][:, t * D:(t + 1) * D], P1T[:, t], VW1[:, g], start=True, stop=True)
                        last.then_inc(s["o1_psum"], 1)
                    if k == at["normed2"]:
                        transpose_tiles(bank[7], ZF[:, g], "zf_set", r_count(1, g)).then_inc(s["zfT_psum"], 1)
                    if k == at["logits"]:
                        logits(1, g)
                    if k == at["weights"]:
                        pe.wait_ge(s["c16_set"], g + 1)
                        pe.wait_ge(s["zlo_set"], r_count(1, g))
                        for t in range(T):
                            last = tr(bank[7][0:2 * E, t * P:(t + 1) * P], c16[:, t].bitcast(F32), ident)
                        last.then_inc(s["cT_psum"], 1)
                    if k == at["bias"]:
                        pe.wait_ge(s["cT_set"], g + 1)
                        pe.wait_ge(s["b2lo_set"], 1)
                        mm(bank[6][:], b2hi[:], cT16[:, g], start=True, stop=False)
                        mm(bank[6][:], b2lo[:], cT16[:, g], start=False, stop=True).then_inc(s["b2_psum"], 1)
                    yield

            def spread_weights(n):
                g, e = divmod(n, E)
                pe.wait_ge(s["cT_set"], g + 1)
                if n:
                    pe.wait_ge(s["cbs_set"], n)
                else:
                    pe.wait_ge(s["sel_set"], 1)
                    pe.wait_ge(s["xmlo_set"], B * E)
                mm(bank[5][:], selr[:, e], cT16[:, g], start=True, stop=True).then_inc(s["cb_psum"], 1)

            def transpose_sum():
                pe.wait_ge(s["acc_set"], E)
                pe.wait_ge(s["b2c_set"], B)
                for t in range(T):
                    last = tr(bank[6][:, t * P:(t + 1) * P], acc[:, t * P:(t + 1) * P], ident)
                last.then_inc(s["accT_psum"], 1)

            def last_sum(part):
                if part == 0:
                    pe.wait_ge(s["acc_set"], B * E - 2)
                    pe.wait_ge(s["x_updated"], x_count("o", 0))
                    pe.wait_ge(s["gelu_set"], B * N1 - 1)
                    pe.wait_ge(s["gelu_hi_set"], B * N1 // 2 - 1)
                    rows = acc[:]
                else:
                    n = B * E - 3 + part
                    pe.wait_ge(s["ym_set"], n + 1)
                    rows = ym[:, n % 2]
                for t in range(T):
                    last = mm(last_bank(t)[:, 0:D], rows[:, t * P:(t + 1) * P], ident, start=part == 0,
                              stop=part == 2)
                    if part == 2:
                        last.then_inc(s["last_psum"], 1)

            def transpose_masked(n):
                pe.wait_ge(s["xm_set"], n + 1)
                if n:
                    pe.wait_ge(s["xmlo_set"], n)
                else:
                    pe.wait_ge(s["kvbd1_set"], 1)
                transpose_tiles(bank[5], xm[:, n % 2]).then_inc(s["xmT_psum"], 1)

            def down0(i):
                g, r = divmod(i, N0)
                u, c = divmod(r, C0)
                pe.wait_ge(s["hlo_set"], i + 1)
                if r == 0 and g:
                    pe.wait_ge(s["yT_set"], g)
                o = 2 * I0 + c * D
                product(bank[4][:], w0hi[:, u, o:o + D], w0lo[:, u, o:o + D], hhi[:, i % HR], hlo[:, i % HR],
                        r == 0, r == N0 - 1).then_inc(s["down0_done"], 1)

            def down1(j):
                n, c = divmod(j, C1)
                pe.wait_ge(s["lo1_set"], j + 1)
                if c == 0:
                    if n >= 2:
                        pe.wait_ge(s["ym_set"], n - 1)
                    elif n == 1:
                        pe.wait_ge(s["yT_set"], B)
                o = F1 + c * D
                e = n % E
                product(bank[3 + n % 2][:], w1hi[:, e, o:o + D], w1lo[:, e, o:o + D], hhi[:, j % HR], hlo[:, j % HR],
                        c == 0, c == C1 - 1).then_inc(s["down1_done"], 1)

            pe.wait_ge(s["const_set"], 1)
            setup0_keys()
            for _ in attention0(0):
                pass
            pe.wait_ge(s["m0_set"], B)
            pe.wait_ge(s["vw0_set"], B)
            beside = [attention0(1), attention1(0), attention1(1)]
            for g in range(B):
                for u in range(U0):
                    for c in range(C0):
                        i = g * N0 + u * C0 + c
                        if c == 0 and g == 0:
                            pe.wait_ge(s["w_lo_set"], u + 1)
                        if c == 0 and u:
                            pe.wait_ge(s["xmlo_set"], g * E + u)
                        elif c == 0:
                            pe.wait_ge(s["zlo_set"], g + 1)
                        n = g * E + u - 1
                        xhi, xlo = (zhi[:, g], zlo[:, g]) if u == 0 else (xmhi[:, n % 2], xmlo[:, n % 2])
                        if i >= 2:
                            pe.wait_ge(s["h_set"], i - 1)
                        for k in range(2):
                            o = k * I0 + c * P
                            product(bank[2 * (i % 2) + k][:], w0hi[:, u, o:o + P], w0lo[:, u, o:o + P], xhi, xlo, True,
                                    True).then_inc(s["gu_psum"], 1)
                        if i == 0:
                            tick(beside[g])
                        if c == 0 and u + 1 < U0:
                            transpose_masked(g * E + u)
                        if i >= LAG0:
                            down0(i - LAG0)
                        if i:
                            tick(beside[g])
            for g in range(B):
                for e in range(E):
                    for c in range(C1):
                        j = g * N1 + e * C1 + c
                        n = g * E + e
                        if c == 0 and g == 0:
                            pe.wait_ge(s["w_lo_set"], U0 + e + 1)
                        if c == 0 and e == 0:
                            pe.wait_ge(s["zlo_set"], r_count(1, g))
                        if j >= 3:
                            pe.wait_ge(s["gelu_set"], j - 2)
                            if j % 2 == 0:
                                pe.wait_ge(s["gelu_hi_set"], (j - 3) // 2 + 1)
                        else:
                            pe.wait_ge(s["h_set"], B * N0 - (j < 2))
                        product(bank[j % 3][:], w1hi[:, e, c * P:(c + 1) * P], w1lo[:, e, c * P:(c + 1) * P], zhi[:, g],
                                zlo[:, g], True, True).then_inc(s["up_psum"], 1)
                        if j < LAG0:
                            down0(B * N0 - LAG0 + j)
                        if c == 0 and n:
                            spread_weights(n - 1)
                        if j >= LAG1:
                            down1(j - LAG1)
                        if g == 1 and e == 2 and c == 1:
                            transpose_sum()
                        tick(*beside[1 + g:])
            spread_weights(B * E - 1)
            for j in range(B * N1 - LAG1, B * N1):
                if j == B * N1 - 1:
                    last_sum(0)
                down1(j)
            last_sum(1)
            last_sum(2)


def kernel(**inputs):
    import concourse.bacc as bacc
    from concourse.bass_utils import run_bass_kernel_spmd

    f32 = np.float32
    a = {k: np.ascontiguousarray(v) for k, v in inputs.items()}

    o = np.arange(P)
    bm0 = (o[:, None] // HD0 == np.arange(H0)[None, :]).astype(f32)
    bm1 = (o[:, None] // HD1 == np.arange(H1)[None, :]).astype(f32)
    half = HD1 // 2
    timescale = (10000.0 ** (2.0 / HD1 * np.arange(half))).astype(f32)
    lane = o % HD1
    sign = np.where(lane < half, -1.0, 1.0).astype(f32)

    def rotation(pos):
        radians = pos.astype(f32)[None, :] / timescale[lane % half][:, None]
        return np.cos(radians).astype(f32), (np.sin(radians) * sign[:, None]).astype(f32)

    cosk, sink = rotation(np.arange(SC))
    column = np.arange(S)
    cosq, sinq = rotation(SC + T * (column % P) + column // P)
    sel = (np.arange(2 * E)[:, None, None] % E == np.arange(E)[None, :, None]) * np.ones((1, 1, P))

    def cols(parts, layout):
        whole = np.concatenate([np.asarray(p_, f32).reshape(parts[0].shape[0], -1) for p_ in parts], axis=1)
        assert whole.shape[1] == layout["_end"]
        return whole

    ctx = a["ctx_1024"].reshape(B * SC, D)
    pack_a = cols([ctx.T, a["L0_xattn_Wk"].T, a["L0_xattn_Wv"].T, bm0 * f32(HD0 ** -0.5), bm0, a["L0_xattn_Wq"],
                   np.eye(P, dtype=f32), a["L0_xattn_Wo"].T], PA_)
    qw = a["L1_xattn_q_w"].transpose(1, 0, 2).reshape(D, H1 * HD1)
    kvw = a["L1_xattn_kv_w"][:, 0]
    pack_b = cols([qw, kvw[0], kvw[1], a["L1_xattn_out_w"].reshape(H1 * HD1, D), a["L1_xattn_rms_scale"][:, None],
                   a["L0_ffn_gate_w"], a["L1_ffn_gate_w"], a["L1_ffn_b1"].reshape(E, C1, P).transpose(2, 0, 1), bm1,
                   bm1 * f32(HD1 ** -0.5), cosk, sink, np.tile(np.arange(E, dtype=f32), (P, 1))], PB_)
    selectors = sel.astype(f32).reshape(2 * E, E * P)
    b2_rows = np.concatenate([a["L1_ffn_b2"]] * 2)
    rope_q = np.stack([cosq, sinq], axis=1)
    masks = np.concatenate([a["mask_BxS2_bk1"].reshape(1, -1), a["mask_BxS2_bk0"].reshape(1, -1)],
                           axis=1)

    def rows(w, c):
        return w.reshape(c, P, -1).transpose(1, 0, 2).reshape(P, -1)

    w0 = np.stack([np.concatenate([g_, u_, rows(d_, C0)], axis=1) for g_, u_, d_ in
                   [(a["L0_ffn_sh_gate"], a["L0_ffn_sh_up"], a["L0_ffn_sh_down"])]
                   + [(a["L0_ffn_rt_gate"][e], a["L0_ffn_rt_up"][e], a["L0_ffn_rt_down"][e]) for e in range(E)]])
    w1 = np.stack([np.concatenate([a["L1_ffn_w1"][e], rows(a["L1_ffn_w2"][e], C1)], axis=1) for e in range(E)])

    nc = bacc.Bacc("TRN2", target_bir_lowering=False, num_devices=1)
    arrays, args = {}, []
    for name, v in dict(x=a["x"], pack_a=pack_a, pack_b=pack_b, selectors=selectors, b2_rows=b2_rows, rope_q=rope_q,
                        ctx=ctx, masks=masks, w0=w0, w1=w1).items():
        v = np.ascontiguousarray(v)
        arrays[f"in_{name}"] = v
        args.append(nc.dram_tensor(f"in_{name}", v.shape, mybir.dt.from_np(v.dtype), kind="ExternalInput").ap())
    out = nc.dram_tensor("out_0", (B, S, D), F32, kind="ExternalOutput").ap()
    two_moe_layers(nc, *args, out)
    r = run_bass_kernel_spmd(nc, [arrays], core_ids=[0])
    return r.results[0]["out_0"]
```
